# Optimizing a Trainium2 kernel written in Bass

```python
import numpy as np
import jax
import jax.numpy as jnp

def _softmax(x, axis=-1):
    return jax.nn.softmax(x, axis=axis)

def _gelu(x):
    return jax.nn.gelu(x, approximate=True)

def _silu(x):
    return jax.nn.silu(x)

def _sigmoid(x):
    return jax.nn.sigmoid(x)

def _layernorm(x, axis=-1, eps=1e-05):
    m = jnp.mean(x, axis=axis, keepdims=True)
    v = jnp.var(x, axis=axis, keepdims=True)
    return (x - m) / jnp.sqrt(v + eps)

def _scatter_add(tgt, idx, src, axis=0):
    return tgt.at[idx].add(src)

def _segment_sum(src, seg, n):
    return jax.ops.segment_sum(src, seg, n)
kernel_name = 'mk_prb_d2_jaxref_r8_12a8ad'

def setup_inputs(seed: int=0):
    np.random.seed(seed)
    _w = jnp.asarray

    def _L0_attn_setup():
        import jax, jax.numpy as jnp
        import numpy as np
        DIM = 256
        D_STATE = 128
        EXPAND = 2
        HEADDIM = 64
        CHUNK = 64
        NGROUPS = 1
        D_INNER = EXPAND * DIM
        NHEADS = D_INNER // HEADDIM
        D_PROJ = D_INNER * 2 + NGROUPS * D_STATE * 2 + NHEADS
        BATCH, SEQ = (2, 512)
        EPS = 1e-05

        def segsum(x):
            T = x.shape[-1]
            xx = jnp.broadcast_to(x[..., :, None], x.shape + (T,))
            keep = jnp.tril(jnp.ones((T, T), dtype=bool), -1)
            xx = jnp.where(keep, xx, 0.0)
            s = jnp.cumsum(xx, axis=-2)
            tri = jnp.tril(jnp.ones((T, T), dtype=bool), 0)
            return jnp.where(tri, s, -jnp.inf)

        def rms_norm(x, w):
            return x * jax.lax.rsqrt(jnp.mean(x * x, axis=-1, keepdims=True) + EPS) * w

        def layer_norm(x, w, b):
            mu = jnp.mean(x, axis=-1, keepdims=True)
            var = jnp.mean((x - mu) ** 2, axis=-1, keepdims=True)
            return (x - mu) * jax.lax.rsqrt(var + EPS) * w + b

        def ssd_chunked(x, A, B, C, chunk):
            b, s, h, p = x.shape
            n = B.shape[-1]
            if B.shape[2] < h:
                r = h // B.shape[2]
                B = jnp.repeat(B, r, axis=2)
                C = jnp.repeat(C, r, axis=2)
            c = s // chunk
            x = x.reshape(b, c, chunk, h, p)
            A = A.reshape(b, c, chunk, h).transpose(0, 3, 1, 2)
            B = B.reshape(b, c, chunk, h, n)
            C = C.reshape(b, c, chunk, h, n)
            L = jnp.exp(segsum(A))
            Y_diag = jnp.einsum('bclhn,bcshn,bhcls,bcshp->bclhp', C, B, L, x)
            A_cumsum = jnp.cumsum(A, axis=-1)
            decay_states = jnp.exp(A_cumsum[..., -1:] - A_cumsum)
            states = jnp.einsum('bclhn,bhcl,bclhp->bchpn', B, decay_states, x)
            A_chunk = jnp.pad(A_cumsum[..., -1], ((0, 0), (0, 0), (1, 0)))
            decay_chunk = jnp.exp(segsum(A_chunk))
            new_states = jnp.einsum('bhzc,bchpn->bzhpn', decay_chunk[:, :, :c, 1:c + 1], states)
            Y_off = jnp.einsum('bclhn,bchpn,bhcl->bclhp', C, new_states, jnp.exp(A_cumsum))
            return (Y_diag + Y_off).reshape(b, s, h, p)

        def mamba3_forward(u, in_proj_w, out_proj_w, D, dt_bias, A_log, bnorm_w, cnorm_w, ln_w, ln_b):
            b, s, _ = u.shape
            u_n = layer_norm(u, ln_w, ln_b)
            proj = jnp.einsum('bsd,ed->bse', u_n, in_proj_w)
            z = proj[..., :D_INNER]
            x = proj[..., D_INNER:2 * D_INNER]
            B = proj[..., 2 * D_INNER:2 * D_INNER + NGROUPS * D_STATE].reshape(b, s, NGROUPS, D_STATE)
            C = proj[..., 2 * D_INNER + NGROUPS * D_STATE:2 * D_INNER + 2 * NGROUPS * D_STATE].reshape(b, s, NGROUPS, D_STATE)
            dt = proj[..., -NHEADS:]
            B = rms_norm(B, bnorm_w)
            C = rms_norm(C, cnorm_w)
            x = x.reshape(b, s, NHEADS, HEADDIM)
            z = z.reshape(b, s, NHEADS, HEADDIM)
            dt_proc = jax.nn.softplus(dt + dt_bias)
            A = -jnp.exp(A_log)
            dA = dt_proc * A
            y = ssd_chunked(x, dA, B, C, CHUNK)
            y = y + x * D[None, None, :, None]
            y = y.reshape(b, s, D_INNER)
            z_flat = z.reshape(b, s, D_INNER)
            y = y * jax.nn.silu(z_flat)
            return u + jnp.einsum('bse,de->bsd', y, out_proj_w)
        key = jax.random.key(seed)
        ks = jax.random.split(key, 6)
        u = jax.random.normal(ks[0], (BATCH, SEQ, DIM), dtype=jnp.float32)
        in_proj_w = jax.random.normal(ks[1], (D_PROJ, DIM), dtype=jnp.float32) * 0.02
        out_proj_w = jax.random.normal(ks[2], (DIM, D_INNER), dtype=jnp.float32) * 0.02
        D = jnp.ones((NHEADS,), dtype=jnp.float32)
        dt_bias = jax.random.normal(ks[3], (NHEADS,), dtype=jnp.float32) * 0.1
        A_log = jnp.log(0.5 + jax.random.uniform(ks[4], (NHEADS,), dtype=jnp.float32) * 0.5)
        bnorm_w = jnp.ones((D_STATE,), dtype=jnp.float32)
        cnorm_w = jnp.ones((D_STATE,), dtype=jnp.float32)
        ln_w = jnp.ones((DIM,), dtype=jnp.float32)
        ln_b = jnp.zeros((DIM,), dtype=jnp.float32)
        return {'u': u, 'in_proj_w': in_proj_w, 'out_proj_w': out_proj_w, 'D': D, 'dt_bias': dt_bias, 'A_log': A_log, 'bnorm_w': bnorm_w, 'cnorm_w': cnorm_w, 'ln_w': ln_w, 'ln_b': ln_b}
    _L0_attn_in = _L0_attn_setup()

    def _L0_ffn_setup():
        import jax, jax.numpy as jnp
        import numpy as np
        B, S, H = (2, 128, 256)
        E, K = (8, 2)
        I = 176
        IS = 704
        WSCALE = 0.02
        key = jax.random.key(seed)
        ks = jax.random.split(key, 9)
        f32 = jnp.float32
        return {'hidden_states': jax.random.normal(ks[0], (B, S, H), dtype=f32), 'gate_w': jax.random.normal(ks[1], (E, H), dtype=f32) * WSCALE, 'w_gate': jax.random.normal(ks[2], (E, H, I), dtype=f32) * WSCALE, 'w_up': jax.random.normal(ks[3], (E, H, I), dtype=f32) * WSCALE, 'w_down': jax.random.normal(ks[4], (E, I, H), dtype=f32) * WSCALE, 'sw_gate': jax.random.normal(ks[5], (H, IS), dtype=f32) * WSCALE, 'sw_up': jax.random.normal(ks[6], (H, IS), dtype=f32) * WSCALE, 'sw_down': jax.random.normal(ks[7], (IS, H), dtype=f32) * WSCALE, 'shared_gate_w': jax.random.normal(ks[8], (H, 1), dtype=f32) * WSCALE}
    _L0_ffn_in = _L0_ffn_setup()

    def _L1_attn_setup():
        import jax, jax.numpy as jnp
        from jax import lax
        import numpy as np
        B, T, HID = (1, 256, 256)
        H, DQ, DV, K = (16, 128, 128, 4)
        SCALE = DQ ** (-0.5)
        LN_EPS = 1e-05

        def _causal_depthwise_conv(x, w, b):
            C = w.shape[0]
            out = lax.conv_general_dilated(x.transpose(0, 2, 1), w[:, None, :], window_strides=(1,), padding=[(K - 1, 0)], feature_group_count=C, dimension_numbers=('NCH', 'OIH', 'NCH'))
            return (out + b[None, :, None]).transpose(0, 2, 1)

        def _delta_scan(q, k, v, a, beta):
            N = q.shape[0]

            def step(S, inp):
                q_t, k_t, v_t, a_t, b_t = inp
                sk = jnp.einsum('ndq,nq->nd', S, k_t)
                err = sk - v_t
                S = S * a_t[:, :, None] - (b_t[:, None] * err)[:, :, None] * k_t[:, None, :]
                o_t = jnp.einsum('ndq,nq->nd', S, q_t)
                return (S, o_t)
            S0 = jnp.zeros((N, DV, DQ), dtype=q.dtype)
            xs = (q.transpose(1, 0, 2), k.transpose(1, 0, 2), v.transpose(1, 0, 2), a.transpose(1, 0, 2), beta.transpose(1, 0))
            _, o = lax.scan(step, S0, xs)
            return o.transpose(1, 0, 2)
        key = jax.random.key(seed)
        ks = jax.random.split(key, 16)
        s = HID ** (-0.5)
        sc = K ** (-0.5)
        return {'x': jax.random.normal(ks[0], (B, T, HID), jnp.float32), 'Wq': jax.random.normal(ks[1], (H * DQ, HID), jnp.float32) * s, 'Wk': jax.random.normal(ks[2], (H * DQ, HID), jnp.float32) * s, 'Wv': jax.random.normal(ks[3], (H * DV, HID), jnp.float32) * s, 'Wa': jax.random.normal(ks[4], (H * DV, HID), jnp.float32) * s, 'ba': jnp.zeros((H * DV,), jnp.float32), 'Wb': jax.random.normal(ks[5], (H, HID), jnp.float32) * s, 'bb': jnp.zeros((H,), jnp.float32), 'qconv_w': jax.random.normal(ks[6], (H * DQ, K), jnp.float32) * sc, 'qconv_b': jnp.zeros((H * DQ,), jnp.float32), 'kconv_w': jax.random.normal(ks[7], (H * DQ, K), jnp.float32) * sc, 'kconv_b': jnp.zeros((H * DQ,), jnp.float32), 'vconv_w': jax.random.normal(ks[8], (H * DV, K), jnp.float32) * sc, 'vconv_b': jnp.zeros((H * DV,), jnp.float32), 'Wg': jax.random.normal(ks[9], (H * DV, HID), jnp.float32) * s, 'Wo': jax.random.normal(ks[10], (HID, H * DV), jnp.float32) * s, 'ln_w': jnp.ones((DV,), jnp.float32), 'ln_b': jnp.zeros((DV,), jnp.float32)}
    _L1_attn_in = _L1_attn_setup()

    def _L1_ffn_setup():
        import jax, jax.numpy as jnp
        import numpy as np
        JITTER_EPS = 0.01
        NUM_EXPERTS = 8
        TOP_K = 2
        HIDDEN = 256
        INTER = 512

        def _routing(logits):
            top2_vals, top2_idx = jax.lax.top_k(logits, TOP_K)

            def one_multiplier(thresh, base_scores, sel):
                factor = jnp.maximum(jnp.abs(logits), thresh)
                jitter_mask = (thresh - logits) / factor > 2.0 * JITTER_EPS
                s = jnp.where(jitter_mask, -jnp.inf, base_scores)
                p = jax.nn.softmax(s, axis=-1)
                return jnp.take_along_axis(p, sel[:, None], axis=-1)
            m1 = one_multiplier(top2_vals[:, 0:1], logits, top2_idx[:, 0])
            sel0_onehot = jax.nn.one_hot(top2_idx[:, 0], logits.shape[-1], dtype=bool)
            scores2 = jnp.where(sel0_onehot, -jnp.inf, logits)
            m2 = one_multiplier(top2_vals[:, 1:2], scores2, top2_idx[:, 1])
            multiplier = jnp.concatenate([m1, m2], axis=-1)
            return (multiplier, top2_idx)
        key = jax.random.key(seed)
        ks = jax.random.split(key, 5)
        B, S = (2, 256)
        hidden_states = jax.random.normal(ks[0], (B, S, HIDDEN), dtype=jnp.float32)
        scale_h = 1.0 / np.sqrt(HIDDEN)
        scale_i = 1.0 / np.sqrt(INTER)
        gate_w = jax.random.normal(ks[1], (NUM_EXPERTS, HIDDEN), dtype=jnp.float32) * scale_h
        w1 = jax.random.normal(ks[2], (NUM_EXPERTS, INTER, HIDDEN), dtype=jnp.float32) * scale_h
        w3 = jax.random.normal(ks[3], (NUM_EXPERTS, INTER, HIDDEN), dtype=jnp.float32) * scale_h
        w2 = jax.random.normal(ks[4], (NUM_EXPERTS, HIDDEN, INTER), dtype=jnp.float32) * scale_i
        return {'hidden_states': hidden_states, 'gate_w': gate_w, 'w1': w1, 'w2': w2, 'w3': w3}
    _L1_ffn_in = _L1_ffn_setup()
    _d = {'L0_attn_u': _L0_attn_in['u'], 'L0_attn_in_proj_w': _L0_attn_in['in_proj_w'], 'L0_attn_out_proj_w': _L0_attn_in['out_proj_w'], 'L0_attn_D': _L0_attn_in['D'], 'L0_attn_dt_bias': _L0_attn_in['dt_bias'], 'L0_attn_A_log': _L0_attn_in['A_log'], 'L0_attn_bnorm_w': _L0_attn_in['bnorm_w'], 'L0_attn_cnorm_w': _L0_attn_in['cnorm_w'], 'L0_attn_ln_w': _L0_attn_in['ln_w'], 'L0_attn_ln_b': _L0_attn_in['ln_b'], 'L0_ffn_gate_w': _L0_ffn_in['gate_w'], 'L0_ffn_w_gate': _L0_ffn_in['w_gate'], 'L0_ffn_w_up': _L0_ffn_in['w_up'], 'L0_ffn_w_down': _L0_ffn_in['w_down'], 'L0_ffn_sw_gate': _L0_ffn_in['sw_gate'], 'L0_ffn_sw_up': _L0_ffn_in['sw_up'], 'L0_ffn_sw_down': _L0_ffn_in['sw_down'], 'L0_ffn_shared_gate_w': _L0_ffn_in['shared_gate_w'], 'L1_attn_Wq': _L1_attn_in['Wq'], 'L1_attn_Wk': _L1_attn_in['Wk'], 'L1_attn_Wv': _L1_attn_in['Wv'], 'L1_attn_Wa': _L1_attn_in['Wa'], 'L1_attn_ba': _L1_attn_in['ba'], 'L1_attn_Wb': _L1_attn_in['Wb'], 'L1_attn_bb': _L1_attn_in['bb'], 'L1_attn_qconv_w': _L1_attn_in['qconv_w'], 'L1_attn_qconv_b': _L1_attn_in['qconv_b'], 'L1_attn_kconv_w': _L1_attn_in['kconv_w'], 'L1_attn_kconv_b': _L1_attn_in['kconv_b'], 'L1_attn_vconv_w': _L1_attn_in['vconv_w'], 'L1_attn_vconv_b': _L1_attn_in['vconv_b'], 'L1_attn_Wg': _L1_attn_in['Wg'], 'L1_attn_Wo': _L1_attn_in['Wo'], 'L1_attn_ln_w': _L1_attn_in['ln_w'], 'L1_attn_ln_b': _L1_attn_in['ln_b'], 'L1_ffn_gate_w': _L1_ffn_in['gate_w'], 'L1_ffn_w1': _L1_ffn_in['w1'], 'L1_ffn_w2': _L1_ffn_in['w2'], 'L1_ffn_w3': _L1_ffn_in['w3']}
    _x0 = _d['L0_attn_u']
    _d['L0_attn_u'] = jax.random.normal(jax.random.fold_in(jax.random.key(seed), 1), (1, 1024, 256), dtype=_x0.dtype)
    del _x0
    return _d

def reference(L0_attn_u, L0_attn_in_proj_w, L0_attn_out_proj_w, L0_attn_D, L0_attn_dt_bias, L0_attn_A_log, L0_attn_bnorm_w, L0_attn_cnorm_w, L0_attn_ln_w, L0_attn_ln_b, L0_ffn_gate_w, L0_ffn_w_gate, L0_ffn_w_up, L0_ffn_w_down, L0_ffn_sw_gate, L0_ffn_sw_up, L0_ffn_sw_down, L0_ffn_shared_gate_w, L1_attn_Wq, L1_attn_Wk, L1_attn_Wv, L1_attn_Wa, L1_attn_ba, L1_attn_Wb, L1_attn_bb, L1_attn_qconv_w, L1_attn_qconv_b, L1_attn_kconv_w, L1_attn_kconv_b, L1_attn_vconv_w, L1_attn_vconv_b, L1_attn_Wg, L1_attn_Wo, L1_attn_ln_w, L1_attn_ln_b, L1_ffn_gate_w, L1_ffn_w1, L1_ffn_w2, L1_ffn_w3):

    def _L0_attn_ref(u, in_proj_w, out_proj_w, D, dt_bias, A_log, bnorm_w, cnorm_w, ln_w, ln_b):
        import jax, jax.numpy as jnp
        import numpy as np
        DIM = 256
        D_STATE = 128
        EXPAND = 2
        HEADDIM = 64
        CHUNK = 64
        NGROUPS = 1
        D_INNER = EXPAND * DIM
        NHEADS = D_INNER // HEADDIM
        D_PROJ = D_INNER * 2 + NGROUPS * D_STATE * 2 + NHEADS
        BATCH, SEQ = (2, 512)
        EPS = 1e-05

        def segsum(x):
            T = x.shape[-1]
            xx = jnp.broadcast_to(x[..., :, None], x.shape + (T,))
            keep = jnp.tril(jnp.ones((T, T), dtype=bool), -1)
            xx = jnp.where(keep, xx, 0.0)
            s = jnp.cumsum(xx, axis=-2)
            tri = jnp.tril(jnp.ones((T, T), dtype=bool), 0)
            return jnp.where(tri, s, -jnp.inf)

        def rms_norm(x, w):
            return x * jax.lax.rsqrt(jnp.mean(x * x, axis=-1, keepdims=True) + EPS) * w

        def layer_norm(x, w, b):
            mu = jnp.mean(x, axis=-1, keepdims=True)
            var = jnp.mean((x - mu) ** 2, axis=-1, keepdims=True)
            return (x - mu) * jax.lax.rsqrt(var + EPS) * w + b

        def ssd_chunked(x, A, B, C, chunk):
            b, s, h, p = x.shape
            n = B.shape[-1]
            if B.shape[2] < h:
                r = h // B.shape[2]
                B = jnp.repeat(B, r, axis=2)
                C = jnp.repeat(C, r, axis=2)
            c = s // chunk
            x = x.reshape(b, c, chunk, h, p)
            A = A.reshape(b, c, chunk, h).transpose(0, 3, 1, 2)
            B = B.reshape(b, c, chunk, h, n)
            C = C.reshape(b, c, chunk, h, n)
            L = jnp.exp(segsum(A))
            Y_diag = jnp.einsum('bclhn,bcshn,bhcls,bcshp->bclhp', C, B, L, x)
            A_cumsum = jnp.cumsum(A, axis=-1)
            decay_states = jnp.exp(A_cumsum[..., -1:] - A_cumsum)
            states = jnp.einsum('bclhn,bhcl,bclhp->bchpn', B, decay_states, x)
            A_chunk = jnp.pad(A_cumsum[..., -1], ((0, 0), (0, 0), (1, 0)))
            decay_chunk = jnp.exp(segsum(A_chunk))
            new_states = jnp.einsum('bhzc,bchpn->bzhpn', decay_chunk[:, :, :c, 1:c + 1], states)
            Y_off = jnp.einsum('bclhn,bchpn,bhcl->bclhp', C, new_states, jnp.exp(A_cumsum))
            return (Y_diag + Y_off).reshape(b, s, h, p)

        def mamba3_forward(u, in_proj_w, out_proj_w, D, dt_bias, A_log, bnorm_w, cnorm_w, ln_w, ln_b):
            b, s, _ = u.shape
            u_n = layer_norm(u, ln_w, ln_b)
            proj = jnp.einsum('bsd,ed->bse', u_n, in_proj_w)
            z = proj[..., :D_INNER]
            x = proj[..., D_INNER:2 * D_INNER]
            B = proj[..., 2 * D_INNER:2 * D_INNER + NGROUPS * D_STATE].reshape(b, s, NGROUPS, D_STATE)
            C = proj[..., 2 * D_INNER + NGROUPS * D_STATE:2 * D_INNER + 2 * NGROUPS * D_STATE].reshape(b, s, NGROUPS, D_STATE)
            dt = proj[..., -NHEADS:]
            B = rms_norm(B, bnorm_w)
            C = rms_norm(C, cnorm_w)
            x = x.reshape(b, s, NHEADS, HEADDIM)
            z = z.reshape(b, s, NHEADS, HEADDIM)
            dt_proc = jax.nn.softplus(dt + dt_bias)
            A = -jnp.exp(A_log)
            dA = dt_proc * A
            y = ssd_chunked(x, dA, B, C, CHUNK)
            y = y + x * D[None, None, :, None]
            y = y.reshape(b, s, D_INNER)
            z_flat = z.reshape(b, s, D_INNER)
            y = y * jax.nn.silu(z_flat)
            return u + jnp.einsum('bse,de->bsd', y, out_proj_w)
        return mamba3_forward(u, in_proj_w, out_proj_w, D, dt_bias, A_log, bnorm_w, cnorm_w, ln_w, ln_b)

    def _L0_ffn_ref(hidden_states, gate_w, w_gate, w_up, w_down, sw_gate, sw_up, sw_down, shared_gate_w):
        import jax, jax.numpy as jnp
        import numpy as np
        B, S, H = (2, 128, 256)
        E, K = (8, 2)
        I = 176
        IS = 704
        WSCALE = 0.02
        x = hidden_states
        logits = jnp.einsum('bsh,eh->bse', x, gate_w)
        probs = jax.nn.softmax(logits, axis=-1)
        top_w, top_i = jax.lax.top_k(probs, K)
        top_w = top_w / jnp.sum(top_w, axis=-1, keepdims=True)
        onehot = jax.nn.one_hot(top_i, E, dtype=x.dtype)
        combine = jnp.einsum('bsk,bske->bse', top_w, onehot)
        g = jnp.einsum('bsh,ehi->besi', x, w_gate)
        u = jnp.einsum('bsh,ehi->besi', x, w_up)
        h = jax.nn.silu(g) * u
        expert_out = jnp.einsum('besi,eih->besh', h, w_down)
        moe_out = jnp.einsum('besh,bse->bsh', expert_out, combine)
        sh = jax.nn.silu(x @ sw_gate) * (x @ sw_up)
        shared_out = sh @ sw_down
        shared_gate = jax.nn.sigmoid(x @ shared_gate_w)
        return moe_out + shared_out * shared_gate

    def _L1_attn_ref(x, Wq, Wk, Wv, Wa, ba, Wb, bb, qconv_w, qconv_b, kconv_w, kconv_b, vconv_w, vconv_b, Wg, Wo, ln_w, ln_b):
        import jax, jax.numpy as jnp
        from jax import lax
        import numpy as np
        B, T, HID = (1, 256, 256)
        H, DQ, DV, K = (16, 128, 128, 4)
        SCALE = DQ ** (-0.5)
        LN_EPS = 1e-05

        def _causal_depthwise_conv(x, w, b):
            C = w.shape[0]
            out = lax.conv_general_dilated(x.transpose(0, 2, 1), w[:, None, :], window_strides=(1,), padding=[(K - 1, 0)], feature_group_count=C, dimension_numbers=('NCH', 'OIH', 'NCH'))
            return (out + b[None, :, None]).transpose(0, 2, 1)

        def _delta_scan(q, k, v, a, beta):
            N = q.shape[0]

            def step(S, inp):
                q_t, k_t, v_t, a_t, b_t = inp
                sk = jnp.einsum('ndq,nq->nd', S, k_t)
                err = sk - v_t
                S = S * a_t[:, :, None] - (b_t[:, None] * err)[:, :, None] * k_t[:, None, :]
                o_t = jnp.einsum('ndq,nq->nd', S, q_t)
                return (S, o_t)
            S0 = jnp.zeros((N, DV, DQ), dtype=q.dtype)
            xs = (q.transpose(1, 0, 2), k.transpose(1, 0, 2), v.transpose(1, 0, 2), a.transpose(1, 0, 2), beta.transpose(1, 0))
            _, o = lax.scan(step, S0, xs)
            return o.transpose(1, 0, 2)
        b, t, _ = x.shape
        q = x @ Wq.T
        k = x @ Wk.T
        v = x @ Wv.T
        q = jax.nn.silu(_causal_depthwise_conv(q, qconv_w, qconv_b))
        k = jax.nn.silu(_causal_depthwise_conv(k, kconv_w, kconv_b))
        v = jax.nn.silu(_causal_depthwise_conv(v, vconv_w, vconv_b))
        q = q.reshape(b, t, H, DQ)
        k = k.reshape(b, t, H, DQ) * SCALE
        v = v.reshape(b, t, H, DV)
        a = jax.nn.sigmoid(x @ Wa.T + ba).reshape(b, t, H, DV)
        beta = jax.nn.sigmoid(x @ Wb.T + bb)
        to_n = lambda z: z.transpose(0, 2, 1, 3).reshape(b * H, t, -1)
        o = _delta_scan(to_n(q), to_n(k), to_n(v), to_n(a), beta.transpose(0, 2, 1).reshape(b * H, t))
        o = o.reshape(b, H, t, DV).transpose(0, 2, 1, 3)
        mu = o.mean(-1, keepdims=True)
        var = ((o - mu) ** 2).mean(-1, keepdims=True)
        o = (o - mu) * lax.rsqrt(var + LN_EPS) * ln_w + ln_b
        g = jax.nn.sigmoid(x @ Wg.T).reshape(b, t, H, DV)
        o = (o * g).reshape(b, t, H * DV)
        return o @ Wo.T

    def _L1_ffn_ref(hidden_states, gate_w, w1, w2, w3):
        import jax, jax.numpy as jnp
        import numpy as np
        JITTER_EPS = 0.01
        NUM_EXPERTS = 8
        TOP_K = 2
        HIDDEN = 256
        INTER = 512

        def _routing(logits):
            top2_vals, top2_idx = jax.lax.top_k(logits, TOP_K)

            def one_multiplier(thresh, base_scores, sel):
                factor = jnp.maximum(jnp.abs(logits), thresh)
                jitter_mask = (thresh - logits) / factor > 2.0 * JITTER_EPS
                s = jnp.where(jitter_mask, -jnp.inf, base_scores)
                p = jax.nn.softmax(s, axis=-1)
                return jnp.take_along_axis(p, sel[:, None], axis=-1)
            m1 = one_multiplier(top2_vals[:, 0:1], logits, top2_idx[:, 0])
            sel0_onehot = jax.nn.one_hot(top2_idx[:, 0], logits.shape[-1], dtype=bool)
            scores2 = jnp.where(sel0_onehot, -jnp.inf, logits)
            m2 = one_multiplier(top2_vals[:, 1:2], scores2, top2_idx[:, 1])
            multiplier = jnp.concatenate([m1, m2], axis=-1)
            return (multiplier, top2_idx)
        B, S, H = hidden_states.shape
        x = hidden_states.reshape(-1, H)
        logits = jnp.einsum('th,eh->te', x, gate_w)
        multiplier, top2_idx = _routing(logits)
        out = jnp.zeros_like(x)
        for e in range(NUM_EXPERTS):
            w_e = jnp.sum(multiplier * (top2_idx == e), axis=-1)
            h = jax.nn.silu(x @ w1[e].T) * (x @ w3[e].T)
            out = out + w_e[:, None] * (h @ w2[e].T)
        return out.reshape(B, S, H)
    x = L0_attn_u
    xn = _layernorm(x, axis=-1)
    x = x + _L0_attn_ref(xn, L0_attn_in_proj_w, L0_attn_out_proj_w, L0_attn_D, L0_attn_dt_bias, L0_attn_A_log, L0_attn_bnorm_w, L0_attn_cnorm_w, L0_attn_ln_w, L0_attn_ln_b) + _L0_ffn_ref(xn, L0_ffn_gate_w, L0_ffn_w_gate, L0_ffn_w_up, L0_ffn_w_down, L0_ffn_sw_gate, L0_ffn_sw_up, L0_ffn_sw_down, L0_ffn_shared_gate_w)
    xn = _layernorm(x, axis=-1)
    x = x + _L1_attn_ref(xn, L1_attn_Wq, L1_attn_Wk, L1_attn_Wv, L1_attn_Wa, L1_attn_ba, L1_attn_Wb, L1_attn_bb, L1_attn_qconv_w, L1_attn_qconv_b, L1_attn_kconv_w, L1_attn_kconv_b, L1_attn_vconv_w, L1_attn_vconv_b, L1_attn_Wg, L1_attn_Wo, L1_attn_ln_w, L1_attn_ln_b) + _L1_ffn_ref(xn, L1_ffn_gate_w, L1_ffn_w1, L1_ffn_w2, L1_ffn_w3)
    return x

_drawn_inputs = setup_inputs


def setup_inputs(seed=0):
    import zlib

    import numpy as np

    out = dict(_drawn_inputs(seed))
    spreads = {'L0_attn_D': (1.0, 0.6),
     'L0_attn_bnorm_w': (1.0, 0.2),
     'L0_attn_cnorm_w': (1.0, 0.2),
     'L0_attn_ln_w': (1.0, 0.2),
     'L0_attn_ln_b': (0.0, 0.1),
     'L1_attn_ba': (0.0, 0.1),
     'L1_attn_bb': (0.0, 0.8),
     'L1_attn_qconv_b': (0.0, 0.1),
     'L1_attn_kconv_b': (0.0, 0.1),
     'L1_attn_vconv_b': (0.0, 0.1),
     'L1_attn_ln_w': (1.0, 0.2),
     'L1_attn_ln_b': (0.0, 0.1)}
    factors = {'L0_ffn_gate_w': 3.244,
     'L0_ffn_w_gate': 3.002,
     'L0_ffn_w_up': 3.192,
     'L0_ffn_w_down': 2.87,
     'L0_ffn_shared_gate_w': 5.55}
    for name, (base, spread) in spreads.items():
        noise = np.random.default_rng([zlib.crc32(name.encode()), seed]).standard_normal(out[name].shape)
        drawn = base * np.exp(spread * noise) if base else spread * noise
        out[name] = jnp.asarray(drawn.astype(out[name].dtype))
    for name, factor in factors.items():
        out[name] = (out[name] * factor).astype(out[name].dtype)
    return out
```

```python
from contextlib import ExitStack

import concourse.bass as bass
from concourse import mybir

F32 = mybir.dt.float32
U32 = mybir.dt.uint32
ALU = mybir.AluOpType
ACT = mybir.ActivationFunctionType
AX = mybir.AxisListType

P = 128
EPS = 1e-5

T = 1024
DM = 256
KC = DM // P
NT = T // P

DI = 512
NH0 = 8
HP0 = DI // NH0
DS = 128
DPROJ = 2 * DI + 2 * DS + NH0
NBD = 2 * DS + NH0

E = 8
I0 = 176
I0B = I0 - P
IS = 704
ISC = 5
ISR = IS - ISC * P

H = 16
D = 128
CONV = 4
TB = 64
NB = T // TB
CH = 32
BK = 8
NCH = TB // CH
NBLK = CH // BK
HG = 4
NG = H // HG
SCALE = float(D) ** -0.5
LOGIT_FLOOR = -20.0

I1 = 512
IC1 = I1 // P


def program(nc, A, out):
    ctx = ExitStack()
    with ctx:
        sems = {}

        def sem(name):
            if name not in sems:
                sems[name] = ctx.enter_context(nc.semaphore(name))
            return sems[name]

        def sb(stack, name, shape, dt=F32):
            return stack.enter_context(nc.sbuf_tensor(name, shape, dt))

        xnT = sb(ctx, "xnT", [P, KC, T])
        ident = sb(ctx, "ident", [P, P])
        ones = sb(ctx, "ones", [P, P])
        mean_w = sb(ctx, "mean_w", [P, P])
        eps_t = sb(ctx, "eps_t", [P, 1])
        x1_dram = nc.dram_tensor("x1_scratch", (T, DM), F32, kind="Internal").ap()

        PS = [ctx.enter_context(nc.psum_tensor(f"bank{i}", [P, 512], F32)) for i in range(8)]

        with ExitStack() as rows_stack:
            x_rows = sb(rows_stack, "x_rows", [P, NT, DM])
            w_tok = sb(rows_stack, "w_tok", [P, NT, E])
            layer0(nc, A, sem, sb, PS, x_rows, xnT, w_tok, ident, ones, mean_w, eps_t)
            experts1(nc, A, sem, sb, PS, x_rows, xnT, w_tok, x1_dram)
        delta1(nc, A, sem, sb, PS, xnT, ident, ones, mean_w, eps_t, x1_dram, out)


def bc(ap, shape):
    return ap.broadcast_to(shape)


def layer0(nc, A, sem, sb, PS, x_rows, xnT, w_tok, ident, ones, mean_w, eps_t):
    with ExitStack() as st:
        def s(name, shape, dt=F32):
            return sb(st, "l0_" + name, shape, dt)

        win = s("win", [P, KC, DPROJ])
        wout = s("wout", [P, DI // P, DM])
        wg = s("wg", [P, E, KC, I0])
        wu = s("wu", [P, E, KC, I0])
        wda = s("wda", [P, E, DM])
        wdb = s("wdb", [I0B, E, DM])
        sg = s("sg", [P, KC, IS])
        su = s("su", [P, KC, IS])
        sda = s("sda", [P, ISC, DM])
        sdb = s("sdb", [ISR, DM])
        gate = s("gate", [P, KC, E + 1])
        gate1 = s("gate1", [P, KC, E])
        rows = s("rows", [P, 2 * DM + 2 * DS])
        hrows = s("hrows", [P, 3, NH0])
        triu = s("triu", [P, P])
        iota = s("iota", [P, E])
        neg_a = s("neg_a", [P, NH0])
        st6 = s("st6", [P, 6]); mv = s("mv", [P, 2]); std = s("std", [P, 1]); rstd = s("rstd", [P, 1])
        xn = s("xn", [P, DM]); un = s("un", [P, DM])
        xuT = s("xuT", [P, 2 * KC, P])
        zs = s("zs", [P, DI]); xs = s("xs", [P, DI])
        sq = s("sq", [P, 2, P]); ssq = s("ssq", [P, 2]); rms = s("rms", [P, 2]); rrms = s("rrms", [P, 2])
        bcn = s("bcn", [P, 2, DS]); bcT = s("bcT", [P, 2, P])
        dtv = s("dtv", [P, NH0]); dta = s("dta", [P, NH0]); dte = s("dte", [P, NH0]); dtl = s("dtl", [P, NH0])
        dA = s("dA", [P, NH0]); dAx = s("dAx", [P, NH0, P])
        cum = s("cum", [P, NH0]); tot = s("tot", [P, NH0]); dend = s("dend", [P, NH0])
        dec_end = s("dec_end", [P, NH0]); dec_in = s("dec_in", [P, NH0]); rho = s("rho", [P, NH0])
        Ld = s("Ld", [P, NH0, P]); Le = s("Le", [P, NH0, P]); Gm = s("Gm", [P, P])
        S0 = s("S0", [P, DI]); xdec = s("xdec", [P, DI])
        y = s("y", [P, DI]); yt = s("yt", [P, DI]); yT = s("yT", [P, DI // P, P])
        lg = s("lg", [P, E + 1]); m8 = s("m8", [P, 8]); i8 = s("i8", [P, 8], U32); i8f = s("i8f", [P, 8])
        nmax = s("nmax", [P, 1]); ex = s("ex", [P, E]); eq0 = s("eq0", [P, E]); eq1 = s("eq1", [P, E])
        msum = s("msum", [P, 1]); mrec = s("mrec", [P, 1]); cw = s("cw", [P, E + 1]); tg = s("tg", [P, 1])
        NGRP = 6
        hs = s("hs", [P, 2, 4, P])
        hA = s("hA", [P, E, P])
        hB = s("hB", [I0B, E, P])
        hS = s("hS", [P, ISC + 1, P])
        acc = s("acc", [P, DM]); wtmp = s("wtmp", [P, DM])
        m8b = s("m8b", [P, 8]); i8b = s("i8b", [P, 8], U32)
        fac = s("fac", [P, E]); dif = s("dif", [P, E]); keep = s("keep", [P, E])
        e12 = s("e12", [P, 2, E]); ek = s("ek", [P, 2, E]); den = s("den", [P, 2]); rden = s("rden", [P, 2])
        taken = s("taken", [P, 1])
        zero8 = s("zero8", [P, E]); ones8 = s("ones8", [P, E])
        x2n = s("x2n", [P, DM])

        groups = [[("e", e, 0, P) for e in range(4)], [("e", e, 0, P) for e in range(4, 8)],
                  [("e", e, P, I0B) for e in range(4)], [("e", e, P, I0B) for e in range(4, 8)],
                  [("s", c, c * P, P) for c in range(4)],
                  [("s", 4, 4 * P, P), ("s", 5, 5 * P, ISR)]]

        LOADS = [
            (x_rows[:], A["L0_attn_u"].rearrange("(n p) d -> p n d", p=P)),
            (win[:], A["in_projT"].rearrange("(k p) e -> p k e", p=P)),
            (rows[:, 0:DM], A["L0_attn_ln_w"].partition_broadcast(P)),
            (rows[:, DM:2 * DM], A["L0_attn_ln_b"].partition_broadcast(P)),
            (rows[:, 2 * DM:2 * DM + DS], A["L0_attn_bnorm_w"].partition_broadcast(P)),
            (rows[:, 2 * DM + DS:], A["L0_attn_cnorm_w"].partition_broadcast(P)),
            (hrows[:, 0], A["L0_attn_D"].partition_broadcast(P)),
            (hrows[:, 1], A["L0_attn_dt_bias"].partition_broadcast(P)),
            (hrows[:, 2], A["L0_attn_A_log"].partition_broadcast(P)),
            (wout[:], A["out_projT"].rearrange("(k p) e -> p k e", p=P)),
            (gate[:], A["gate0T"].rearrange("(k p) e -> p k e", p=P)),
            (gate1[:], A["gate1T"].rearrange("(k p) e -> p k e", p=P)),
            (wg[:, 0:4], A["L0_ffn_w_gate"][0:4].rearrange("e (k p) i -> p e k i", p=P)),
            (wg[:, 4:8], A["L0_ffn_w_gate"][4:8].rearrange("e (k p) i -> p e k i", p=P)),
            (wu[:, 0:4], A["L0_ffn_w_up"][0:4].rearrange("e (k p) i -> p e k i", p=P)),
            (wu[:, 4:8], A["L0_ffn_w_up"][4:8].rearrange("e (k p) i -> p e k i", p=P)),
            (sg[:], A["L0_ffn_sw_gate"].rearrange("(k p) i -> p k i", p=P)),
            (su[:], A["L0_ffn_sw_up"].rearrange("(k p) i -> p k i", p=P)),
            (wda[:], A["L0_ffn_w_down"][:, 0:P].rearrange("e p d -> p e d")),
            (wdb[:], A["L0_ffn_w_down"][:, P:I0].rearrange("e p d -> p e d")),
            (sda[:], A["L0_ffn_sw_down"][0:ISC * P].rearrange("(c p) d -> p c d", p=P)),
            (sdb[:], A["L0_ffn_sw_down"][ISC * P:IS]),
        ]
        loaded = sem("weights0_loaded")
        n_loads = len(LOADS)
        block = st.enter_context(nc.Block())

        @block.sync
        def _(sp):
            for dst, src in LOADS:
                sp.dma_start(dst, src).then_inc(loaded, 16)

        @block.gpsimd
        def _(g):
            const = sem("const_step")
            g.memset(ident[:], 0.0).then_inc(const, 1)
            g.memset(triu[:], 1.0).then_inc(const, 1)
            g.wait_ge(const, 2)
            g.affine_select(out=ident[:], in_=ident[:], compare_op=ALU.not_equal, fill=1.0,
                            base=0, pattern=[[-1, P]], channel_multiplier=1)
            g.affine_select(out=triu[:], in_=triu[:], compare_op=ALU.is_ge, fill=0.0,
                            base=0, pattern=[[1, P]], channel_multiplier=-1)
            g.iota(iota[:], pattern=[[1, E]], base=0, channel_multiplier=0,
                   allow_small_or_imprecise_dtypes=True).then_inc(sem("consts_ready"), 1)

        @block.vector
        def _(v):
            chain, count = sem("vec0_step"), [0]

            def link(ins, n=None):
                ins.then_inc(chain, 1)
                count[0] += 1
                v.wait_ge(chain, count[0] if n is None else n * PER + count[0])
            v.memset(ones[:], 1.0)
            v.memset(mean_w[:], 1.0 / P)
            v.memset(zero8[:], 0.0)
            v.memset(ones8[:], 1.0)
            v.memset(S0[:], 0.0)
            v.memset(eps_t[:], EPS).then_inc(sem("vconst_ready"), 1)
            v.wait_ge(sem("vconst_ready"), 1)
            v.wait_ge(loaded, 16 * n_loads)
            v.wait_ge(sem("consts_ready"), 1)
            v.wait_ge(sem("nega_exp"), 1)
            v.tensor_scalar(neg_a[:], neg_a[:], -1.0, None, ALU.mult).then_inc(sem("tile0_done"), 1)
            v.wait_ge(sem("tile0_done"), 1)

            with v.Fori(0, NT) as n:
                m = [0]

                def step(ins):
                    ins.then_inc(chain, 1)
                    m[0] += 1
                    v.wait_ge(chain, n * STEPS0 + m[0])

                def take_wait():
                    v.memset(taken[:], 0.0)

                def normed(dst, src, k):
                    take_wait()
                    step(v.bn_stats(st6[:], src))
                    take_wait()
                    v.bn_aggr(mv[:], st6[:]).then_inc(sem("moments"), 1)
                    v.wait_ge(sem("std_ready"), 3 * n + k)
                    step(v.reciprocal(rstd[:], std[:]))
                    return v.tensor_scalar(dst, src, mv[:, 0:1], rstd[:, 0:1], ALU.subtract, ALU.mult)

                step(normed(xn[:], x_rows[:, n, :], 1))
                step(normed(un[:], xn[:], 2))
                step(v.tensor_tensor(un[:], un[:], rows[:, 0:DM], ALU.mult))
                v.tensor_tensor(un[:], un[:], rows[:, DM:2 * DM], ALU.add).then_inc(sem("xn_un"), 1)
                v.tensor_tensor(acc[:], x_rows[:, n, :], xn[:], ALU.add)
                v.wait_ge(sem("proj_done"), n + 1)
                v.tensor_copy(xs[:], PS[2][:])
                step(v.tensor_tensor(dtv[:], PS[3][:, 2 * DS:NBD], hrows[:, 1], ALU.add))
                v.scalar_tensor_tensor(out=dta[:], in0=dtv[:], scalar=-1.0, in1=dtv[:],
                                       op0=ALU.mult, op1=ALU.max).then_inc(sem("dt_abs"), 1)
                v.wait_ge(sem("ssq_rms"), n + 1)
                step(v.reciprocal(rrms[:], rms[:]))
                for j in range(2):
                    last = v.scalar_tensor_tensor(
                        out=bcn[:, j], in0=PS[3][:, j * DS:(j + 1) * DS], scalar=rrms[:, j:j + 1],
                        in1=rows[:, 2 * DM + j * DS:2 * DM + (j + 1) * DS], op0=ALU.mult, op1=ALU.mult)
                last.then_inc(sem("bc_normed"), 1)
                v.wait_ge(sem("dt_ln"), n + 1)
                step(v.scalar_tensor_tensor(out=dtv[:], in0=dtv[:], scalar=0.0, in1=dtl[:],
                                            op0=ALU.max, op1=ALU.add))
                step(v.tensor_tensor(dA[:], dtv[:], neg_a[:], ALU.mult))
                v.tensor_tensor(dAx[:], bc(triu[:].unsqueeze(1), [P, NH0, P]),
                                bc(dA[:].unsqueeze(2), [P, NH0, P]), ALU.mult).then_inc(sem("dA_ready"), 1)
                v.wait_ge(sem("cum_done"), n + 1)
                v.tensor_copy(tot[:], PS[6][:, NH0:2 * NH0])
                step(v.tensor_copy(cum[:], PS[6][:, 0:NH0]))
                step(v.tensor_tensor(dend[:], tot[:], cum[:], ALU.subtract))
                for h in range(NH0):
                    last = v.tensor_scalar(Ld[:, h, :], PS[4 + h // 4][:, (h % 4) * P:(h % 4 + 1) * P],
                                           cum[:, h:h + 1], 0.0, ALU.subtract, ALU.min)
                last.then_inc(sem("logs_ready"), 1)
                v.wait_ge(sem("gram_done"), n + 1)
                step(v.tensor_tensor(Gm[:], PS[7][:, 0:P], triu[:], ALU.mult))
                v.wait_ge(sem("exps_ready"), n + 1)
                v.tensor_tensor(xdec[:].rearrange("p (h q) -> p h q", h=NH0),
                                xs[:].rearrange("p (h q) -> p h q", h=NH0),
                                bc(dec_end[:].unsqueeze(2), [P, NH0, HP0]), ALU.mult)
                v.tensor_tensor(Le[:], Le[:], bc(Gm[:].unsqueeze(1), [P, NH0, P]),
                                ALU.mult).then_inc(sem("mix_ready"), 1)
                v.tensor_tensor(yt[:].rearrange("p (h q) -> p h q", h=NH0),
                                xs[:].rearrange("p (h q) -> p h q", h=NH0),
                                bc(hrows[:, 0].unsqueeze(2), [P, NH0, HP0]), ALU.mult)
                v.wait_ge(sem("y_done"), n + 1)
                step(v.tensor_tensor(y[:].rearrange("p (h q) -> p h q", h=NH0),
                                     PS[2][:].rearrange("p (h q) -> p h q", h=NH0),
                                     bc(dec_in[:].unsqueeze(2), [P, NH0, HP0]), ALU.mult))
                step(v.tensor_tensor(y[:], y[:], PS[1][:], ALU.add))
                step(v.tensor_tensor(y[:], y[:], yt[:], ALU.add))
                v.tensor_tensor(y[:], y[:], zs[:], ALU.mult).then_inc(sem("y_ready"), 1)
                step(v.tensor_tensor(S0[:].rearrange("p (h q) -> p h q", h=NH0),
                                     S0[:].rearrange("p (h q) -> p h q", h=NH0),
                                     bc(rho[:].unsqueeze(2), [P, NH0, HP0]), ALU.mult))
                step(v.tensor_tensor(S0[:], S0[:], PS[3][:], ALU.add))

                v.wait_ge(sem("logits_done"), n + 1)
                step(v.tensor_copy(lg[:], PS[6][:, 256:256 + E + 1]))
                take_wait()
                step(v.max(m8[:], lg[:, 0:E]))
                take_wait()
                step(v.max_index(i8[:], m8[:], lg[:, 0:E]))
                v.tensor_copy(i8f[:], i8[:])
                v.tensor_scalar(nmax[:], m8[:, 0:1], -1.0, None, ALU.mult).then_inc(sem("nmax0"), 1)
                v.wait_ge(sem("nmax0"), n + 1)
                v.tensor_scalar(eq0[:], iota[:], i8f[:, 0:1], None, ALU.is_equal)
                step(v.tensor_scalar(eq1[:], iota[:], i8f[:, 1:2], None, ALU.is_equal))
                step(v.tensor_tensor(eq0[:], eq0[:], eq1[:], ALU.add))
                v.wait_ge(sem("router_exp"), n + 1)
                step(v.tensor_tensor(ex[:], ex[:], eq0[:], ALU.mult))
                step(v.reduce_sum(msum[:], ex[:], AX.X))
                step(v.reciprocal(mrec[:], msum[:]))
                v.tensor_scalar(cw[:, 0:E], ex[:], mrec[:, 0:1], None, ALU.mult)
                step(v.tensor_scalar(cw[:, E:E + 1], tg[:], 1.0, 0.5, ALU.add, ALU.mult))

                v.wait_ge(sem("mixer_done"), n + 1)
                step(v.tensor_tensor(acc[:], acc[:], PS[1][:, 0:DM], ALU.add))

                for gi, grp in enumerate(groups):
                    v.wait_ge(sem("up_done"), NGRP * n + gi + 1)
                    v.wait_ge(sem("silu_done"), NGRP * n + gi + 1)
                    ub = PS[5 if gi % 2 == 0 else 7]
                    kind, c0 = grp[0][0], grp[0][1]
                    if gi == 5:
                        v.tensor_tensor(hS[:, 4, :], hs[:, 1, 0, :], ub[:, 0:P], ALU.mult)
                        last = v.tensor_tensor(hS[0:ISR, 5, :], hs[0:ISR, 1, 1, :], ub[0:ISR, P:2 * P], ALU.mult)
                    else:
                        m_rows = grp[0][3]
                        dst = {"s": hS}.get(kind, hA if m_rows == P else hB)
                        last = v.tensor_tensor(
                            dst[0:m_rows, c0:c0 + 4, :], hs[0:m_rows, gi % 2],
                            ub[0:m_rows].rearrange("p (c t) -> p c t", c=4), ALU.mult)
                    last.then_inc(sem("h_ready"), 1)
                for e in range(E + 1):
                    v.wait_ge(sem("down_done"), (E + 1) * n + e + 1)
                    v.scalar_tensor_tensor(out=acc[:] if e < E else x_rows[:, n, :],
                                           in0=PS[1 + e % 2][:, 0:DM], scalar=cw[:, e:e + 1], in1=acc[:],
                                           op0=ALU.mult, op1=ALU.add).then_inc(sem("down_used"), 1)
                    v.wait_ge(sem("down_used"), (E + 1) * n + e + 1)
                normed(x2n[:], x_rows[:, n, :], 3).then_inc(sem("x2n"), 1)
                v.wait_ge(sem("logits1_done"), n + 1)
                lg1 = lg[:, 0:E]
                step(v.tensor_copy(lg1, PS[6][:, 0:E]))
                take_wait()
                step(v.max(m8b[:], lg1))
                take_wait()
                step(v.max_index(i8b[:], m8b[:], lg1))
                v.tensor_copy(i8f[:], i8b[:])
                v.tensor_scalar(ek[:, 0], lg1, m8b[:, 0:1], 0.0, ALU.subtract, ALU.min)
                v.tensor_scalar(ek[:, 1], lg1, m8b[:, 1:2], 0.0, ALU.subtract, ALU.min).then_inc(sem("nmax1"), 1)
                v.wait_ge(sem("nmax1"), n + 1)
                v.tensor_scalar(eq0[:], iota[:], i8f[:, 0:1], None, ALU.is_equal)
                step(v.tensor_scalar(eq1[:], iota[:], i8f[:, 1:2], None, ALU.is_equal))
                v.wait_ge(sem("router_exp1"), n + 1)
                for j in range(2):
                    step(v.scalar_tensor_tensor(out=fac[:], in0=lg1, scalar=-1.0, in1=lg1, op0=ALU.mult, op1=ALU.max))
                    step(v.tensor_scalar(fac[:], fac[:], m8b[:, j:j + 1], None, ALU.max))
                    step(v.tensor_scalar(dif[:], lg1, -1.0, m8b[:, j:j + 1], ALU.mult, ALU.add))
                    step(v.scalar_tensor_tensor(out=keep[:], in0=fac[:], scalar=0.02, in1=dif[:],
                                                op0=ALU.mult, op1=ALU.is_ge))
                    if j == 1:
                        step(v.tensor_tensor(fac[:], ones8[:], eq0[:], ALU.subtract))
                        step(v.tensor_tensor(keep[:], keep[:], fac[:], ALU.mult))
                    step(v.tensor_tensor(ek[:, j], e12[:, j], keep[:], ALU.mult))
                    step(v.reduce_sum(den[:, j:j + 1], ek[:, j], AX.X))
                step(v.reciprocal(rden[:], den[:]))
                step(v.tensor_scalar(eq0[:], eq0[:], rden[:, 0:1], None, ALU.mult))
                step(v.scalar_tensor_tensor(out=w_tok[:, n, :], in0=eq1[:], scalar=rden[:, 1:2], in1=eq0[:],
                                            op0=ALU.mult, op1=ALU.add))
                v.wait_ge(sem("x2nT_kept"), n + 1)
                v.tensor_copy(tg[:], tg[:]).then_inc(sem("tile0_done"), 1)
                assert m[0] == STEPS0, m[0]

        @block.scalar
        def _(a):
            a.wait_ge(loaded, 16 * n_loads)
            a.wait_ge(sem("vconst_ready"), 1)
            a.activation(neg_a[:], hrows[:, 2], ACT.Exp).then_inc(sem("nega_exp"), 1)
            with a.Fori(0, NT) as n:
                m = [0]

                def step(ins):
                    ins.then_inc(sem("act0_step"), 1)
                    m[0] += 1
                    a.wait_ge(sem("act0_step"), n * ASTEPS0 + m[0])

                def std_of(k):
                    a.wait_ge(sem("moments"), 3 * n + k)
                    a.activation(std[:], mv[:, 1:2], ACT.Sqrt, bias=eps_t[:, 0:1]).then_inc(sem("std_ready"), 1)

                std_of(1)
                std_of(2)
                a.wait_ge(sem("xn_T"), n + 1)
                a.copy(xuT[:].rearrange("p c t -> p (c t)"), PS[0][:]).then_inc(sem("xuT_ready"), 1)
                a.wait_ge(sem("dt_abs"), n + 1)
                for j in range(2):
                    last = a.activation(sq[:, j], PS[3][:, j * DS:(j + 1) * DS], ACT.Square,
                                        accum_out=ssq[:, j:j + 1])
                step(last)
                a.activation(rms[:], ssq[:], ACT.Sqrt, bias=eps_t[:, 0:1],
                             scale=1.0 / DS).then_inc(sem("ssq_rms"), 1)
                a.activation(zs[:], PS[1][:], ACT.Silu)
                step(a.activation(dte[:], dta[:], ACT.Exp, scale=-1.0))
                a.activation(dtl[:], dte[:], ACT.Ln, bias=1.0).then_inc(sem("dt_ln"), 1)
                a.wait_ge(sem("bcT_done"), n + 1)
                a.copy(bcT[:].rearrange("p c t -> p (c t)"), PS[0][:, 0:2 * P]).then_inc(sem("bcT_ready"), 1)
                a.wait_ge(sem("logs_ready"), n + 1)
                a.activation(dec_in[:], cum[:], ACT.Exp)
                a.activation(rho[:], tot[:], ACT.Exp)
                a.activation(dec_end[:], dend[:], ACT.Exp)
                a.activation(Le[:], Ld[:], ACT.Exp).then_inc(sem("exps_ready"), 1)
                a.wait_ge(sem("nmax0"), n + 1)
                a.activation(ex[:], lg[:, 0:E], ACT.Exp, bias=nmax[:, 0:1])
                a.activation(tg[:], lg[:, E:E + 1], ACT.Tanh, scale=0.5).then_inc(sem("router_exp"), 1)
                a.wait_ge(sem("yT_done"), n + 1)
                a.copy(yT[:].rearrange("p c t -> p (c t)"), PS[0][:]).then_inc(sem("yT_ready"), 1)
                for gi, grp in enumerate(groups):
                    a.wait_ge(sem("up_done"), NGRP * n + gi + 1)
                    if gi >= 2:
                        a.wait_ge(sem("h_ready"), NGRP * n + gi - 1)
                    gb = PS[4 if gi % 2 == 0 else 6]
                    if gi == 5:
                        a.activation(hs[:, 1, 0, :], gb[:, 0:P], ACT.Silu)
                        last = a.activation(hs[0:ISR, 1, 1, :], gb[0:ISR, P:2 * P], ACT.Silu)
                    else:
                        r = grp[0][3]
                        last = a.activation(hs[0:r, gi % 2].rearrange("p c t -> p (c t)"), gb[0:r, :], ACT.Silu)
                    last.then_inc(sem("silu_done"), 1)
                std_of(3)
                a.wait_ge(sem("x2nT_done"), n + 1)
                a.copy(xuT[:, 0:KC, :].rearrange("p c t -> p (c t)"), PS[0][:, 0:2 * P]).then_inc(sem("x2nT_ready"), 1)
                a.copy(xnT[:, :, bass.ts(n, P)], PS[0][:, 0:2 * P].rearrange("p (c t) -> p c t", c=KC)).then_inc(sem("x2nT_kept"), 1)
                a.wait_ge(sem("nmax1"), n + 1)
                last = a.activation(e12[:], ek[:], ACT.Exp)
                last.then_inc(sem("router_exp1"), 1)
                assert m[0] == ASTEPS0, m[0]

        @block.tensor
        def _(pe):
            pe.wait_ge(loaded, 16 * n_loads)
            pe.wait_ge(sem("consts_ready"), 1)
            with pe.Fori(0, NT) as n:
                pe.wait_ge(sem("tile0_done"), n + 1)
                pe.wait_ge(sem("xn_un"), n + 1)
                for j in range(2):
                    for k in range(KC):
                        last = pe.transpose(PS[0][:, (2 * j + k) * P:(2 * j + k + 1) * P],
                                            (xn, un)[j][:, k * P:(k + 1) * P], ident[:])
                last.then_inc(sem("xn_T"), 1)
                pe.wait_ge(sem("xuT_ready"), n + 1)
                for b, (c0, c1) in enumerate([(0, DI), (DI, 2 * DI), (2 * DI, DPROJ)]):
                    for k in range(KC):
                        last = pe.matmul(PS[1 + b][:, 0:c1 - c0], xuT[:, KC + k, :], win[:, k, c0:c1],
                                         start=(k == 0), stop=(k == KC - 1))
                last.then_inc(sem("proj_done"), 1)
                pe.wait_ge(sem("bc_normed"), n + 1)
                for j in range(2):
                    last = pe.transpose(PS[0][:, j * P:(j + 1) * P], bcn[:, j], ident[:])
                last.then_inc(sem("bcT_done"), 1)
                pe.wait_ge(sem("dA_ready"), n + 1)
                pe.matmul(PS[6][:, 0:NH0], triu[:], dA[:], start=True, stop=True)
                pe.matmul(PS[6][:, NH0:2 * NH0], ones[:], dA[:], start=True, stop=True)
                for b in range(2):
                    last = pe.matmul(PS[4 + b][:], ones[:], dAx[:, 4 * b:4 * b + 4, :], start=True, stop=True)
                last.then_inc(sem("cum_done"), 1)
                pe.wait_ge(sem("bcT_ready"), n + 1)
                pe.matmul(PS[7][:, 0:P], bcT[:, 0], bcT[:, 1], start=True, stop=True).then_inc(sem("gram_done"), 1)
                pe.wait_ge(sem("logs_ready"), n + 1)
                for k in range(KC):
                    last = pe.matmul(PS[6][:, 256:256 + E + 1], xuT[:, k, :], gate[:, k, :],
                                     start=(k == 0), stop=(k == KC - 1))
                last.then_inc(sem("logits_done"), 1)
                pe.wait_ge(sem("mix_ready"), n + 1)
                pe.matmul(PS[2][:], bcT[:, 1], S0[:], start=True, stop=True)
                for h in range(NH0):
                    pe.matmul(PS[1][:, h * HP0:(h + 1) * HP0], Le[:, h, :], xs[:, h * HP0:(h + 1) * HP0],
                              start=True, stop=True)
                pe.matmul(PS[3][:], bcn[:, 0], xdec[:], start=True, stop=True).then_inc(sem("y_done"), 1)
                pe.wait_ge(sem("y_ready"), n + 1)
                for c in range(DI // P):
                    last = pe.transpose(PS[0][:, c * P:(c + 1) * P], y[:, c * P:(c + 1) * P], ident[:])
                last.then_inc(sem("yT_done"), 1)
                pe.wait_ge(sem("yT_ready"), n + 1)
                for c in range(DI // P):
                    last = pe.matmul(PS[1][:, 0:DM], yT[:, c, :], wout[:, c, :], start=(c == 0), stop=(c == DI // P - 1))
                last.then_inc(sem("mixer_done"), 1)
                for gi, grp in enumerate(groups):
                    if gi == 1:
                        pe.wait_ge(sem("nmax0"), n + 1)
                    if gi >= 2:
                        pe.wait_ge(sem("h_ready"), NGRP * n + gi - 1)
                    gb, ub = (PS[4], PS[5]) if gi % 2 == 0 else (PS[6], PS[7])
                    for bank, we, ws in ((gb, wg, sg), (ub, wu, su)):
                        for c, (kind, e, i0, r) in enumerate(grp):
                            for k in range(KC):
                                w = we[:, e, k, i0:i0 + r] if kind == "e" else ws[:, k, i0:i0 + r]
                                last = pe.matmul(bank[0:r, c * P:(c + 1) * P], w, xuT[:, k, :],
                                                 start=(k == 0), stop=(k == KC - 1))
                    last.then_inc(sem("up_done"), 1)
                pe.wait_ge(sem("h_ready"), NGRP * n + NGRP)
                for e in range(E + 1):
                    o = PS[1 + e % 2][:, 0:DM]
                    if e >= 2:
                        pe.wait_ge(sem("down_used"), (E + 1) * n + e - 1)
                    if e < E:
                        pe.matmul(o, hA[:, e, :], wda[:, e, :], start=True, stop=False)
                        last = pe.matmul(o, hB[:, e, :], wdb[:, e, :], start=False, stop=True)
                    else:
                        for c in range(ISC):
                            pe.matmul(o, hS[:, c, :], sda[:, c, :], start=(c == 0), stop=False)
                        last = pe.matmul(o, hS[0:ISR, ISC, :], sdb[:], start=False, stop=True)
                    last.then_inc(sem("down_done"), 1)
                pe.wait_ge(sem("x2n"), n + 1)
                for k in range(KC):
                    last = pe.transpose(PS[0][:, k * P:(k + 1) * P], x2n[:, k * P:(k + 1) * P], ident[:])
                last.then_inc(sem("x2nT_done"), 1)
                pe.wait_ge(sem("x2nT_ready"), n + 1)
                for k in range(KC):
                    last = pe.matmul(PS[6][:, 0:E], xuT[:, k, :], gate1[:, k, :],
                                     start=(k == 0), stop=(k == KC - 1))
                last.then_inc(sem("logits1_done"), 1)


STEPS0 = 52
ASTEPS0 = 2


def experts1(nc, A, sem, sb, PS, x_rows, xnT, w_tok, x1_dram):
    with ExitStack() as st:
        NW = 2
        w1 = [sb(st, f"w1_{i}", [P, KC, I1]) for i in range(NW)]
        w3 = [sb(st, f"w3_{i}", [P, KC, I1]) for i in range(NW)]
        w2 = [sb(st, f"w2_{i}", [P, IC1, DM]) for i in range(NW)]
        hs = sb(st, "hs1", [P, 2, 512])
        mark = sb(st, "mark1", [P, 5])
        h = sb(st, "h1", [P, 2, IC1, 512])
        HALVES = T // 512
        UPS = HALVES * IC1
        DOWNS = T // P
        loaded = [sem(f"w1_loaded{i}") for i in range(NW)]
        block = st.enter_context(nc.Block())
        d1 = A["w1T"].rearrange("e (k p) i -> e p k i", p=P)
        d3 = A["w3T"].rearrange("e (k p) i -> e p k i", p=P)
        d2 = A["w2T"].rearrange("e (k p) i -> e p k i", p=P)

        @block.sync
        def _(sp):
            for i in range(NW):
                for dst, src in ((w1, d1), (w3, d3), (w2, d2)):
                    sp.dma_start(dst[i][:], src[i]).then_inc(loaded[i], 16)
            with sp.Fori(1, E // NW) as g:
                for i in range(NW):
                    e = sp.snap(g * NW + i)
                    sp.wait_ge(sem("down1_done"), g * (NW * DOWNS) + (i + 1 - NW) * DOWNS)
                    for dst, src in ((w1, d1), (w3, d3), (w2, d2)):
                        sp.dma_start(dst[i][:], src[bass.ds(e, 1)].rearrange("o p k i -> (o p) k i")).then_inc(loaded[i], 16)
            sp.wait_ge(sem("experts1_done"), 1)
            sp.dma_start(x1_dram.rearrange("(n p) d -> p n d", p=P), x_rows[:]).then_inc(sem("x1_stored"), 16)
            sp.wait_ge(sem("x1_stored"), 16)

        @block.tensor
        def _(pe):
            with pe.Fori(0, E // NW) as g:
                for i in range(NW):
                    pe.wait_ge(loaded[i], g * 48 + 48)
                    for half in range(HALVES):
                        for c in range(IC1):
                            u = half * IC1 + c
                            pe.wait_ge(sem("h1_ready"), g * (NW * UPS) + i * UPS + u + 1)
                            for b, w in ((0, w1), (1, w3)):
                                for k in range(KC):
                                    last = pe.matmul(PS[2 * (u % 2) + b][:], w[i][:, k, c * P:(c + 1) * P],
                                                     xnT[:, k, half * 512:(half + 1) * 512],
                                                     start=(k == 0), stop=(k == KC - 1))
                            last.then_inc(sem("up1_done"), 1)
                        pe.wait_ge(sem("h1_ready"), g * (NW * UPS) + i * UPS + (half + 1) * IC1 + 2)
                        for t in range(4):
                            n = half * 4 + t
                            pe.wait_ge(sem("down1_used"), g * (NW * DOWNS) + i * DOWNS + n + 1)
                            for c in range(IC1):
                                last = pe.matmul(PS[4 + n % 2][:, 0:DM], h[:, half, c, t * P:(t + 1) * P],
                                                 w2[i][:, c, :], start=(c == 0), stop=(c == IC1 - 1))
                            last.then_inc(sem("down1_done"), 1)

        @block.scalar
        def _(a):
            with a.Fori(0, E // NW) as g:
                for i in range(NW):
                    for u in range(UPS):
                        a.wait_ge(sem("up1_done"), g * (NW * UPS) + i * UPS + u + 1)
                        a.wait_ge(sem("h1_ready"), g * (NW * UPS) + i * UPS + u + 1)
                        a.activation(hs[:, u % 2], PS[2 * (u % 2)][:], ACT.Silu).then_inc(sem("silu1_done"), 1)

        @block.vector
        def _(v):
            for j, name in enumerate(("h1_ready", "h1_ready", "down1_used", "down1_used")):
                v.memset(mark[:, j:j + 1], 0.0).then_inc(sem(name), 1)
            with v.Fori(0, E // NW) as g:
                for i in range(NW):
                    for half in range(HALVES):
                        for c in range(IC1):
                            u = half * IC1 + c
                            v.wait_ge(sem("silu1_done"), g * (NW * UPS) + i * UPS + u + 1)
                            v.tensor_tensor(h[:, half, c, :], hs[:, u % 2], PS[2 * (u % 2) + 1][:],
                                            ALU.mult).then_inc(sem("h1_ready"), 1)
                        for t in range(4):
                            n = half * 4 + t
                            v.wait_ge(sem("down1_done"), g * (NW * DOWNS) + i * DOWNS + n + 1)
                            v.scalar_tensor_tensor(
                                out=x_rows[:, n, :], in0=PS[4 + n % 2][:, 0:DM],
                                scalar=w_tok[:, n, bass.ds(g * NW + i, 1)], in1=x_rows[:, n, :],
                                op0=ALU.mult, op1=ALU.add).then_inc(sem("down1_used"), 1)
            v.wait_ge(sem("down1_used"), E * DOWNS + 2)
            v.memset(mark[:, 4:5], 0.0).then_inc(sem("experts1_done"), 1)


def delta1(nc, A, sem, sb, PS, xnT, ident, ones, mean_w, eps_t, x1_dram, out):
    with ExitStack() as st:
        def s(name, shape, dt=F32):
            return sb(st, "l1_" + name, shape, dt)

        wp = [s(f"wp_{x}", [P, KC, H * D]) for x in "qkvag"]
        wo = s("wo", [P, H, DM])
        wb = s("wb", [P, KC, H])
        cw = s("cw", [P, 3, H, CONV]); cb = s("cb", [P, 3, H]); ba = s("ba", [P, H]); bb = s("bb", [H, 1]); nbb = s("nbb", [H, 1])
        lnw = s("lnw", [P, 1]); lnb = s("lnb", [P, 1])
        maskh = s("maskh", [P, HG, 1])
        pr = s("pr", [P, H, NBLK, 64])
        raw = pr[:].rearrange("p h b w -> p (h b w)")[:, 0:3 * H * (TB + CONV - 1)].rearrange(
            "p (x h t) -> p x h t", x=3, h=H)
        halo = s("halo", [P, 3, H, CONV - 1])
        ca = s("ca", [P, H, TB])
        kq = s("kq", [P, H, TB, 2])
        kb = s("kb", [P, NCH, H, CH])
        vv = s("vv", [P, H, TB])
        ia = s("ia", [P, H, TB])
        aa = s("aa", [P, H, TB])
        gg = s("gg", [P, H, TB])
        Ef = s("Ef", [P, H * TB // BK, BK]); Ei = s("Ei", [P, H * TB // BK, BK])
        eref = s("eref", [P, H, TB // BK]); rho = s("rho", [P, H, TB // BK])
        dcy = s("dcy", [P, H, NBLK + 1]); edc = s("edc", [P, H, NBLK])
        bt = s("bt", [H, TB])
        gb = s("gb", [P, 2, H, 64])
        gs = s("gs", [P, NG, HG, 2 * CH])
        kr = s("kr", [P, NG, D])
        y0 = ca
        cbuf = osq = gb[:, 0]
        tmp = s("tmp", [P, H, 16]); z = s("z", [P, H, BK])
        hist = s("hist", [P, H, CH]); hT = s("hT", [P, NG, D])
        S = s("S", [P, H, D]); sT = s("sT", [P, H, D])
        o = aa
        on = s("on", [P, H, TB])
        be = on[0:H]
        mark = s("mark", [P, 3])
        xr = s("xr", [TB, DM])

        LOADS = [
            *[(wp[i][:], A[f"W{x}T"].rearrange("(k p) e -> p k e", p=P)) for i, x in enumerate("qkvag")],
            (wb[:], A["WbT"].rearrange("(k p) e -> p k e", p=P)),
            *[(cw[:, i], A[f"{x}conv_wT"]) for i, x in enumerate("qkv")],
            *[(cb[:, i], A[f"{x}conv_bT"]) for i, x in enumerate("qkv")],
            (ba[:], A["baT"]), (bb[:], A["bbT"]), (lnw[:], A["ln_wT"]), (lnb[:], A["ln_bT"]),
            (wo[:], A["WoT"].rearrange("(h p) e -> p h e", p=P)),
        ]
        loaded = sem("delta_loaded")
        block = st.enter_context(nc.Block())
        offs = [sum(15 - 2 * q for q in range(t)) for t in range(BK + 1)]

        def heads(ap8):
            return ap8.rearrange("p (h t) -> p h t", h=8)

        @block.sync
        def _(sp):
            for dst, src in LOADS:
                sp.dma_start(dst, src).then_inc(loaded, 16)
            sp.dma_start(xr[:], x1_dram[0:TB]).then_inc(sem("xr_loaded"), 16)
            with sp.Fori(0, NB - 1) as i:
                row = sp.snap(i * TB)
                next_row = sp.snap(i * TB + TB)
                sp.wait_ge(sem("xo_ready"), i + 1)
                sp.dma_start(out[bass.ds(row, TB)], xr[:]).then_inc(sem("out_stored"), 16)
                sp.wait_ge(sem("out_stored"), i * 16 + 16)
                sp.dma_start(xr[:], x1_dram[bass.ds(next_row, TB)]).then_inc(sem("xr_loaded"), 16)
            sp.wait_ge(sem("xo_ready"), NB)
            sp.dma_start(out[T - TB:T], xr[:]).then_inc(sem("out_stored"), 16)
            sp.wait_ge(sem("out_stored"), 16 * NB)

        @block.gpsimd
        def _(g):
            g.memset(maskh[:], 1.0).then_inc(sem("pconst"), 1)
            g.wait_ge(sem("pconst"), 1)
            g.affine_select(out=maskh[:, :, 0], in_=maskh[:, :, 0], compare_op=ALU.is_ge, fill=0.0, base=0,
                            pattern=[[-CH, HG]], channel_multiplier=1).then_inc(sem("pconst"), 1)
            g.wait_ge(sem("pconst"), 2)
            g.affine_select(out=maskh[:, :, 0], in_=maskh[:, :, 0], compare_op=ALU.is_ge, fill=0.0, base=CH - 1,
                            pattern=[[CH, HG]], channel_multiplier=-1).then_inc(sem("mask_ready"), 1)
            with g.Fori(0, NB) as i:
                g.wait_ge(sem("kb_ready"), i + 1)
                for c in range(NCH):
                    if c:
                        g.wait_ge(sem("gbc_done"), i * (NCH * NBLK) + c * NBLK)
                    kqc = kq[:].rearrange("p h t j -> p h (t j)")
                    for t in range(BK):
                        w = 15 - 2 * t
                        for b in range(NBLK):
                            t0 = c * CH + b * BK
                            last = g.tensor_tensor(
                                pr[:, :, b, offs[t]:offs[t] + w],
                                kqc[:, :, 2 * t0 + 2 * t + 1:2 * t0 + 2 * BK],
                                bc(kb[:, c, :, b * BK + t:b * BK + t + 1], [P, H, w]), ALU.mult)
                    last.then_inc(sem("pairs_ready"), 1)

        @block.vector
        def _(v):
            chain = sem("vec1_step")
            v.memset(S[:], 0.0)
            v.memset(Ef[:], 1.0)
            v.memset(Ei[:], 1.0)
            v.memset(sT[:], 0.0)
            v.memset(halo[:], 0.0).then_inc(sem("halo_ready"), 1)
            v.wait_ge(loaded, 16 * len(LOADS))
            v.wait_ge(sem("mask_ready"), 1)
            v.tensor_scalar(nbb[:], bb[:], -1.0, None, ALU.mult).then_inc(sem("bb_neg"), 1)
            v.memset(mark[:, 0:1], 0.0).then_inc(sem("out_used"), 1)
            v.wait_ge(sem("out_used"), 1)
            with v.Fori(0, NB) as i:
                m = [0]

                def step(ins):
                    ins.then_inc(chain, 1)
                    m[0] += 1
                    v.wait_ge(chain, i * STEPS1 + m[0])

                for x in range(3):
                    step(v.tensor_copy(raw[:, x, :, 0:CONV - 1], halo[:, x]))
                    v.wait_ge(sem("raw_ready"), 3 * i + x + 1)
                    if x >= 1:
                        v.wait_ge(sem("conv_used"), 3 * i + x)
                    for q in range(CONV):
                        w = bc(cw[:, x, :, q:q + 1], [P, H, TB])
                        r = raw[:, x, :, q:q + TB]
                        if q == 0:
                            step(v.tensor_tensor(ca[:], r, w, ALU.mult))
                        else:
                            step(v.tensor_tensor(cbuf, r, w, ALU.mult))
                            step(v.tensor_tensor(ca[:], ca[:], cbuf, ALU.add))
                    v.tensor_copy(halo[:, x], raw[:, x, :, TB:TB + CONV - 1])
                    v.tensor_tensor(ca[:], ca[:], bc(cb[:, x].unsqueeze(2), [P, H, TB]),
                                    ALU.add).then_inc(sem("conv_ready"), 1)
                    v.wait_ge(sem("conv_ready"), 3 * i + x + 1)
                v.wait_ge(sem("conv_used"), 3 * i + 3)
                v.memset(mark[:, 1:2], 0.0).then_inc(sem("halo_ready"), 1)
                v.wait_ge(sem("a_done"), i + 1)
                for b in range(2):
                    last = v.tensor_tensor(ia[:, 8 * b:8 * b + 8], heads(PS[6 + b][:]),
                                           bc(ba[:, 8 * b:8 * b + 8].unsqueeze(2), [P, 8, TB]), ALU.add)
                step(last)
                v.tensor_scalar(ia[:], ia[:], LOGIT_FLOOR, None, ALU.max).then_inc(sem("a_logits"), 1)
                v.wait_ge(sem("exps1"), i + 1)
                v.tensor_scalar(bt[:], bt[:], 1.0, None, ALU.add)
                v.tensor_scalar(gg[:], gg[:], 1.0, None, ALU.add)
                step(v.tensor_scalar(ia[:], ia[:], 1.0, None, ALU.add))
                step(v.reciprocal(bt[:], bt[:]))
                v.tensor_tensor(be, bc(bt[:].unsqueeze(1), [H, H, TB]),
                                bc(ident[0:H, 0:H].unsqueeze(2), [H, H, TB]), ALU.mult).then_inc(sem("beta_rows"), 1)
                v.reciprocal(gg[:], gg[:])
                step(v.reciprocal(aa[:], ia[:]))
                a8 = aa[:].rearrange("p h (b t) -> p (h b) t", t=BK)
                M = BK // 2 - 1
                v.tensor_copy(Ef[:, :, M + 1], a8[:, :, M + 1])
                step(v.tensor_copy(Ei[:, :, M - 1], a8[:, :, M]))
                v.tensor_tensor(Ei[:, :, 1], Ei[:, :, 2], a8[:, :, 2], ALU.mult)
                step(v.tensor_tensor(Ef[:, :, 5], Ef[:, :, 4], a8[:, :, 5], ALU.mult))
                v.tensor_tensor(Ei[:, :, 0], Ei[:, :, 1], a8[:, :, 1], ALU.mult)
                step(v.tensor_tensor(Ef[:, :, 6], Ef[:, :, 5], a8[:, :, 6], ALU.mult))
                er = eref[:].rearrange("p h b -> p (h b)")
                v.tensor_tensor(er, Ei[:, :, 0], a8[:, :, 0], ALU.mult)
                step(v.tensor_tensor(Ef[:, :, 7], Ef[:, :, 6], a8[:, :, 7], ALU.mult))
                v.tensor_tensor(rho[:].rearrange("p h b -> p (h b)"), er, Ef[:, :, 7], ALU.mult)
                v.reciprocal(Ef[:, :, 0:M], Ei[:, :, 0:M])
                step(v.reciprocal(Ei[:, :, M + 1:BK], Ef[:, :, M + 1:BK]))
                step(v.tensor_tensor(vv[:], vv[:], Ei[:].rearrange("p (h b) t -> p h (b t)", h=H), ALU.mult))
                step(v.tensor_tensor(vv[:], vv[:], aa[:], ALU.mult))
                step(v.tensor_scalar(kq[:, :, :, 0], kq[:, :, :, 0], SCALE, None, ALU.mult))
                v.wait_ge(sem("beta_done"), i + 1)
                for b in range(2):
                    for c in range(NCH):
                        last = v.tensor_tensor(kb[:, c, 8 * b:8 * b + 8], kq[:, 8 * b:8 * b + 8, c * CH:(c + 1) * CH, 0],
                                               heads(PS[4 + b][:])[:, :, c * CH:(c + 1) * CH], ALU.mult)
                last.then_inc(sem("kb_ready"), 1)

                for c in range(NCH):
                    g0 = i * NCH + c
                    v.memset(hist[:], 0.0)
                    v.tensor_copy(dcy[:, :, 1:2], rho[:, :, c * NBLK:c * NBLK + 1])
                    step(v.tensor_copy(edc[:, :, 0:1], eref[:, :, c * NBLK:c * NBLK + 1]))
                    for b in range(1, NBLK):
                        v.tensor_tensor(edc[:, :, b:b + 1], dcy[:, :, b:b + 1],
                                        eref[:, :, c * NBLK + b:c * NBLK + b + 1], ALU.mult)
                        step(v.tensor_tensor(dcy[:, :, b + 1:b + 2], dcy[:, :, b:b + 1],
                                             rho[:, :, c * NBLK + b:c * NBLK + b + 1], ALU.mult))
                    v.wait_ge(sem("gram1_done"), g0 + 1)
                    for gi in range(NG):
                        last = v.tensor_tensor(
                            gs[:, gi], PS[4 + gi // 2][:, (gi % 2) * 256:(gi % 2) * 256 + 256].rearrange("p (h t) -> p h t", h=HG),
                            bc(maskh[:], [P, HG, 2 * CH]), ALU.mult)
                    last.then_inc(sem("gs_ready"), 1)
                    v.wait_ge(sem("gs_ready"), g0 + 1)
                    for b in range(NBLK):
                        q0 = 2 * BK * b
                        blk = y0[:, :, q0:q0 + 2 * BK]
                        if b == 0:
                            v.wait_ge(sem("y0_ready"), g0 + 1)
                        step(v.tensor_tensor(blk, y0[:, :, q0:q0 + 2 * BK],
                                             bc(edc[:, :, b:b + 1], [P, H, 2 * BK]), ALU.mult))
                        if b:
                            v.wait_ge(sem("seen_done"), g0 * (NBLK - 1) + b)
                            step(v.tensor_tensor(tmp[:], PS[3][:, 0:256].rearrange("p (h t) -> p h t", h=H),
                                                 bc(eref[:, :, c * NBLK + b:c * NBLK + b + 1], [P, H, 2 * BK]), ALU.mult))
                            step(v.tensor_tensor(blk, blk, tmp[:], ALU.subtract))
                        kpart = blk.rearrange("p h (t j) -> p h t j", j=2)[:, :, :, 0]
                        t0 = c * CH + b * BK
                        step(v.tensor_tensor(kpart, kpart, vv[:, :, t0:t0 + BK], ALU.subtract))
                        v.wait_ge(sem("gb_ready"), g0 * NBLK + b + 1)
                        for t in range(BK):
                            w = 15 - 2 * t
                            step(v.tensor_tensor(z[:, :, t:t + 1], ia[:, :, t0 + t:t0 + t + 1],
                                                 blk[:, :, 2 * t:2 * t + 1], ALU.mult))
                            step(v.tensor_tensor(tmp[:, :, 0:w], gb[:, b % 2, :, offs[t]:offs[t] + w],
                                                 bc(z[:, :, t:t + 1], [P, H, w]), ALU.mult))
                            ins = v.tensor_tensor(blk[:, :, 2 * t + 1:], blk[:, :, 2 * t + 1:], tmp[:, :, 0:w], ALU.subtract)
                            if t < BK - 1:
                                step(ins)
                            else:
                                ins.then_inc(sem("gb_used"), 1)
                                v.wait_ge(sem("gb_used"), g0 * NBLK + b + 1)
                        e7 = Ef[:].rearrange("p (h b) t -> p h b t", h=H)[:, :, c * NBLK + b, BK - 1:BK]
                        if b:
                            v.tensor_tensor(hist[:, :, 0:BK * b], hist[:, :, 0:BK * b],
                                            bc(rho[:, :, c * NBLK + b:c * NBLK + b + 1], [P, H, BK * b]), ALU.mult)
                        v.tensor_tensor(hist[:, :, BK * b:BK * b + BK], z[:], bc(e7, [P, H, BK]),
                                        ALU.mult).then_inc(sem("hist_ready"), 1)
                        v.wait_ge(sem("hist_ready"), g0 * NBLK + b + 1)
                    step(v.tensor_tensor(o[:, :, c * CH:(c + 1) * CH],
                                         y0[:].rearrange("p h (t j) -> p h t j", j=2)[:, :, :, 1],
                                         Ef[:].rearrange("p (h b) t -> p h (b t)", h=H)[:, :, c * CH:(c + 1) * CH], ALU.mult))
                    step(v.tensor_tensor(S[:], S[:], bc(dcy[:, :, NBLK:NBLK + 1], [P, H, D]), ALU.mult))
                    v.wait_ge(sem("write_done"), g0 + 1)
                    for q in range(HG):
                        sv = S[:].rearrange("p (g q) d -> p g q d", q=HG)[:, :, q, :]
                        last = v.tensor_tensor(sv, sv, PS[4 + q][:].rearrange("p (g d) -> p g d", g=NG), ALU.subtract)
                    last.then_inc(sem("S_ready"), 1)
                v.wait_ge(sem("mean_done"), i + 1)
                for b in range(2):
                    last = v.tensor_tensor(o[:, 8 * b:8 * b + 8], o[:, 8 * b:8 * b + 8], heads(PS[b][:]), ALU.subtract)
                last.then_inc(sem("centred"), 1)
                v.wait_ge(sem("std1_ready"), i + 1)
                step(v.reciprocal(osq, osq))
                step(v.tensor_tensor(o[:], o[:], osq, ALU.mult))
                step(v.tensor_scalar(o[:], o[:], lnw[:, 0:1], lnb[:, 0:1], ALU.mult, ALU.add))
                v.tensor_tensor(on[:], o[:], gg[:], ALU.mult).then_inc(sem("gated"), 1)
                v.wait_ge(sem("xr_loaded"), i * 16 + 16)
                v.wait_ge(sem("attn_done"), i + 1)
                v.tensor_tensor(xr[:], xr[:], PS[2][0:TB, 0:DM], ALU.add).then_inc(sem("xo_ready"), 1)
                v.wait_ge(sem("xo_ready"), i + 1)
                v.memset(mark[:, 2:3], 0.0).then_inc(sem("out_used"), 1)
                assert m[0] == STEPS1, m[0]

        @block.scalar
        def _(a):
            with a.Fori(0, NB) as i:
                for x in range(3):
                    a.wait_ge(sem("proj1_done"), 3 * i + x + 1)
                    if x == 0:
                        a.wait_ge(sem("halo_ready"), i + 1)
                    for b in range(2):
                        last = a.copy(raw[:, x, 8 * b:8 * b + 8, CONV - 1:], heads(PS[2 * x + b][:]))
                    last.then_inc(sem("raw_ready"), 1)
                for x in range(3):
                    a.wait_ge(sem("conv_ready"), 3 * i + x + 1)
                    dst = (kq[:, :, :, 1], kq[:, :, :, 0], vv[:])[x]
                    a.activation(dst, ca[:], ACT.Silu).then_inc(sem("conv_used"), 1)
                a.wait_ge(sem("g_done"), i + 1)
                for b in range(2):
                    a.activation(gg[:, 8 * b:8 * b + 8], heads(PS[b][:]), ACT.Exp, scale=-1.0)
                a.wait_ge(sem("bb_neg"), 1)
                a.activation(bt[:], PS[2][0:H, 0:TB], ACT.Exp, scale=-1.0, bias=nbb[:, 0:1])
                a.wait_ge(sem("a_logits"), i + 1)
                a.activation(ia[:], ia[:], ACT.Exp, scale=-1.0).then_inc(sem("exps1"), 1)
                for c in range(NCH):
                    g0 = i * NCH + c
                    a.wait_ge(sem("y0_done"), g0 + 1)
                    for b in range(2):
                        last = a.copy(y0[:, 8 * b:8 * b + 8], heads(PS[b][:]))
                    last.then_inc(sem("y0_ready"), 1)
                    a.wait_ge(sem("kr_done"), g0 + 1)
                    a.copy(kr[:].rearrange("p g d -> p (g d)"), PS[2][:]).then_inc(sem("kr_ready"), 1)
                    for b in range(NBLK):
                        a.wait_ge(sem("gbc_done"), g0 * NBLK + b + 1)
                        if b >= 2 or c:
                            a.wait_ge(sem("gb_used"), g0 * NBLK + b - 1)
                        for hh in range(2):
                            last = a.copy(gb[:, b % 2, 8 * hh:8 * hh + 8], heads(PS[6 + hh][:]))
                        last.then_inc(sem("gb_ready"), 1)
                        a.wait_ge(sem("histT_done"), g0 * NBLK + b + 1)
                        a.copy(hT[:].rearrange("p g d -> p (g d)"), PS[2][:]).then_inc(sem("hT_ready"), 1)
                    a.wait_ge(sem("sT_done"), g0 + 1)
                    for q in range(4):
                        last = a.copy(sT[:, 4 * q:4 * q + 4].rearrange("p h d -> p (h d)"), PS[4 + q][:])
                    last.then_inc(sem("sT_ready"), 1)
                a.wait_ge(sem("centred"), i + 1)
                a.activation(osq, o[:], ACT.Square).then_inc(sem("squared"), 1)
                a.wait_ge(sem("var_done"), i + 1)
                for b in range(2):
                    last = a.activation(osq[:, 8 * b:8 * b + 8], heads(PS[b][:]), ACT.Sqrt, bias=eps_t[:, 0:1])
                last.then_inc(sem("std1_ready"), 1)

        @block.tensor
        def _(pe):
            pe.wait_ge(loaded, 16 * len(LOADS))
            with pe.Fori(0, NB) as i:
                pe.wait_ge(sem("out_used"), i + 1)

                def project(w, b0):
                    for h in range(H):
                        for k in range(KC):
                            last = pe.matmul(PS[b0 + h // 8][:, (h % 8) * TB:(h % 8 + 1) * TB],
                                             w[:, k, h * D:(h + 1) * D], xnT[:, k, bass.ds(i * TB, TB)],
                                             start=(k == 0), stop=(k == KC - 1))
                    return last
                for x in range(3):
                    project(wp[x], 2 * x).then_inc(sem("proj1_done"), 1)
                project(wp[3], 6).then_inc(sem("a_done"), 1)
                pe.wait_ge(sem("raw_ready"), 3 * i + 2)
                project(wp[4], 0)
                for k in range(KC):
                    last = pe.matmul(PS[2][0:H, 0:TB], wb[:, k, :], xnT[:, k, bass.ds(i * TB, TB)],
                                     start=(k == 0), stop=(k == KC - 1))
                last.then_inc(sem("g_done"), 1)
                pe.wait_ge(sem("beta_rows"), i + 1)
                pe.wait_ge(sem("raw_ready"), 3 * i + 3)
                for b in range(2):
                    last = pe.matmul(PS[4 + b][:], ones[0:H, :], be[:, 8 * b:8 * b + 8, :], start=True, stop=True)
                last.then_inc(sem("beta_done"), 1)
                pe.wait_ge(sem("kb_ready"), i + 1)
                kqf = kq[:].rearrange("p h t j -> p h (t j)")
                for c in range(NCH):
                    g0 = i * NCH + c
                    if c:
                        pe.wait_ge(sem("sT_ready"), g0)
                    for g in range(NG):
                        last = pe.matmul(PS[4 + g // 2][:, (g % 2) * 256:(g % 2) * 256 + 256],
                                         kb[:, c, HG * g:HG * g + HG, :],
                                         kqf[:, HG * g:HG * g + HG, 2 * c * CH:2 * (c + 1) * CH], start=True, stop=True)
                    last.then_inc(sem("gram1_done"), 1)
                    for h in range(H):
                        last = pe.matmul(PS[h // 8][:, (h % 8) * 64:(h % 8 + 1) * 64], sT[:, h, :],
                                         kqf[:, h, 2 * c * CH:2 * (c + 1) * CH], start=True, stop=True)
                    last.then_inc(sem("y0_done"), 1)
                    for g in range(NG):
                        last = pe.transpose(PS[2][:, g * P:(g + 1) * P], kb[:, c, HG * g:HG * g + HG, :],
                                            ident[:])
                    last.then_inc(sem("kr_done"), 1)
                    pe.wait_ge(sem("pairs_ready"), g0 + 1)
                    for b in range(NBLK):
                        if b:
                            pe.wait_ge(sem("gb_ready"), g0 * NBLK + b)
                        for hh in range(2):
                            last = pe.matmul(PS[6 + hh][:], ones[:], pr[:, 8 * hh:8 * hh + 8, b, :], start=True, stop=True)
                        last.then_inc(sem("gbc_done"), 1)
                        if b == 0:
                            pe.wait_ge(sem("kr_ready"), g0 + 1)
                        pe.wait_ge(sem("hist_ready"), g0 * NBLK + b + 1)
                        for g in range(NG):
                            last = pe.transpose(PS[2][:, g * P:(g + 1) * P], hist[:, HG * g:HG * g + HG, :], ident[:])
                        last.then_inc(sem("histT_done"), 1)
                        pe.wait_ge(sem("hT_ready"), g0 * NBLK + b + 1)
                        if b < NBLK - 1:
                            for g in range(NG):
                                last = pe.matmul(PS[3][:, g * 64:(g + 1) * 64], hT[:, g, :],
                                                 gs[:, g, :, 2 * BK * (b + 1):2 * BK * (b + 2)], start=True, stop=True)
                            last.then_inc(sem("seen_done"), 1)
                    pe.wait_ge(sem("gb_ready"), g0 * NBLK + NBLK)
                    for q in range(HG):
                        for g in range(NG):
                            last = pe.matmul(PS[4 + q][:, g * D:(g + 1) * D], hT[CH * q:CH * q + CH, g, :],
                                             kr[CH * q:CH * q + CH, g, :], start=True, stop=True)
                    last.then_inc(sem("write_done"), 1)
                    pe.wait_ge(sem("S_ready"), g0 + 1)
                    for h in range(H):
                        last = pe.transpose(PS[4 + h // 4][:, (h % 4) * P:(h % 4 + 1) * P], S[:, h, :], ident[:])
                    last.then_inc(sem("sT_done"), 1)
                pe.wait_ge(sem("sT_ready"), i * NCH + NCH)
                for b in range(2):
                    last = pe.matmul(PS[b][:], mean_w[:], o[:, 8 * b:8 * b + 8, :], start=True, stop=True)
                last.then_inc(sem("mean_done"), 1)
                pe.wait_ge(sem("squared"), i + 1)
                for b in range(2):
                    last = pe.matmul(PS[b][:], mean_w[:], osq[:, 8 * b:8 * b + 8, :], start=True, stop=True)
                last.then_inc(sem("var_done"), 1)
                pe.wait_ge(sem("gated"), i + 1)
                for h in range(H):
                    last = pe.matmul(PS[2][0:TB, 0:DM], on[:, h, :], wo[:, h, :], start=(h == 0), stop=(h == H - 1))
                last.then_inc(sem("attn_done"), 1)


STEPS1 = 263


def kernel(**inputs):
    import numpy as np
    import concourse.bacc as bacc
    from concourse.bass_utils import run_bass_kernel_spmd as run

    nc = bacc.Bacc("TRN2", target_bir_lowering=False, num_devices=1)
    i = {k: np.asarray(v) for k, v in inputs.items()}
    c = np.ascontiguousarray
    arrays = {
        "L0_attn_u": c(i["L0_attn_u"].reshape(T, DM)),
        "in_projT": c(i["L0_attn_in_proj_w"].T),
        "out_projT": c(i["L0_attn_out_proj_w"].T),
        "gate0T": c(np.concatenate([i["L0_ffn_gate_w"].T, i["L0_ffn_shared_gate_w"]], axis=1)),
        "gate1T": c(i["L1_ffn_gate_w"].T),
        "w1T": c(i["L1_ffn_w1"].transpose(0, 2, 1)),
        "w3T": c(i["L1_ffn_w3"].transpose(0, 2, 1)),
        "w2T": c(i["L1_ffn_w2"].transpose(0, 2, 1)),
        "WbT": c(i["L1_attn_Wb"].T),
        "WoT": c(i["L1_attn_Wo"].T),
        "baT": c(i["L1_attn_ba"].reshape(H, D).T),
        "bbT": c(i["L1_attn_bb"].reshape(H, 1)),
        "ln_wT": c(i["L1_attn_ln_w"].reshape(D, 1)),
        "ln_bT": c(i["L1_attn_ln_b"].reshape(D, 1)),
    }
    for x in "qkvag":
        arrays[f"W{x}T"] = c(i[f"L1_attn_W{x}"].T)
    for x in "qkv":
        arrays[f"{x}conv_wT"] = c(i[f"L1_attn_{x}conv_w"].reshape(H, D, CONV).transpose(1, 0, 2))
        arrays[f"{x}conv_bT"] = c(i[f"L1_attn_{x}conv_b"].reshape(H, D).T)
    for name in ("L0_attn_D", "L0_attn_dt_bias", "L0_attn_A_log", "L0_attn_bnorm_w", "L0_attn_cnorm_w",
                 "L0_attn_ln_w", "L0_attn_ln_b", "L0_ffn_w_gate", "L0_ffn_w_up", "L0_ffn_w_down",
                 "L0_ffn_sw_gate", "L0_ffn_sw_up", "L0_ffn_sw_down"):
        arrays[name] = c(i[name])
    A = {n: nc.dram_tensor(f"in_{n}", a.shape, mybir.dt.from_np(a.dtype), kind="ExternalInput").ap()
         for n, a in arrays.items()}
    out = nc.dram_tensor("out", (T, DM), F32, kind="ExternalOutput").ap()
    program(nc, A, out)
    r = run(nc, [{f"in_{n}": a for n, a in arrays.items()}], core_ids=[0])
    return r.results[0]["out"].reshape(1, T, DM)
```

```python
from contextlib import ExitStack

import concourse.bass as bass
from concourse import mybir

F32 = mybir.dt.float32
U32 = mybir.dt.uint32
ALU = mybir.AluOpType
ACT = mybir.ActivationFunctionType
AX = mybir.AxisListType

P = 128
EPS = 1e-5

T = 1024
DM = 256
KC = DM // P
NT = T // P

DI = 512
NH0 = 8
HP0 = DI // NH0
DS = 128
DPROJ = 2 * DI + 2 * DS + NH0
NBD = 2 * DS + NH0

E = 8
I0 = 176
I0B = I0 - P
IS = 704
ISC = 5
ISR = IS - ISC * P

H = 16
D = 128
CONV = 4
TB = 64
NB = T // TB
CH = 32
BK = 8
NCH = TB // CH
NBLK = CH // BK
HH = H // 2
HG = 4
NG = H // HG
SCALE = float(D) ** -0.5
LOGIT_FLOOR = -20.0

I1 = 512
IC1 = I1 // P


def program(nc, A, out):
    ctx = ExitStack()
    with ctx:
        sems = {}

        def sem(name):
            if name not in sems:
                sems[name] = ctx.enter_context(nc.semaphore(name))
            return sems[name]

        def sb(stack, name, shape, dt=F32):
            return stack.enter_context(nc.sbuf_tensor(name, shape, dt))

        xnT = sb(ctx, "xnT", [P, KC, T + TB])
        ident = sb(ctx, "ident", [P, P])
        ones = sb(ctx, "ones", [P, P])
        eps_t = sb(ctx, "eps_t", [P, 1])
        x1_dram = nc.dram_tensor("x1_scratch", (T, DM), F32, kind="Internal").ap()

        PS = [ctx.enter_context(nc.psum_tensor(f"bank{i}", [P, 512], F32)) for i in range(8)]

        with ExitStack() as rows_stack:
            mean_w = sb(rows_stack, "mean_w", [P, P])
            x_rows = sb(rows_stack, "x_rows", [P, NT, DM])
            w_tok = sb(rows_stack, "w_tok", [P, NT, E])
            layer0(nc, A, sem, sb, PS, x_rows, xnT, w_tok, ident, ones, mean_w, eps_t)
            experts1(nc, A, sem, sb, PS, x_rows, xnT, w_tok, x1_dram)
        delta1(nc, A, sem, sb, PS, xnT, ident, ones, eps_t, x1_dram, out)


def bc(ap, shape):
    return ap.broadcast_to(shape)


def layer0(nc, A, sem, sb, PS, x_rows, xnT, w_tok, ident, ones, mean_w, eps_t):
    with ExitStack() as st:
        def s(name, shape, dt=F32):
            return sb(st, "l0_" + name, shape, dt)

        win = s("win", [P, KC, DPROJ])
        wout = s("wout", [P, DI // P, DM])
        wg = s("wg", [P, E, KC, I0])
        wu = s("wu", [P, E, KC, I0])
        wda = s("wda", [P, E, DM])
        wdb = s("wdb", [I0B, E, DM])
        sg = s("sg", [P, KC, IS])
        su = s("su", [P, KC, IS])
        sda = s("sda", [P, ISC, DM])
        sdb = s("sdb", [ISR, DM])
        gate = s("gate", [P, KC, E + 1])
        gate1 = s("gate1", [P, KC, E])
        rows = s("rows", [P, 2 * DM + 2 * DS])
        hrows = s("hrows", [P, 3, NH0])
        triu = s("triu", [P, P])
        iota = s("iota", [P, E])
        neg_a = s("neg_a", [P, NH0])
        st6 = s("st6", [P, 6]); mv = s("mv", [P, 2]); std = s("std", [P, 1]); rstd = s("rstd", [P, 1])
        xn = s("xn", [P, DM]); un = s("un", [P, DM])
        xuT = s("xuT", [P, 2 * KC, P])
        zs = s("zs", [P, DI]); xs = s("xs", [P, DI])
        sq = s("sq", [P, 2, P]); ssq = s("ssq", [P, 2]); rms = s("rms", [P, 2]); rrms = s("rrms", [P, 2])
        bcn = s("bcn", [P, 2, DS]); bcT = s("bcT", [P, 2, P])
        dtv = s("dtv", [P, NH0]); dta = s("dta", [P, NH0]); dte = s("dte", [P, NH0]); dtl = s("dtl", [P, NH0])
        dA = s("dA", [P, NH0]); dAx = s("dAx", [P, NH0, P])
        cum = s("cum", [P, NH0]); tot = s("tot", [P, NH0]); dend = s("dend", [P, NH0])
        dec_end = s("dec_end", [P, NH0]); dec_in = s("dec_in", [P, NH0]); rho = s("rho", [P, NH0])
        Ld = s("Ld", [P, NH0, P]); Le = s("Le", [P, NH0, P]); Gm = s("Gm", [P, P])
        S0 = s("S0", [P, DI]); xdec = s("xdec", [P, DI])
        y = s("y", [P, DI]); yt = s("yt", [P, DI]); yT = s("yT", [P, DI // P, P])
        lg = s("lg", [P, E + 1]); m8 = s("m8", [P, 8]); i8 = s("i8", [P, 8], U32); i8f = s("i8f", [P, 8])
        nmax = s("nmax", [P, 1]); ex = s("ex", [P, E]); eq0 = s("eq0", [P, E]); eq1 = s("eq1", [P, E])
        msum = s("msum", [P, 1]); mrec = s("mrec", [P, 1]); cw = s("cw", [P, E + 1]); tg = s("tg", [P, 1])
        NGRP = 6
        hs = s("hs", [P, 2, 4, P])
        hA = s("hA", [P, E, P])
        hB = s("hB", [I0B, E, P])
        hS = s("hS", [P, ISC + 1, P])
        acc = s("acc", [P, DM]); wtmp = s("wtmp", [P, DM])
        m8b = s("m8b", [P, 8]); i8b = s("i8b", [P, 8], U32)
        fac = s("fac", [P, E]); dif = s("dif", [P, E]); keep = s("keep", [P, E])
        e12 = s("e12", [P, 2, E]); ek = s("ek", [P, 2, E]); den = s("den", [P, 2]); rden = s("rden", [P, 2])
        taken = s("taken", [P, 1])
        zero8 = s("zero8", [P, E]); ones8 = s("ones8", [P, E])
        x2n = s("x2n", [P, DM])

        groups = [[("e", e, 0, P) for e in range(4)], [("e", e, 0, P) for e in range(4, 8)],
                  [("e", e, P, I0B) for e in range(4)], [("e", e, P, I0B) for e in range(4, 8)],
                  [("s", c, c * P, P) for c in range(4)],
                  [("s", 4, 4 * P, P), ("s", 5, 5 * P, ISR)]]

        LOADS = [
            (x_rows[:], A["L0_attn_u"].rearrange("(n p) d -> p n d", p=P)),
            (win[:], A["in_projT"].rearrange("(k p) e -> p k e", p=P)),
            (rows[:, 0:DM], A["L0_attn_ln_w"].partition_broadcast(P)),
            (rows[:, DM:2 * DM], A["L0_attn_ln_b"].partition_broadcast(P)),
            (rows[:, 2 * DM:2 * DM + DS], A["L0_attn_bnorm_w"].partition_broadcast(P)),
            (rows[:, 2 * DM + DS:], A["L0_attn_cnorm_w"].partition_broadcast(P)),
            (hrows[:, 0], A["L0_attn_D"].partition_broadcast(P)),
            (hrows[:, 1], A["L0_attn_dt_bias"].partition_broadcast(P)),
            (hrows[:, 2], A["L0_attn_A_log"].partition_broadcast(P)),
            (wout[:], A["out_projT"].rearrange("(k p) e -> p k e", p=P)),
            (gate[:], A["gate0T"].rearrange("(k p) e -> p k e", p=P)),
            (gate1[:], A["gate1T"].rearrange("(k p) e -> p k e", p=P)),
            (wg[:, 0:4], A["L0_ffn_w_gate"][0:4].rearrange("e (k p) i -> p e k i", p=P)),
            (wg[:, 4:8], A["L0_ffn_w_gate"][4:8].rearrange("e (k p) i -> p e k i", p=P)),
            (wu[:, 0:4], A["L0_ffn_w_up"][0:4].rearrange("e (k p) i -> p e k i", p=P)),
            (wu[:, 4:8], A["L0_ffn_w_up"][4:8].rearrange("e (k p) i -> p e k i", p=P)),
            (sg[:], A["L0_ffn_sw_gate"].rearrange("(k p) i -> p k i", p=P)),
            (su[:], A["L0_ffn_sw_up"].rearrange("(k p) i -> p k i", p=P)),
            (wda[:], A["L0_ffn_w_down"][:, 0:P].rearrange("e p d -> p e d")),
            (wdb[:], A["L0_ffn_w_down"][:, P:I0].rearrange("e p d -> p e d")),
            (sda[:], A["L0_ffn_sw_down"][0:ISC * P].rearrange("(c p) d -> p c d", p=P)),
            (sdb[:], A["L0_ffn_sw_down"][ISC * P:IS]),
        ]
        loaded = sem("weights0_loaded")
        n_loads = len(LOADS)
        block = st.enter_context(nc.Block())

        @block.sync
        def _(sp):
            for dst, src in LOADS:
                sp.dma_start(dst, src).then_inc(loaded, 16)

        @block.gpsimd
        def _(g):
            const = sem("const_step")
            g.memset(ident[:], 0.0).then_inc(const, 1)
            g.memset(triu[:], 1.0).then_inc(const, 1)
            g.wait_ge(const, 2)
            g.affine_select(out=ident[:], in_=ident[:], compare_op=ALU.not_equal, fill=1.0,
                            base=0, pattern=[[-1, P]], channel_multiplier=1)
            g.affine_select(out=triu[:], in_=triu[:], compare_op=ALU.is_ge, fill=0.0,
                            base=0, pattern=[[1, P]], channel_multiplier=-1)
            g.iota(iota[:], pattern=[[1, E]], base=0, channel_multiplier=0,
                   allow_small_or_imprecise_dtypes=True).then_inc(sem("consts_ready"), 1)

        @block.vector
        def _(v):
            chain, count = sem("vec0_step"), [0]

            def link(ins, n=None):
                ins.then_inc(chain, 1)
                count[0] += 1
                v.wait_ge(chain, count[0] if n is None else n * PER + count[0])
            v.memset(ones[:], 1.0)
            v.memset(mean_w[:], 1.0 / P)
            v.memset(zero8[:], 0.0)
            v.memset(ones8[:], 1.0)
            v.memset(S0[:], 0.0)
            v.memset(eps_t[:], EPS).then_inc(sem("vconst_ready"), 1)
            v.wait_ge(sem("vconst_ready"), 1)
            v.wait_ge(loaded, 16 * n_loads)
            v.wait_ge(sem("consts_ready"), 1)
            v.wait_ge(sem("nega_exp"), 1)
            v.tensor_scalar(neg_a[:], neg_a[:], -1.0, None, ALU.mult).then_inc(sem("tile0_done"), 1)
            v.wait_ge(sem("tile0_done"), 1)

            with v.Fori(0, NT) as n:
                m = [0]

                def step(ins):
                    ins.then_inc(chain, 1)
                    m[0] += 1
                    v.wait_ge(chain, n * STEPS0 + m[0])

                def take_wait():
                    v.memset(taken[:], 0.0)

                def normed(dst, src, k):
                    take_wait()
                    step(v.bn_stats(st6[:], src))
                    take_wait()
                    v.bn_aggr(mv[:], st6[:]).then_inc(sem("moments"), 1)
                    v.wait_ge(sem("std_ready"), 3 * n + k)
                    step(v.reciprocal(rstd[:], std[:]))
                    return v.tensor_scalar(dst, src, mv[:, 0:1], rstd[:, 0:1], ALU.subtract, ALU.mult)

                step(normed(xn[:], x_rows[:, n, :], 1))
                step(normed(un[:], xn[:], 2))
                step(v.tensor_tensor(un[:], un[:], rows[:, 0:DM], ALU.mult))
                v.tensor_tensor(un[:], un[:], rows[:, DM:2 * DM], ALU.add).then_inc(sem("xn_un"), 1)
                v.tensor_tensor(acc[:], x_rows[:, n, :], xn[:], ALU.add)
                v.wait_ge(sem("proj_done"), n + 1)
                v.tensor_copy(xs[:], PS[2][:])
                step(v.tensor_tensor(dtv[:], PS[3][:, 2 * DS:NBD], hrows[:, 1], ALU.add))
                v.scalar_tensor_tensor(out=dta[:], in0=dtv[:], scalar=-1.0, in1=dtv[:],
                                       op0=ALU.mult, op1=ALU.max).then_inc(sem("dt_abs"), 1)
                v.wait_ge(sem("ssq_rms"), n + 1)
                step(v.reciprocal(rrms[:], rms[:]))
                for j in range(2):
                    last = v.scalar_tensor_tensor(
                        out=bcn[:, j], in0=PS[3][:, j * DS:(j + 1) * DS], scalar=rrms[:, j:j + 1],
                        in1=rows[:, 2 * DM + j * DS:2 * DM + (j + 1) * DS], op0=ALU.mult, op1=ALU.mult)
                last.then_inc(sem("bc_normed"), 1)
                v.wait_ge(sem("dt_ln"), n + 1)
                step(v.scalar_tensor_tensor(out=dtv[:], in0=dtv[:], scalar=0.0, in1=dtl[:],
                                            op0=ALU.max, op1=ALU.add))
                step(v.tensor_tensor(dA[:], dtv[:], neg_a[:], ALU.mult))
                v.tensor_tensor(dAx[:], bc(triu[:].unsqueeze(1), [P, NH0, P]),
                                bc(dA[:].unsqueeze(2), [P, NH0, P]), ALU.mult).then_inc(sem("dA_ready"), 1)
                v.wait_ge(sem("cum_done"), n + 1)
                v.tensor_copy(tot[:], PS[6][:, NH0:2 * NH0])
                step(v.tensor_copy(cum[:], PS[6][:, 0:NH0]))
                step(v.tensor_tensor(dend[:], tot[:], cum[:], ALU.subtract))
                for h in range(NH0):
                    last = v.tensor_scalar(Ld[:, h, :], PS[4 + h // 4][:, (h % 4) * P:(h % 4 + 1) * P],
                                           cum[:, h:h + 1], 0.0, ALU.subtract, ALU.min)
                last.then_inc(sem("logs_ready"), 1)
                v.wait_ge(sem("gram_done"), n + 1)
                step(v.tensor_tensor(Gm[:], PS[7][:, 0:P], triu[:], ALU.mult))
                v.wait_ge(sem("exps_ready"), n + 1)
                v.tensor_tensor(xdec[:].rearrange("p (h q) -> p h q", h=NH0),
                                xs[:].rearrange("p (h q) -> p h q", h=NH0),
                                bc(dec_end[:].unsqueeze(2), [P, NH0, HP0]), ALU.mult)
                v.tensor_tensor(Le[:], Le[:], bc(Gm[:].unsqueeze(1), [P, NH0, P]),
                                ALU.mult).then_inc(sem("mix_ready"), 1)
                v.tensor_tensor(yt[:].rearrange("p (h q) -> p h q", h=NH0),
                                xs[:].rearrange("p (h q) -> p h q", h=NH0),
                                bc(hrows[:, 0].unsqueeze(2), [P, NH0, HP0]), ALU.mult)
                v.wait_ge(sem("y_done"), n + 1)
                step(v.tensor_tensor(y[:].rearrange("p (h q) -> p h q", h=NH0),
                                     PS[2][:].rearrange("p (h q) -> p h q", h=NH0),
                                     bc(dec_in[:].unsqueeze(2), [P, NH0, HP0]), ALU.mult))
                step(v.tensor_tensor(y[:], y[:], PS[1][:], ALU.add))
                step(v.tensor_tensor(y[:], y[:], yt[:], ALU.add))
                v.tensor_tensor(y[:], y[:], zs[:], ALU.mult).then_inc(sem("y_ready"), 1)
                step(v.tensor_tensor(S0[:].rearrange("p (h q) -> p h q", h=NH0),
                                     S0[:].rearrange("p (h q) -> p h q", h=NH0),
                                     bc(rho[:].unsqueeze(2), [P, NH0, HP0]), ALU.mult))
                step(v.tensor_tensor(S0[:], S0[:], PS[3][:], ALU.add))

                v.wait_ge(sem("logits_done"), n + 1)
                step(v.tensor_copy(lg[:], PS[6][:, 256:256 + E + 1]))
                take_wait()
                step(v.max(m8[:], lg[:, 0:E]))
                take_wait()
                step(v.max_index(i8[:], m8[:], lg[:, 0:E]))
                v.tensor_copy(i8f[:], i8[:])
                v.tensor_scalar(nmax[:], m8[:, 0:1], -1.0, None, ALU.mult).then_inc(sem("nmax0"), 1)
                v.wait_ge(sem("nmax0"), n + 1)
                v.tensor_scalar(eq0[:], iota[:], i8f[:, 0:1], None, ALU.is_equal)
                step(v.tensor_scalar(eq1[:], iota[:], i8f[:, 1:2], None, ALU.is_equal))
                step(v.tensor_tensor(eq0[:], eq0[:], eq1[:], ALU.add))
                v.wait_ge(sem("router_exp"), n + 1)
                step(v.tensor_tensor(ex[:], ex[:], eq0[:], ALU.mult))
                step(v.reduce_sum(msum[:], ex[:], AX.X))
                step(v.reciprocal(mrec[:], msum[:]))
                v.tensor_scalar(cw[:, 0:E], ex[:], mrec[:, 0:1], None, ALU.mult)
                step(v.tensor_scalar(cw[:, E:E + 1], tg[:], 1.0, 0.5, ALU.add, ALU.mult))

                v.wait_ge(sem("mixer_done"), n + 1)
                step(v.tensor_tensor(acc[:], acc[:], PS[1][:, 0:DM], ALU.add))

                for gi, grp in enumerate(groups):
                    v.wait_ge(sem("up_done"), NGRP * n + gi + 1)
                    v.wait_ge(sem("silu_done"), NGRP * n + gi + 1)
                    ub = PS[5 if gi % 2 == 0 else 7]
                    kind, c0 = grp[0][0], grp[0][1]
                    if gi == 5:
                        v.tensor_tensor(hS[:, 4, :], hs[:, 1, 0, :], ub[:, 0:P], ALU.mult)
                        last = v.tensor_tensor(hS[0:ISR, 5, :], hs[0:ISR, 1, 1, :], ub[0:ISR, P:2 * P], ALU.mult)
                    else:
                        m_rows = grp[0][3]
                        dst = {"s": hS}.get(kind, hA if m_rows == P else hB)
                        last = v.tensor_tensor(
                            dst[0:m_rows, c0:c0 + 4, :], hs[0:m_rows, gi % 2],
                            ub[0:m_rows].rearrange("p (c t) -> p c t", c=4), ALU.mult)
                    last.then_inc(sem("h_ready"), 1)
                for e in range(E + 1):
                    v.wait_ge(sem("down_done"), (E + 1) * n + e + 1)
                    v.scalar_tensor_tensor(out=acc[:] if e < E else x_rows[:, n, :],
                                           in0=PS[1 + e % 2][:, 0:DM], scalar=cw[:, e:e + 1], in1=acc[:],
                                           op0=ALU.mult, op1=ALU.add).then_inc(sem("down_used"), 1)
                    v.wait_ge(sem("down_used"), (E + 1) * n + e + 1)
                normed(x2n[:], x_rows[:, n, :], 3).then_inc(sem("x2n"), 1)
                v.wait_ge(sem("logits1_done"), n + 1)
                lg1 = lg[:, 0:E]
                step(v.tensor_copy(lg1, PS[6][:, 0:E]))
                take_wait()
                step(v.max(m8b[:], lg1))
                take_wait()
                step(v.max_index(i8b[:], m8b[:], lg1))
                v.tensor_copy(i8f[:], i8b[:])
                v.tensor_scalar(ek[:, 0], lg1, m8b[:, 0:1], 0.0, ALU.subtract, ALU.min)
                v.tensor_scalar(ek[:, 1], lg1, m8b[:, 1:2], 0.0, ALU.subtract, ALU.min).then_inc(sem("nmax1"), 1)
                v.wait_ge(sem("nmax1"), n + 1)
                v.tensor_scalar(eq0[:], iota[:], i8f[:, 0:1], None, ALU.is_equal)
                step(v.tensor_scalar(eq1[:], iota[:], i8f[:, 1:2], None, ALU.is_equal))
                v.wait_ge(sem("router_exp1"), n + 1)
                for j in range(2):
                    step(v.scalar_tensor_tensor(out=fac[:], in0=lg1, scalar=-1.0, in1=lg1, op0=ALU.mult, op1=ALU.max))
                    step(v.tensor_scalar(fac[:], fac[:], m8b[:, j:j + 1], None, ALU.max))
                    step(v.tensor_scalar(dif[:], lg1, -1.0, m8b[:, j:j + 1], ALU.mult, ALU.add))
                    step(v.scalar_tensor_tensor(out=keep[:], in0=fac[:], scalar=0.02, in1=dif[:],
                                                op0=ALU.mult, op1=ALU.is_ge))
                    if j == 1:
                        step(v.tensor_tensor(fac[:], ones8[:], eq0[:], ALU.subtract))
                        step(v.tensor_tensor(keep[:], keep[:], fac[:], ALU.mult))
                    step(v.tensor_tensor(ek[:, j], e12[:, j], keep[:], ALU.mult))
                    step(v.reduce_sum(den[:, j:j + 1], ek[:, j], AX.X))
                step(v.reciprocal(rden[:], den[:]))
                step(v.tensor_scalar(eq0[:], eq0[:], rden[:, 0:1], None, ALU.mult))
                step(v.scalar_tensor_tensor(out=w_tok[:, n, :], in0=eq1[:], scalar=rden[:, 1:2], in1=eq0[:],
                                            op0=ALU.mult, op1=ALU.add))
                v.wait_ge(sem("x2nT_kept"), n + 1)
                v.tensor_copy(tg[:], tg[:]).then_inc(sem("tile0_done"), 1)
                assert m[0] == STEPS0, m[0]

        @block.scalar
        def _(a):
            a.wait_ge(loaded, 16 * n_loads)
            a.wait_ge(sem("vconst_ready"), 1)
            a.activation(neg_a[:], hrows[:, 2], ACT.Exp).then_inc(sem("nega_exp"), 1)
            with a.Fori(0, NT) as n:
                m = [0]

                def step(ins):
                    ins.then_inc(sem("act0_step"), 1)
                    m[0] += 1
                    a.wait_ge(sem("act0_step"), n * ASTEPS0 + m[0])

                def std_of(k):
                    a.wait_ge(sem("moments"), 3 * n + k)
                    a.activation(std[:], mv[:, 1:2], ACT.Sqrt, bias=eps_t[:, 0:1]).then_inc(sem("std_ready"), 1)

                std_of(1)
                std_of(2)
                a.wait_ge(sem("xn_T"), n + 1)
                a.copy(xuT[:].rearrange("p c t -> p (c t)"), PS[0][:]).then_inc(sem("xuT_ready"), 1)
                a.wait_ge(sem("dt_abs"), n + 1)
                for j in range(2):
                    last = a.activation(sq[:, j], PS[3][:, j * DS:(j + 1) * DS], ACT.Square,
                                        accum_out=ssq[:, j:j + 1])
                step(last)
                a.activation(rms[:], ssq[:], ACT.Sqrt, bias=eps_t[:, 0:1],
                             scale=1.0 / DS).then_inc(sem("ssq_rms"), 1)
                a.activation(zs[:], PS[1][:], ACT.Silu)
                step(a.activation(dte[:], dta[:], ACT.Exp, scale=-1.0))
                a.activation(dtl[:], dte[:], ACT.Ln, bias=1.0).then_inc(sem("dt_ln"), 1)
                a.wait_ge(sem("bcT_done"), n + 1)
                a.copy(bcT[:].rearrange("p c t -> p (c t)"), PS[0][:, 0:2 * P]).then_inc(sem("bcT_ready"), 1)
                a.wait_ge(sem("logs_ready"), n + 1)
                a.activation(dec_in[:], cum[:], ACT.Exp)
                a.activation(rho[:], tot[:], ACT.Exp)
                a.activation(dec_end[:], dend[:], ACT.Exp)
                a.activation(Le[:], Ld[:], ACT.Exp).then_inc(sem("exps_ready"), 1)
                a.wait_ge(sem("nmax0"), n + 1)
                a.activation(ex[:], lg[:, 0:E], ACT.Exp, bias=nmax[:, 0:1])
                a.activation(tg[:], lg[:, E:E + 1], ACT.Tanh, scale=0.5).then_inc(sem("router_exp"), 1)
                a.wait_ge(sem("yT_done"), n + 1)
                a.copy(yT[:].rearrange("p c t -> p (c t)"), PS[0][:]).then_inc(sem("yT_ready"), 1)
                for gi, grp in enumerate(groups):
                    a.wait_ge(sem("up_done"), NGRP * n + gi + 1)
                    if gi >= 2:
                        a.wait_ge(sem("h_ready"), NGRP * n + gi - 1)
                    gb = PS[4 if gi % 2 == 0 else 6]
                    if gi == 5:
                        a.activation(hs[:, 1, 0, :], gb[:, 0:P], ACT.Silu)
                        last = a.activation(hs[0:ISR, 1, 1, :], gb[0:ISR, P:2 * P], ACT.Silu)
                    else:
                        r = grp[0][3]
                        last = a.activation(hs[0:r, gi % 2].rearrange("p c t -> p (c t)"), gb[0:r, :], ACT.Silu)
                    last.then_inc(sem("silu_done"), 1)
                std_of(3)
                a.wait_ge(sem("x2nT_done"), n + 1)
                a.copy(xuT[:, 0:KC, :].rearrange("p c t -> p (c t)"), PS[0][:, 0:2 * P]).then_inc(sem("x2nT_ready"), 1)
                a.copy(xnT[:, :, bass.ts(n, P)], PS[0][:, 0:2 * P].rearrange("p (c t) -> p c t", c=KC)).then_inc(sem("x2nT_kept"), 1)
                a.wait_ge(sem("nmax1"), n + 1)
                last = a.activation(e12[:], ek[:], ACT.Exp)
                last.then_inc(sem("router_exp1"), 1)
                assert m[0] == ASTEPS0, m[0]

        @block.tensor
        def _(pe):
            pe.wait_ge(loaded, 16 * n_loads)
            pe.wait_ge(sem("consts_ready"), 1)
            with pe.Fori(0, NT) as n:
                pe.wait_ge(sem("tile0_done"), n + 1)
                pe.wait_ge(sem("xn_un"), n + 1)
                for j in range(2):
                    for k in range(KC):
                        last = pe.transpose(PS[0][:, (2 * j + k) * P:(2 * j + k + 1) * P],
                                            (xn, un)[j][:, k * P:(k + 1) * P], ident[:])
                last.then_inc(sem("xn_T"), 1)
                pe.wait_ge(sem("xuT_ready"), n + 1)
                for b, (c0, c1) in enumerate([(0, DI), (DI, 2 * DI), (2 * DI, DPROJ)]):
                    for k in range(KC):
                        last = pe.matmul(PS[1 + b][:, 0:c1 - c0], xuT[:, KC + k, :], win[:, k, c0:c1],
                                         start=(k == 0), stop=(k == KC - 1))
                last.then_inc(sem("proj_done"), 1)
                pe.wait_ge(sem("bc_normed"), n + 1)
                for j in range(2):
                    last = pe.transpose(PS[0][:, j * P:(j + 1) * P], bcn[:, j], ident[:])
                last.then_inc(sem("bcT_done"), 1)
                pe.wait_ge(sem("dA_ready"), n + 1)
                pe.matmul(PS[6][:, 0:NH0], triu[:], dA[:], start=True, stop=True)
                pe.matmul(PS[6][:, NH0:2 * NH0], ones[:], dA[:], start=True, stop=True)
                for b in range(2):
                    last = pe.matmul(PS[4 + b][:], ones[:], dAx[:, 4 * b:4 * b + 4, :], start=True, stop=True)
                last.then_inc(sem("cum_done"), 1)
                pe.wait_ge(sem("bcT_ready"), n + 1)
                pe.matmul(PS[7][:, 0:P], bcT[:, 0], bcT[:, 1], start=True, stop=True).then_inc(sem("gram_done"), 1)
                pe.wait_ge(sem("logs_ready"), n + 1)
                for k in range(KC):
                    last = pe.matmul(PS[6][:, 256:256 + E + 1], xuT[:, k, :], gate[:, k, :],
                                     start=(k == 0), stop=(k == KC - 1))
                last.then_inc(sem("logits_done"), 1)
                pe.wait_ge(sem("mix_ready"), n + 1)
                pe.matmul(PS[2][:], bcT[:, 1], S0[:], start=True, stop=True)
                for h in range(NH0):
                    pe.matmul(PS[1][:, h * HP0:(h + 1) * HP0], Le[:, h, :], xs[:, h * HP0:(h + 1) * HP0],
                              start=True, stop=True)
                pe.matmul(PS[3][:], bcn[:, 0], xdec[:], start=True, stop=True).then_inc(sem("y_done"), 1)
                pe.wait_ge(sem("y_ready"), n + 1)
                for c in range(DI // P):
                    last = pe.transpose(PS[0][:, c * P:(c + 1) * P], y[:, c * P:(c + 1) * P], ident[:])
                last.then_inc(sem("yT_done"), 1)
                pe.wait_ge(sem("yT_ready"), n + 1)
                for c in range(DI // P):
                    last = pe.matmul(PS[1][:, 0:DM], yT[:, c, :], wout[:, c, :], start=(c == 0), stop=(c == DI // P - 1))
                last.then_inc(sem("mixer_done"), 1)
                for gi, grp in enumerate(groups):
                    if gi == 1:
                        pe.wait_ge(sem("nmax0"), n + 1)
                    if gi >= 2:
                        pe.wait_ge(sem("h_ready"), NGRP * n + gi - 1)
                    gb, ub = (PS[4], PS[5]) if gi % 2 == 0 else (PS[6], PS[7])
                    for bank, we, ws in ((gb, wg, sg), (ub, wu, su)):
                        for c, (kind, e, i0, r) in enumerate(grp):
                            for k in range(KC):
                                w = we[:, e, k, i0:i0 + r] if kind == "e" else ws[:, k, i0:i0 + r]
                                last = pe.matmul(bank[0:r, c * P:(c + 1) * P], w, xuT[:, k, :],
                                                 start=(k == 0), stop=(k == KC - 1))
                    last.then_inc(sem("up_done"), 1)
                pe.wait_ge(sem("h_ready"), NGRP * n + NGRP)
                for e in range(E + 1):
                    o = PS[1 + e % 2][:, 0:DM]
                    if e >= 2:
                        pe.wait_ge(sem("down_used"), (E + 1) * n + e - 1)
                    if e < E:
                        pe.matmul(o, hA[:, e, :], wda[:, e, :], start=True, stop=False)
                        last = pe.matmul(o, hB[:, e, :], wdb[:, e, :], start=False, stop=True)
                    else:
                        for c in range(ISC):
                            pe.matmul(o, hS[:, c, :], sda[:, c, :], start=(c == 0), stop=False)
                        last = pe.matmul(o, hS[0:ISR, ISC, :], sdb[:], start=False, stop=True)
                    last.then_inc(sem("down_done"), 1)
                pe.wait_ge(sem("x2n"), n + 1)
                for k in range(KC):
                    last = pe.transpose(PS[0][:, k * P:(k + 1) * P], x2n[:, k * P:(k + 1) * P], ident[:])
                last.then_inc(sem("x2nT_done"), 1)
                pe.wait_ge(sem("x2nT_ready"), n + 1)
                for k in range(KC):
                    last = pe.matmul(PS[6][:, 0:E], xuT[:, k, :], gate1[:, k, :],
                                     start=(k == 0), stop=(k == KC - 1))
                last.then_inc(sem("logits1_done"), 1)


STEPS0 = 52
ASTEPS0 = 2


def experts1(nc, A, sem, sb, PS, x_rows, xnT, w_tok, x1_dram):
    with ExitStack() as st:
        NW = 2
        w1 = [sb(st, f"w1_{i}", [P, KC, I1]) for i in range(NW)]
        w3 = [sb(st, f"w3_{i}", [P, KC, I1]) for i in range(NW)]
        w2 = [sb(st, f"w2_{i}", [P, IC1, DM]) for i in range(NW)]
        hs = sb(st, "hs1", [P, 2, 512])
        mark = sb(st, "mark1", [P, 5])
        h = sb(st, "h1", [P, 2, IC1, 512])
        HALVES = T // 512
        UPS = HALVES * IC1
        DOWNS = T // P
        loaded = [sem(f"w1_loaded{i}") for i in range(NW)]
        block = st.enter_context(nc.Block())
        d1 = A["w1T"].rearrange("e (k p) i -> e p k i", p=P)
        d3 = A["w3T"].rearrange("e (k p) i -> e p k i", p=P)
        d2 = A["w2T"].rearrange("e (k p) i -> e p k i", p=P)

        @block.sync
        def _(sp):
            for i in range(NW):
                for dst, src in ((w1, d1), (w3, d3), (w2, d2)):
                    sp.dma_start(dst[i][:], src[i]).then_inc(loaded[i], 16)
            with sp.Fori(1, E // NW) as g:
                for i in range(NW):
                    e = sp.snap(g * NW + i)
                    sp.wait_ge(sem("down1_done"), g * (NW * DOWNS) + (i + 1 - NW) * DOWNS)
                    for dst, src in ((w1, d1), (w3, d3), (w2, d2)):
                        sp.dma_start(dst[i][:], src[bass.ds(e, 1)].rearrange("o p k i -> (o p) k i")).then_inc(loaded[i], 16)
            sp.wait_ge(sem("experts1_done"), 1)
            sp.dma_start(x1_dram.rearrange("(n p) d -> p n d", p=P), x_rows[:]).then_inc(sem("x1_stored"), 16)
            sp.wait_ge(sem("x1_stored"), 16)

        @block.tensor
        def _(pe):
            with pe.Fori(0, E // NW) as g:
                for i in range(NW):
                    pe.wait_ge(loaded[i], g * 48 + 48)
                    for half in range(HALVES):
                        for c in range(IC1):
                            u = half * IC1 + c
                            pe.wait_ge(sem("h1_ready"), g * (NW * UPS) + i * UPS + u + 1)
                            for b, w in ((0, w1), (1, w3)):
                                for k in range(KC):
                                    last = pe.matmul(PS[2 * (u % 2) + b][:], w[i][:, k, c * P:(c + 1) * P],
                                                     xnT[:, k, half * 512:(half + 1) * 512],
                                                     start=(k == 0), stop=(k == KC - 1))
                            last.then_inc(sem("up1_done"), 1)
                        pe.wait_ge(sem("h1_ready"), g * (NW * UPS) + i * UPS + (half + 1) * IC1 + 2)
                        for t in range(4):
                            n = half * 4 + t
                            pe.wait_ge(sem("down1_used"), g * (NW * DOWNS) + i * DOWNS + n + 1)
                            for c in range(IC1):
                                last = pe.matmul(PS[4 + n % 2][:, 0:DM], h[:, half, c, t * P:(t + 1) * P],
                                                 w2[i][:, c, :], start=(c == 0), stop=(c == IC1 - 1))
                            last.then_inc(sem("down1_done"), 1)

        @block.scalar
        def _(a):
            with a.Fori(0, E // NW) as g:
                for i in range(NW):
                    for u in range(UPS):
                        a.wait_ge(sem("up1_done"), g * (NW * UPS) + i * UPS + u + 1)
                        a.wait_ge(sem("h1_ready"), g * (NW * UPS) + i * UPS + u + 1)
                        a.activation(hs[:, u % 2], PS[2 * (u % 2)][:], ACT.Silu).then_inc(sem("silu1_done"), 1)

        @block.vector
        def _(v):
            for j, name in enumerate(("h1_ready", "h1_ready", "down1_used", "down1_used")):
                v.memset(mark[:, j:j + 1], 0.0).then_inc(sem(name), 1)
            with v.Fori(0, E // NW) as g:
                for i in range(NW):
                    for half in range(HALVES):
                        for c in range(IC1):
                            u = half * IC1 + c
                            v.wait_ge(sem("silu1_done"), g * (NW * UPS) + i * UPS + u + 1)
                            v.tensor_tensor(h[:, half, c, :], hs[:, u % 2], PS[2 * (u % 2) + 1][:],
                                            ALU.mult).then_inc(sem("h1_ready"), 1)
                        for t in range(4):
                            n = half * 4 + t
                            v.wait_ge(sem("down1_done"), g * (NW * DOWNS) + i * DOWNS + n + 1)
                            v.scalar_tensor_tensor(
                                out=x_rows[:, n, :], in0=PS[4 + n % 2][:, 0:DM],
                                scalar=w_tok[:, n, bass.ds(g * NW + i, 1)], in1=x_rows[:, n, :],
                                op0=ALU.mult, op1=ALU.add).then_inc(sem("down1_used"), 1)
            v.wait_ge(sem("down1_used"), E * DOWNS + 2)
            v.memset(mark[:, 4:5], 0.0).then_inc(sem("experts1_done"), 1)


def delta1(nc, A, sem, sb, PS, xnT, ident, ones, eps_t, x1_dram, out):
    with ExitStack() as st:
        def s(name, shape, dt=F32):
            return sb(st, "l1_" + name, shape, dt)

        wp = [s(f"wp_{x}", [P, KC, H * D]) for x in "qkvag"]
        wo = s("wo", [P, H, DM])
        wb = s("wb", [P, KC, H])
        cw = s("cw", [P, 3, H, CONV]); cb = s("cb", [P, 3, H]); ba = s("ba", [P, H]); bb = s("bb", [H, 1]); hbb = s("hbb", [H, 1])
        lnw = s("lnw", [P, 1]); lnb = s("lnb", [P, 1])
        maskh = s("maskh", [P, HG, 1])
        pr = s("pr", [P, H, 2, 64])
        raw = s("raw", [P, 2, HH, TB + CONV - 1])
        halo = s("halo", [P, 3, H, CONV - 1])
        ca = s("ca", [P, 2, HH, TB])
        kq = s("kq", [P, 2, H, TB, 2])
        vv = s("vv", [P, 2, H, TB])
        ia = s("ia", [P, H, TB])
        Ef = s("Ef", [P, H * TB // BK, BK])
        eref = s("eref", [P, H, TB // BK]); rho = s("rho", [P, H, TB // BK])
        kb = s("kb", [P, NCH, H, CH])
        ea = s("ea", [P, H, TB])
        gg = s("gg", [P, H, TB])
        dcy = s("dcy", [P, H, NBLK + 1]); edc = s("edc", [P, H, NBLK])
        bt = s("bt", [H, TB])
        gb = s("gb", [P, 2, H, 64])
        gs = s("gs", [P, NG, HG, 2 * (CH - BK)])
        kr = gs[:].rearrange("p g h t -> p (g h t)")[:, 0:NG * D].rearrange("p (g d) -> p g d", g=NG)
        y0 = s("y0", [P, H, TB])
        cbuf = ea[:, 0:HH]
        osq = y0[:]
        Ei = y0[:].rearrange("p h (b t) -> p (h b) t", t=BK)
        aa = on = ca[:].rearrange("p u h t -> p (u h t)").rearrange("p (h t) -> p h t", h=H)
        tmp = s("tmp", [P, H, 16]); z = s("z", [P, H, BK])
        hist = s("hist", [P, H, CH]); hT = s("hT", [P, NG, D])
        S = s("S", [P, H, D]); sT = s("sT", [P, H, D])
        be = pr[0:H, :, 0, :]
        mark = s("mark", [P, 3])
        xr = s("xr", [TB, DM])

        LOADS = [
            *[(wp[i][:], A[f"W{x}T"].rearrange("(k p) e -> p k e", p=P)) for i, x in enumerate("qkvag")],
            (wb[:], A["WbT"].rearrange("(k p) e -> p k e", p=P)),
            *[(cw[:, i], A[f"{x}conv_wT"]) for i, x in enumerate("qkv")],
            *[(cb[:, i], A[f"{x}conv_bT"]) for i, x in enumerate("qkv")],
            (ba[:], A["baT"]), (bb[:], A["bbT"]), (lnw[:], A["ln_wT"]), (lnb[:], A["ln_bT"]),
            (wo[:], A["WoT"].rearrange("(h p) e -> p h e", p=P)),
        ]
        loaded = sem("delta_loaded")
        block = st.enter_context(nc.Block())
        offs = [sum(15 - 2 * q for q in range(t)) for t in range(BK + 1)]

        def heads(ap8):
            return ap8.rearrange("p (h t) -> p h t", h=8)

        @block.sync
        def _(sp):
            for dst, src in LOADS:
                sp.dma_start(dst, src).then_inc(loaded, 16)
            sp.dma_start(xr[:], x1_dram[0:TB]).then_inc(sem("xr_loaded"), 16)
            with sp.Fori(0, NB - 1) as i:
                row = sp.snap(i * TB)
                next_row = sp.snap(i * TB + TB)
                sp.wait_ge(sem("xo_ready"), i + 1)
                sp.dma_start(out[bass.ds(row, TB)], xr[:]).then_inc(sem("out_stored"), 16)
                sp.wait_ge(sem("out_stored"), i * 16 + 16)
                sp.dma_start(xr[:], x1_dram[bass.ds(next_row, TB)]).then_inc(sem("xr_loaded"), 16)
            sp.wait_ge(sem("xo_ready"), NB)
            sp.dma_start(out[T - TB:T], xr[:]).then_inc(sem("out_stored"), 16)
            sp.wait_ge(sem("out_stored"), 16 * NB)

        @block.gpsimd
        def _(g):
            g.memset(maskh[:], 1.0).then_inc(sem("pconst"), 1)
            g.wait_ge(sem("pconst"), 1)
            g.affine_select(out=maskh[:, :, 0], in_=maskh[:, :, 0], compare_op=ALU.is_ge, fill=0.0, base=0,
                            pattern=[[-CH, HG]], channel_multiplier=1).then_inc(sem("pconst"), 1)
            g.wait_ge(sem("pconst"), 2)
            g.affine_select(out=maskh[:, :, 0], in_=maskh[:, :, 0], compare_op=ALU.is_ge, fill=0.0, base=CH - 1,
                            pattern=[[CH, HG]], channel_multiplier=-1).then_inc(sem("mask_ready"), 1)
            with g.Fori(0, NB // 2) as j:
                for u in range(2):
                    i = j * 2 + u
                    g.wait_ge(sem("kb_ready"), i + 1)
                    kqf = kq[:, u].rearrange("p h t j -> p h (t j)")
                    for c in range(NCH):
                        for b in range(NBLK):
                            if c or b >= 2:
                                g.wait_ge(sem("gbc_done"), i * (NCH * NBLK) + c * NBLK + b - 1)
                            t0 = c * CH + b * BK
                            for t in range(BK):
                                w = 15 - 2 * t
                                last = g.tensor_tensor(
                                    pr[:, :, b % 2, offs[t]:offs[t] + w],
                                    kqf[:, :, 2 * t0 + 2 * t + 1:2 * t0 + 2 * BK],
                                    bc(kb[:, c, :, b * BK + t:b * BK + t + 1], [P, H, w]), ALU.mult)
                            last.then_inc(sem("pairs_ready"), 1)

        @block.vector
        def _(v):
            chain = sem("vec1_step")
            v.memset(S[:], 0.0)
            v.memset(xnT[:, :, T:], 0.0)
            v.memset(sT[:], 0.0)
            v.memset(halo[:], 0.0)
            v.wait_ge(loaded, 16 * len(LOADS))
            v.wait_ge(sem("mask_ready"), 1)
            v.tensor_scalar(hbb[:], bb[:], 0.5, None, ALU.mult).then_inc(sem("bb_half"), 1)
            v.memset(mark[:, 0:1], 0.0).then_inc(sem("out_used"), 1)
            v.wait_ge(sem("out_used"), 1)
            m = [0]
            base = [0]

            def step(ins):
                ins.then_inc(chain, 1)
                m[0] += 1
                v.wait_ge(chain, base[0] + m[0])

            def convolve(n, k):
                x, hf = k // 2, k % 2
                hs = slice(HH * hf, HH * hf + HH)
                step(v.tensor_copy(raw[:, hf, :, 0:CONV - 1], halo[:, x, hs]))
                v.wait_ge(sem("raw_ready"), 6 * n + k + 1)
                if not (isinstance(n, int) and k < 2):
                    v.wait_ge(sem("silu_ready"), 6 * n + k - 1)
                for q in range(CONV):
                    w = bc(cw[:, x, hs, q:q + 1], [P, HH, TB])
                    r = raw[:, hf, :, q:q + TB]
                    if q == 0:
                        step(v.tensor_tensor(ca[:, hf], r, w, ALU.mult))
                    else:
                        step(v.tensor_tensor(cbuf, r, w, ALU.mult))
                        step(v.tensor_tensor(ca[:, hf], ca[:, hf], cbuf, ALU.add))
                v.tensor_copy(halo[:, x, hs], raw[:, hf, :, TB:TB + CONV - 1])
                v.tensor_tensor(ca[:, hf], ca[:, hf], bc(cb[:, x, hs].unsqueeze(2), [P, HH, TB]),
                                ALU.add).then_inc(sem("conv_ready"), 1)
                v.wait_ge(sem("conv_ready"), 6 * n + k + 1)

            def decay_logits(n, u):
                v.wait_ge(sem("a_copied"), 2 * n + 2)
                step(v.tensor_tensor(ea[:], ea[:], bc(ba[:].unsqueeze(2), [P, H, TB]), ALU.add))
                v.tensor_scalar(ea[:], ea[:], LOGIT_FLOOR, None, ALU.max).then_inc(sem("a_logits"), 1)

            def invert(n, u, hf):
                hs = slice(HH * hf, HH * hf + HH)
                v.wait_ge(sem("exps1"), n + 1)
                v.wait_ge(sem("silu_ready"), 6 * n + 6)
                step(v.tensor_scalar(ea[:, hs], ea[:, hs], 1.0, None, ALU.add))
                step(v.reciprocal(aa[:, hs], ea[:, hs]))

            def beta_diagonal(n):
                v.wait_ge(sem("beta_tanh"), n + 1)
                step(v.tensor_scalar(bt[:], bt[:], 0.5, 0.5, ALU.mult, ALU.add))
                v.tensor_tensor(be, bc(bt[:].unsqueeze(1), [H, H, TB]),
                                bc(ident[0:H, 0:H].unsqueeze(2), [H, H, TB]), ALU.mult).then_inc(sem("beta_rows"), 1)

            def decays(n, u):
                E = Ef
                a8 = aa.rearrange("p h (b t) -> p (h b) t", t=BK)
                v.tensor_copy(ia[:], ea[:])
                i8 = ea[:].rearrange("p h (b t) -> p (h b) t", t=BK)
                M = BK // 2 - 1
                for src, past, before in ((a8, E, Ei), (i8, Ei, E)):
                    v.tensor_copy(past[:, :, M + 1], src[:, :, M + 1])
                    v.memset(past[:, :, M], 1.0)
                    last = v.tensor_copy(before[:, :, M - 1], src[:, :, M])
                step(last)
                for t in range(1, M):
                    for src, past, before in ((a8, E, Ei), (i8, Ei, E)):
                        v.tensor_tensor(before[:, :, M - 1 - t], before[:, :, M - t], src[:, :, M - t], ALU.mult)
                        last = v.tensor_tensor(past[:, :, M + 1 + t], past[:, :, M + t], src[:, :, M + 1 + t], ALU.mult)
                    step(last)
                er = eref[:].rearrange("p h b -> p (h b)")
                v.tensor_tensor(er, Ei[:, :, 0], a8[:, :, 0], ALU.mult)
                v.tensor_tensor(Ei[:, :, 7], Ei[:, :, 6], i8[:, :, 7], ALU.mult)
                step(v.tensor_tensor(E[:, :, 7], E[:, :, 6], a8[:, :, 7], ALU.mult))
                v.tensor_tensor(rho[:].rearrange("p h b -> p (h b)"), er, E[:, :, 7], ALU.mult)
                step(v.tensor_tensor(vv[:, u], vv[:, u], Ei.rearrange("p (h b) t -> p h (b t)", h=H), ALU.mult))
                step(v.tensor_tensor(vv[:, u], vv[:, u], aa, ALU.mult))

            def scaled_keys(n, u):
                v.wait_ge(sem("beta_done"), n + 1)
                for b in range(2):
                    for c in range(NCH):
                        last = v.scalar_tensor_tensor(
                            out=kb[:, c, 8 * b:8 * b + 8], in0=kq[:, u, 8 * b:8 * b + 8, c * CH:(c + 1) * CH, 0],
                            scalar=SCALE * SCALE, in1=heads(PS[4 + b][:])[:, :, c * CH:(c + 1) * CH],
                            op0=ALU.mult, op1=ALU.mult)
                last.then_inc(sem("kb_ready"), 1)

            for k in range(6):
                convolve(0, k)
            decay_logits(0, 0)
            invert(0, 0, 0)
            invert(0, 0, 1)
            beta_diagonal(0)
            decays(0, 0)
            scaled_keys(0, 0)
            assert m[0] == STEPS1P, m[0]
            m[0] = 0
            with v.Fori(0, NB // 2) as j:
              base[0] = j * STEPS1 + STEPS1P
              for u in range(2):
                i = j * 2 + u
                nxt = j * 2 + u + 1
                vv_ = vv[:, u]
                o = vv_

                for c in range(NCH):
                    g0 = i * NCH + c
                    v.memset(hist[:], 0.0)
                    v.tensor_copy(dcy[:, :, 1:2], rho[:, :, c * NBLK:c * NBLK + 1])
                    step(v.tensor_copy(edc[:, :, 0:1], eref[:, :, c * NBLK:c * NBLK + 1]))
                    for b in range(1, NBLK):
                        v.tensor_tensor(edc[:, :, b:b + 1], dcy[:, :, b:b + 1],
                                        eref[:, :, c * NBLK + b:c * NBLK + b + 1], ALU.mult)
                        step(v.tensor_tensor(dcy[:, :, b + 1:b + 2], dcy[:, :, b:b + 1],
                                             rho[:, :, c * NBLK + b:c * NBLK + b + 1], ALU.mult))
                    for b in range(NBLK):
                        q0 = 2 * BK * b
                        blk = y0[:, :, q0:q0 + 2 * BK]
                        if b == 0:
                            v.wait_ge(sem("y0_done"), g0 + 1)
                        for half in range(2):
                            last = v.tensor_tensor(
                                blk.rearrange("p (g q) c -> p q g c", q=HG)[:, 2 * half:2 * half + 2],
                                PS[half][:].rearrange("p (q g c) -> p q g c", q=2, g=NG)[:, :, :, q0:q0 + 2 * BK],
                                bc(edc[:, :, b:b + 1], [P, H, 2 * BK]).rearrange("p (g q) c -> p q g c", q=HG)[:, 2 * half:2 * half + 2],
                                ALU.mult)
                        step(last)
                        if b:
                            v.wait_ge(sem("seen_done"), g0 * (NBLK - 1) + b)
                            step(v.tensor_tensor(tmp[:], PS[3][:, 0:256].rearrange("p (h t) -> p h t", h=H),
                                                 bc(eref[:, :, c * NBLK + b:c * NBLK + b + 1], [P, H, 2 * BK]), ALU.mult))
                            step(v.tensor_tensor(blk, blk, tmp[:], ALU.subtract))
                        kpart = blk.rearrange("p h (t j) -> p h t j", j=2)[:, :, :, 0]
                        t0 = c * CH + b * BK
                        step(v.tensor_tensor(kpart, kpart, vv_[:, :, t0:t0 + BK], ALU.subtract))
                        if b == 0:
                            v.wait_ge(sem("gram1_done"), g0 + 1)
                            for gi in range(NG):
                                last = v.tensor_tensor(
                                    gs[:, gi], PS[4 + gi // 2][:, (gi % 2) * 256:(gi % 2) * 256 + 256].rearrange(
                                        "p (h t) -> p h t", h=HG)[:, :, 2 * BK:],
                                    bc(maskh[:], [P, HG, 2 * (CH - BK)]), ALU.mult)
                            last.then_inc(sem("gs_ready"), 1)
                        v.wait_ge(sem("gb_ready"), g0 * NBLK + b + 1)
                        for t in range(BK):
                            w = 15 - 2 * t
                            step(v.tensor_tensor(z[:, :, t:t + 1], ia[:, :, t0 + t:t0 + t + 1],
                                                 blk[:, :, 2 * t:2 * t + 1], ALU.mult))
                            step(v.tensor_tensor(tmp[:, :, 0:w], gb[:, b % 2, :, offs[t]:offs[t] + w],
                                                 bc(z[:, :, t:t + 1], [P, H, w]), ALU.mult))
                            ins = v.tensor_tensor(blk[:, :, 2 * t + 1:], blk[:, :, 2 * t + 1:], tmp[:, :, 0:w], ALU.subtract)
                            if t < BK - 1:
                                step(ins)
                            else:
                                ins.then_inc(sem("gb_used"), 1)
                                v.wait_ge(sem("gb_used"), g0 * NBLK + b + 1)
                        e7 = Ef[:].rearrange("p (h b) t -> p h b t", h=H)[:, :, c * NBLK + b, BK - 1:BK]
                        if b:
                            v.tensor_tensor(hist[:, :, 0:BK * b], hist[:, :, 0:BK * b],
                                            bc(rho[:, :, c * NBLK + b:c * NBLK + b + 1], [P, H, BK * b]), ALU.mult)
                        v.tensor_tensor(hist[:, :, BK * b:BK * b + BK], z[:], bc(e7, [P, H, BK]),
                                        ALU.mult).then_inc(sem("hist_ready"), 1)
                        v.wait_ge(sem("hist_ready"), g0 * NBLK + b + 1)
                        if c == 0:
                            for k in ((0,), (1,), (2,), (3, 4))[b]:
                                convolve(nxt, k)
                        elif b == 0:
                            convolve(nxt, 5)
                        elif b == 1:
                            decay_logits(nxt, 1 - u)
                        elif b == 2:
                            invert(nxt, 1 - u, 0)
                        else:
                            invert(nxt, 1 - u, 1)
                            beta_diagonal(nxt)
                    step(v.scalar_tensor_tensor(
                        out=o[:, :, c * CH:(c + 1) * CH], in0=y0[:].rearrange("p h (t j) -> p h t j", j=2)[:, :, :, 1],
                        scalar=1.0 / SCALE,
                        in1=Ef[:].rearrange("p (h b) t -> p h (b t)", h=H)[:, :, c * CH:(c + 1) * CH],
                        op0=ALU.mult, op1=ALU.mult))
                    step(v.tensor_tensor(S[:], S[:], bc(dcy[:, :, NBLK:NBLK + 1], [P, H, D]), ALU.mult))
                    for q in range(HG):
                        v.wait_ge(sem("write_done"), g0 * HG + q + 1)
                        sv = S[:].rearrange("p (g q) d -> p g q d", q=HG)[:, :, q, :]
                        v.tensor_tensor(sv, sv, PS[4 + q][:].rearrange("p (g d) -> p g d", g=NG),
                                        ALU.subtract).then_inc(sem("S_ready"), 1)
                    v.wait_ge(sem("S_ready"), g0 * HG + HG)
                decays(nxt, 1 - u)
                scaled_keys(nxt, 1 - u)
                v.wait_ge(sem("mean_done"), i + 1)
                for b in range(2):
                    last = v.scalar_tensor_tensor(out=o[:, 8 * b:8 * b + 8], in0=heads(PS[b][:]), scalar=-1.0 / D,
                                                  in1=o[:, 8 * b:8 * b + 8], op0=ALU.mult, op1=ALU.add)
                last.then_inc(sem("centred"), 1)
                v.wait_ge(sem("std1_ready"), i + 1)
                step(v.reciprocal(osq, osq))
                step(v.tensor_tensor(o, o, osq, ALU.mult))
                step(v.tensor_scalar(o, o, lnw[:, 0:1], lnb[:, 0:1], ALU.mult, ALU.add))
                step(v.tensor_scalar(gg[:], gg[:], 0.5, 0.5, ALU.mult, ALU.add))
                v.tensor_tensor(on, o, gg[:], ALU.mult).then_inc(sem("gated"), 1)
                v.wait_ge(sem("xr_loaded"), i * 16 + 16)
                v.wait_ge(sem("attn_done"), i + 1)
                v.tensor_tensor(xr[:], xr[:], PS[2][0:TB, 0:DM], ALU.add).then_inc(sem("xo_ready"), 1)
                v.wait_ge(sem("xo_ready"), i + 1)
                v.memset(mark[:, 2:3], 0.0).then_inc(sem("out_used"), 1)
              assert m[0] == STEPS1, m[0]

        @block.scalar
        def _(a):
            def copy_projected(n, k):
                a.wait_ge(sem("proj1_done"), 6 * n + k + 1)
                if not (isinstance(n, int) and k < 2):
                    a.wait_ge(sem("conv_ready"), 6 * n + k - 1)
                a.copy(raw[:, k % 2, :, CONV - 1:], heads(PS[4 + k % 2][:])).then_inc(sem("raw_ready"), 1)

            def silu(n, u, k):
                hs = slice(HH * (k % 2), HH * (k % 2) + HH)
                dst = (kq[:, u, hs, :, 1], kq[:, u, hs, :, 0], vv[:, u, hs])[k // 2]
                a.wait_ge(sem("conv_ready"), 6 * n + k + 1)
                a.activation(dst, ca[:, k % 2], ACT.Silu).then_inc(sem("silu_ready"), 1)

            def copy_logits(n, u):
                for hf in range(2):
                    a.wait_ge(sem("a_done"), 2 * n + hf + 1)
                    a.copy(ea[:, HH * hf:HH * hf + HH], heads(PS[4 + hf][:])).then_inc(sem("a_copied"), 1)

            def gates(n, u):
                a.wait_ge(sem("bb_half"), 1)
                a.wait_ge(sem("b_done"), n + 1)
                a.activation(bt[:], PS[4][0:H, 0:TB], ACT.Tanh, scale=0.5, bias=hbb[:, 0:1]).then_inc(sem("beta_tanh"), 1)
                a.wait_ge(sem("a_logits"), n + 1)
                a.activation(ea[:], ea[:], ACT.Exp, scale=-1.0).then_inc(sem("exps1"), 1)

            for k in range(6):
                copy_projected(0, k)
                silu(0, 0, k)
            copy_logits(0, 0)
            gates(0, 0)
            with a.Fori(0, NB // 2) as j:
              for u in range(2):
                i = j * 2 + u
                nxt = j * 2 + u + 1
                for c in range(NCH):
                    g0 = i * NCH + c
                    for b in range(-1, NBLK):
                        if b < NBLK - 1:
                            a.wait_ge(sem("gbc_done"), g0 * NBLK + b + 2)
                            if b >= 1 or c:
                                a.wait_ge(sem("gb_used"), g0 * NBLK + b)
                            for hh in range(2):
                                last = a.copy(gb[:, (b + 1) % 2, 8 * hh:8 * hh + 8], heads(PS[6 + hh][:]))
                            last.then_inc(sem("gb_ready"), 1)
                        if b < 0:
                            continue
                        if b == NBLK - 1:
                            a.wait_ge(sem("kr_done"), g0 + 1)
                            a.copy(kr.rearrange("p g d -> p (g d)"), PS[2][:]).then_inc(sem("kr_ready"), 1)
                        if c == 0:
                            for k in ((), (0,), (1,), (2,))[b]:
                                silu(nxt, 1 - u, k)
                            for k in ((0,), (1,), (2,), (3, 4))[b]:
                                copy_projected(nxt, k)
                        elif b == 0:
                            silu(nxt, 1 - u, 3)
                            silu(nxt, 1 - u, 4)
                            copy_projected(nxt, 5)
                        elif b == 1:
                            silu(nxt, 1 - u, 5)
                            copy_logits(nxt, 1 - u)
                        elif b == 2:
                            a.wait_ge(sem("g_done"), 2 * i + 1)
                            a.activation(gg[:, 0:HH], heads(PS[5][:]), ACT.Tanh, scale=0.5).then_inc(sem("g_ready"), 1)
                            gates(nxt, 1 - u)
                        else:
                            a.wait_ge(sem("g_done"), 2 * i + 2)
                            a.activation(gg[:, HH:H], heads(PS[4][:]), ACT.Tanh, scale=0.5).then_inc(sem("g_ready"), 1)
                        a.wait_ge(sem("histT_done"), g0 * NBLK + b + 1)
                        a.copy(hT[:].rearrange("p g d -> p (g d)"), PS[2][:]).then_inc(sem("hT_ready"), 1)
                    for q in range(HG):
                        a.wait_ge(sem("sT_done"), g0 * HG + q + 1)
                        a.copy(sT[:].rearrange("p (g q) d -> p g q d", q=HG)[:, :, q, :],
                               PS[4 + q][:].rearrange("p (g d) -> p g d", g=NG)).then_inc(sem("sT_ready"), 1)
                a.wait_ge(sem("centred"), i + 1)
                a.activation(osq, vv[:, u], ACT.Square).then_inc(sem("squared"), 1)
                a.wait_ge(sem("var_done"), i + 1)
                for b in range(2):
                    last = a.activation(osq[:, 8 * b:8 * b + 8], heads(PS[b][:]), ACT.Sqrt, scale=1.0 / D,
                                        bias=eps_t[:, 0:1])
                last.then_inc(sem("std1_ready"), 1)

        @block.tensor
        def _(pe):
            pe.wait_ge(loaded, 16 * len(LOADS))
            pe.wait_ge(sem("out_used"), 1)

            def project(w, hf, bank, n):
                for h in range(HH):
                    for k in range(KC):
                        hd = HH * hf + h
                        last = pe.matmul(PS[bank][:, h * TB:(h + 1) * TB], w[:, k, hd * D:(hd + 1) * D],
                                         xnT[:, k, bass.ds(n * TB, TB)], start=(k == 0), stop=(k == KC - 1))
                return last

            def project_qkv(n, k):
                if not (isinstance(n, int) and k < 2):
                    pe.wait_ge(sem("raw_ready"), 6 * n + k - 1)
                project(wp[k // 2], k % 2, 4 + k % 2, n).then_inc(sem("proj1_done"), 1)

            def project_a(n):
                for hf in range(2):
                    pe.wait_ge(sem("raw_ready"), 6 * n + 5 + hf)
                    project(wp[3], hf, 4 + hf, n).then_inc(sem("a_done"), 1)

            def project_b(n):
                for k in range(KC):
                    last = pe.matmul(PS[4][0:H, 0:TB], wb[:, k, :], xnT[:, k, bass.ds(n * TB, TB)],
                                     start=(k == 0), stop=(k == KC - 1))
                last.then_inc(sem("b_done"), 1)

            def spread_beta(n):
                pe.wait_ge(sem("beta_rows"), n + 1)
                for b in range(2):
                    last = pe.matmul(PS[4 + b][:], ones[0:H, :], be[:, 8 * b:8 * b + 8, :], start=True, stop=True)
                last.then_inc(sem("beta_done"), 1)

            for k in range(6):
                project_qkv(0, k)
            project_a(0)
            pe.wait_ge(sem("a_copied"), 2)
            project_b(0)
            spread_beta(0)
            with pe.Fori(0, NB // 2) as j:
              for u in range(2):
                i = j * 2 + u
                nxt = j * 2 + u + 1
                pe.wait_ge(sem("out_used"), i + 1)
                pe.wait_ge(sem("kb_ready"), i + 1)
                kqf = kq[:, u].rearrange("p h t j -> p h (t j)")
                for c in range(NCH):
                    g0 = i * NCH + c
                    for q in range(HG):
                        if c:
                            pe.wait_ge(sem("sT_ready"), g0 * HG - HG + q + 1)
                        for g in range(NG):
                            p0 = ((q % 2) * NG + g) * 64
                            last = pe.matmul(PS[q // 2][:, p0:p0 + 64], sT[:, HG * g + q, :],
                                             kqf[:, HG * g + q, 2 * c * CH:2 * (c + 1) * CH], start=True, stop=True)
                    last.then_inc(sem("y0_done"), 1)

                    def pair_sums(b):
                        pe.wait_ge(sem("pairs_ready"), g0 * NBLK + b + 1)
                        for hh in range(2):
                            last = pe.matmul(PS[6 + hh][:], ones[:], pr[:, 8 * hh:8 * hh + 8, b % 2, :], start=True, stop=True)
                        last.then_inc(sem("gbc_done"), 1)
                    pair_sums(0)
                    for g in range(NG):
                        last = pe.matmul(PS[4 + g // 2][:, (g % 2) * 256:(g % 2) * 256 + 256],
                                         kb[:, c, HG * g:HG * g + HG, :],
                                         kqf[:, HG * g:HG * g + HG, 2 * c * CH:2 * (c + 1) * CH], start=True, stop=True)
                    last.then_inc(sem("gram1_done"), 1)
                    for b in range(NBLK):
                        if b < NBLK - 1:
                            pe.wait_ge(sem("gb_ready"), g0 * NBLK + b + 1)
                            pair_sums(b + 1)
                        if b == 0:
                            pe.wait_ge(sem("gs_ready"), g0 + 1)
                        if b == NBLK - 1:
                            for g in range(NG):
                                last = pe.transpose(PS[2][:, g * P:(g + 1) * P], kb[:, c, HG * g:HG * g + HG, :],
                                                    ident[:])
                            last.then_inc(sem("kr_done"), 1)
                        if c == 0:
                            for k in ((0,), (1,), (2,), (3, 4))[b]:
                                project_qkv(nxt, k)
                        elif b == 0:
                            project_qkv(nxt, 5)
                        elif b == 1:
                            project_a(nxt)
                        elif b == 2:
                            pe.wait_ge(sem("a_copied"), 2 * nxt + 2)
                            project(wp[4], 0, 5, i).then_inc(sem("g_done"), 1)
                            project_b(nxt)
                        else:
                            pe.wait_ge(sem("beta_tanh"), nxt + 1)
                            project(wp[4], 1, 4, i).then_inc(sem("g_done"), 1)
                        if b == NBLK - 1:
                            pe.wait_ge(sem("kr_ready"), g0 + 1)
                        pe.wait_ge(sem("hist_ready"), g0 * NBLK + b + 1)
                        for g in range(NG):
                            last = pe.transpose(PS[2][:, g * P:(g + 1) * P], hist[:, HG * g:HG * g + HG, :], ident[:])
                        last.then_inc(sem("histT_done"), 1)
                        pe.wait_ge(sem("hT_ready"), g0 * NBLK + b + 1)
                        if b < NBLK - 1:
                            for g in range(NG):
                                last = pe.matmul(PS[3][:, g * 64:(g + 1) * 64], hT[:, g, :],
                                                 gs[:, g, :, 2 * BK * b:2 * BK * (b + 1)], start=True, stop=True)
                            last.then_inc(sem("seen_done"), 1)
                    pe.wait_ge(sem("gb_ready"), g0 * NBLK + NBLK)
                    if c == 0:
                        pe.wait_ge(sem("raw_ready"), 6 * nxt + 5)
                    else:
                        pe.wait_ge(sem("g_ready"), 2 * i + 2)
                    for q in range(HG):
                        for g in range(NG):
                            last = pe.matmul(PS[4 + q][:, g * D:(g + 1) * D], hT[CH * q:CH * q + CH, g, :],
                                             kr[CH * q:CH * q + CH, g, :], start=True, stop=True)
                        last.then_inc(sem("write_done"), 1)
                    for q in range(HG):
                        pe.wait_ge(sem("S_ready"), g0 * HG + q + 1)
                        for g in range(NG):
                            last = pe.transpose(PS[4 + q][:, g * P:(g + 1) * P], S[:, HG * g + q, :], ident[:])
                        last.then_inc(sem("sT_done"), 1)
                pe.wait_ge(sem("sT_ready"), (i * NCH + NCH) * HG)
                spread_beta(nxt)
                for b in range(2):
                    last = pe.matmul(PS[b][:], ones[:], vv[:, u, 8 * b:8 * b + 8, :], start=True, stop=True)
                last.then_inc(sem("mean_done"), 1)
                pe.wait_ge(sem("squared"), i + 1)
                for b in range(2):
                    last = pe.matmul(PS[b][:], ones[:], osq[:, 8 * b:8 * b + 8, :], start=True, stop=True)
                last.then_inc(sem("var_done"), 1)
                pe.wait_ge(sem("gated"), i + 1)
                for h in range(H):
                    last = pe.matmul(PS[2][0:TB, 0:DM], on[:, h, :], wo[:, h, :], start=(h == 0), stop=(h == H - 1))
                last.then_inc(sem("attn_done"), 1)


STEPS1 = 576
STEPS1P = 60


def kernel(**inputs):
    import numpy as np
    import concourse.bacc as bacc
    from concourse.bass_utils import run_bass_kernel_spmd as run

    nc = bacc.Bacc("TRN2", target_bir_lowering=False, num_devices=1)
    i = {k: np.asarray(v) for k, v in inputs.items()}
    c = np.ascontiguousarray
    arrays = {
        "L0_attn_u": c(i["L0_attn_u"].reshape(T, DM)),
        "in_projT": c(i["L0_attn_in_proj_w"].T),
        "out_projT": c(i["L0_attn_out_proj_w"].T),
        "gate0T": c(np.concatenate([i["L0_ffn_gate_w"].T, i["L0_ffn_shared_gate_w"]], axis=1)),
        "gate1T": c(i["L1_ffn_gate_w"].T),
        "w1T": c(i["L1_ffn_w1"].transpose(0, 2, 1)),
        "w3T": c(i["L1_ffn_w3"].transpose(0, 2, 1)),
        "w2T": c(i["L1_ffn_w2"].transpose(0, 2, 1)),
        "WbT": c(i["L1_attn_Wb"].T),
        "WoT": c(i["L1_attn_Wo"].T),
        "baT": c(i["L1_attn_ba"].reshape(H, D).T),
        "bbT": c(i["L1_attn_bb"].reshape(H, 1)),
        "ln_wT": c(i["L1_attn_ln_w"].reshape(D, 1)),
        "ln_bT": c(i["L1_attn_ln_b"].reshape(D, 1)),
    }
    for x in "qkvag":
        arrays[f"W{x}T"] = c(i[f"L1_attn_W{x}"].T)
    for x in "qkv":
        arrays[f"{x}conv_wT"] = c(i[f"L1_attn_{x}conv_w"].reshape(H, D, CONV).transpose(1, 0, 2))
        arrays[f"{x}conv_bT"] = c(i[f"L1_attn_{x}conv_b"].reshape(H, D).T)
    for name in ("L0_attn_D", "L0_attn_dt_bias", "L0_attn_A_log", "L0_attn_bnorm_w", "L0_attn_cnorm_w",
                 "L0_attn_ln_w", "L0_attn_ln_b", "L0_ffn_w_gate", "L0_ffn_w_up", "L0_ffn_w_down",
                 "L0_ffn_sw_gate", "L0_ffn_sw_up", "L0_ffn_sw_down"):
        arrays[name] = c(i[name])
    A = {n: nc.dram_tensor(f"in_{n}", a.shape, mybir.dt.from_np(a.dtype), kind="ExternalInput").ap()
         for n, a in arrays.items()}
    out = nc.dram_tensor("out", (T, DM), F32, kind="ExternalOutput").ap()
    program(nc, A, out)
    r = run(nc, [{f"in_{n}": a for n, a in arrays.items()}], core_ids=[0])
    return r.results[0]["out"].reshape(1, T, DM)
```

```python
from contextlib import ExitStack

import concourse.bass as bass
from concourse import mybir

F32 = mybir.dt.float32
U32 = mybir.dt.uint32
ALU = mybir.AluOpType
ACT = mybir.ActivationFunctionType
AX = mybir.AxisListType

P = 128
EPS = 1e-5

T = 1024
DM = 256
KC = DM // P
NT = T // P

DI = 512
NH0 = 8
HP0 = DI // NH0
DS = 128
DPROJ = 2 * DI + 2 * DS + NH0
NBD = 2 * DS + NH0

E = 8
I0 = 176
I0B = I0 - P
IS = 704
ISC = 5
ISR = IS - ISC * P

H = 16
D = 128
CONV = 4
TB = 64
NB = T // TB
CH = 32
BK = 8
NCH = TB // CH
NBLK = CH // BK
HH = H // 2
HG = 4
NG = H // HG
SCALE = float(D) ** -0.5
LOGIT_FLOOR = -20.0

I1 = 512
IC1 = I1 // P


def program(nc, A, out):
    ctx = ExitStack()
    with ctx:
        sems = {}

        def sem(name):
            if name not in sems:
                sems[name] = ctx.enter_context(nc.semaphore(name))
            return sems[name]

        def sb(stack, name, shape, dt=F32):
            return stack.enter_context(nc.sbuf_tensor(name, shape, dt))

        xnT = sb(ctx, "xnT", [P, KC, T + 2 * TB])
        ident = sb(ctx, "ident", [P, P])
        ones = sb(ctx, "ones", [P, P])
        eps_t = sb(ctx, "eps_t", [P, 1])
        x1_dram = nc.dram_tensor("x1_scratch", (T, DM), F32, kind="Internal").ap()

        PS = [ctx.enter_context(nc.psum_tensor(f"bank{i}", [P, 512], F32)) for i in range(8)]

        wp = [sb(ctx, f"l1_wp_{x}", [P, KC, H * D]) for x in "qkva"]

        with ExitStack() as rows_stack:
            mean_w = sb(rows_stack, "mean_w", [P, P])
            x_rows = sb(rows_stack, "x_rows", [P, NT + 1, DM])
            w_tok = sb(rows_stack, "w_tok", [P, NT, E])
            layer0(nc, A, sem, sb, PS, x_rows, xnT, w_tok, ident, ones, mean_w, eps_t, wp)
            experts1(nc, A, sem, sb, PS, x_rows, xnT, w_tok, x1_dram)
        delta1(nc, A, sem, sb, PS, xnT, ident, ones, eps_t, wp, x1_dram, out)


def bc(ap, shape):
    return ap.broadcast_to(shape)


def layer0(nc, A, sem, sb, PS, x_rows, xnT, w_tok, ident, ones, mean_w, eps_t, wp):
    with ExitStack() as st:
        def s(name, shape, dt=F32):
            return sb(st, "l0_" + name, shape, dt)

        win = s("win", [P, KC, DPROJ])
        wout = s("wout", [P, DI // P, DM])
        wg = s("wg", [P, E, KC, I0])
        wu = s("wu", [P, E, KC, I0])
        wda = s("wda", [P, E, DM])
        wdb = s("wdb", [I0B, E, DM])
        sg = s("sg", [P, KC, IS])
        su = s("su", [P, KC, IS])
        sda = s("sda", [P, ISC, DM])
        sdb = s("sdb", [ISR, DM])
        gate = s("gate", [P, KC, E + 1])
        gate1 = s("gate1", [P, KC, E])
        rows = s("rows", [P, 2 * DM + 2 * DS])
        hrows = s("hrows", [P, 3, NH0])
        triu = s("triu", [P, P])
        iota = s("iota", [P, E])
        neg_a = s("neg_a", [P, NH0])
        st6 = s("st6", [P, 6]); mv = s("mv", [P, 2]); std = s("std", [P, 1]); rstd = s("rstd", [P, 1])
        xn = s("xn", [P, DM]); un = s("un", [P, DM])
        xuT = s("xuT", [P, 2 * KC, P])
        zs = s("zs", [P, DI]); xs = s("xs", [P, DI])
        sq = s("sq", [P, 2, P]); ssq = s("ssq", [P, 2]); rms = s("rms", [P, 2]); rrms = s("rrms", [P, 2])
        bcn = s("bcn", [P, 2, DS]); bcT = s("bcT", [P, 2, P])
        dtv = s("dtv", [P, NH0]); dta = s("dta", [P, NH0]); dte = s("dte", [P, NH0]); dtl = s("dtl", [P, NH0])
        dA = s("dA", [P, NH0]); dAx = s("dAx", [P, NH0, P])
        cum = s("cum", [P, NH0]); tot = s("tot", [P, NH0]); dend = s("dend", [P, NH0])
        dec_end = s("dec_end", [P, NH0]); dec_in = s("dec_in", [P, NH0]); rho = s("rho", [P, NH0])
        Ld = Le = s("Ld", [P, NH0, P])
        Gm = s("Gm", [P, P])
        S0 = s("S0", [P, DI]); xdec = s("xdec", [P, DI])
        y = s("y", [P, DI]); yt = s("yt", [P, DI]); yT = s("yT", [P, DI // P, P])
        lg = s("lg", [P, E + 1]); m8 = s("m8", [P, 8]); i8 = s("i8", [P, 8], U32); i8f = s("i8f", [P, 8])
        nmax = s("nmax", [P, 1]); ex = s("ex", [P, E]); eq0 = s("eq0", [P, E]); eq1 = s("eq1", [P, E])
        msum = s("msum", [P, 1]); mrec = s("mrec", [P, 1]); cw = s("cw", [P, E + 1]); tg = s("tg", [P, 1])
        NGRP = 6
        hs = s("hs", [P, 2, 4, P])
        hA = s("hA", [P, E, P])
        hB = s("hB", [I0B, E, P])
        hS = s("hS", [P, ISC + 1, P])
        acc = s("acc", [P, DM])
        m8b = s("m8b", [P, 8]); i8b = s("i8b", [P, 8], U32)
        fac = s("fac", [P, E]); dif = s("dif", [P, E]); keep = s("keep", [P, E])
        e12 = s("e12", [P, 2, E]); ek = s("ek", [P, 2, E]); den = s("den", [P, 2]); rden = s("rden", [P, 2])
        taken = s("taken", [P, 1])
        zero8 = s("zero8", [P, E]); ones8 = s("ones8", [P, E])
        x2n = s("x2n", [P, DM]); x2T = s("x2T", [P, KC, P])

        groups = [[("e", e, 0, P) for e in range(4)], [("e", e, 0, P) for e in range(4, 8)],
                  [("e", e, P, I0B) for e in range(4)], [("e", e, P, I0B) for e in range(4, 8)],
                  [("s", c, c * P, P) for c in range(4)],
                  [("s", 4, 4 * P, P), ("s", 5, 5 * P, ISR)]]

        LOADS = [
            (x_rows[:, 0:NT], A["L0_attn_u"].rearrange("(n p) d -> p n d", p=P)),
            (win[:], A["in_projT"].rearrange("(k p) e -> p k e", p=P)),
            (rows[:, 0:DM], A["L0_attn_ln_w"].partition_broadcast(P)),
            (rows[:, DM:2 * DM], A["L0_attn_ln_b"].partition_broadcast(P)),
            (rows[:, 2 * DM:2 * DM + DS], A["L0_attn_bnorm_w"].partition_broadcast(P)),
            (rows[:, 2 * DM + DS:], A["L0_attn_cnorm_w"].partition_broadcast(P)),
            (hrows[:, 0], A["L0_attn_D"].partition_broadcast(P)),
            (hrows[:, 1], A["L0_attn_dt_bias"].partition_broadcast(P)),
            (hrows[:, 2], A["L0_attn_A_log"].partition_broadcast(P)),
            (wout[:], A["out_projT"].rearrange("(k p) e -> p k e", p=P)),
            (gate[:], A["gate0T"].rearrange("(k p) e -> p k e", p=P)),
            (gate1[:], A["gate1T"].rearrange("(k p) e -> p k e", p=P)),
            (wg[:, 0:4], A["L0_ffn_w_gate"][0:4].rearrange("e (k p) i -> p e k i", p=P)),
            (wg[:, 4:8], A["L0_ffn_w_gate"][4:8].rearrange("e (k p) i -> p e k i", p=P)),
            (wu[:, 0:4], A["L0_ffn_w_up"][0:4].rearrange("e (k p) i -> p e k i", p=P)),
            (wu[:, 4:8], A["L0_ffn_w_up"][4:8].rearrange("e (k p) i -> p e k i", p=P)),
            (sg[:], A["L0_ffn_sw_gate"].rearrange("(k p) i -> p k i", p=P)),
            (su[:], A["L0_ffn_sw_up"].rearrange("(k p) i -> p k i", p=P)),
            (wda[:], A["L0_ffn_w_down"][:, 0:P].rearrange("e p d -> p e d")),
            (wdb[:], A["L0_ffn_w_down"][:, P:I0].rearrange("e p d -> p e d")),
            (sda[:], A["L0_ffn_sw_down"][0:ISC * P].rearrange("(c p) d -> p c d", p=P)),
            (sdb[:], A["L0_ffn_sw_down"][ISC * P:IS]),
        ]
        MIXER_LOADS = 12
        loaded, experts_loaded = sem("weights0_loaded"), sem("experts0_loaded")
        block = st.enter_context(nc.Block())

        @block.sync
        def _(sp):
            for dst, src in LOADS[:MIXER_LOADS]:
                sp.dma_start(dst, src).then_inc(loaded, 16)
            for dst, src in LOADS[MIXER_LOADS:]:
                sp.dma_start(dst, src).then_inc(experts_loaded, 16)
            for w, x in zip(wp, "qkva"):
                sp.dma_start(w[:], A[f"W{x}T"].rearrange("(k p) e -> p k e", p=P)).then_inc(sem("wp_loaded"), 16)

        @block.gpsimd
        def _(g):
            const = sem("const_step")
            g.memset(ident[:], 0.0).then_inc(const, 1)
            g.memset(triu[:], 1.0).then_inc(const, 1)
            g.wait_ge(const, 2)
            g.affine_select(out=ident[:], in_=ident[:], compare_op=ALU.not_equal, fill=1.0,
                            base=0, pattern=[[-1, P]], channel_multiplier=1)
            g.affine_select(out=triu[:], in_=triu[:], compare_op=ALU.is_ge, fill=0.0,
                            base=0, pattern=[[1, P]], channel_multiplier=-1)
            g.iota(iota[:], pattern=[[1, E]], base=0, channel_multiplier=0,
                   allow_small_or_imprecise_dtypes=True).then_inc(sem("consts_ready"), 1)

        @block.vector
        def _(v):
            chain = sem("vec0_step")
            v.memset(x_rows[:, NT], 0.0)
            v.memset(ones[:], 1.0)
            v.memset(mean_w[:], 1.0 / P)
            v.memset(zero8[:], 0.0)
            v.memset(ones8[:], 1.0)
            v.memset(S0[:], 0.0)
            v.memset(eps_t[:], EPS).then_inc(sem("vconst_ready"), 1)
            v.wait_ge(sem("vconst_ready"), 1)
            v.wait_ge(loaded, 16 * MIXER_LOADS)
            v.wait_ge(sem("consts_ready"), 1)
            v.wait_ge(sem("nega_exp"), 1)
            v.tensor_scalar(neg_a[:], neg_a[:], -1.0, None, ALU.mult).then_inc(sem("tile0_done"), 1)
            v.wait_ge(sem("tile0_done"), 1)

            m, base = [0], [0]

            def step(ins):
                ins.then_inc(chain, 1)
                m[0] += 1
                v.wait_ge(chain, base[0] + m[0])

            def take_wait():
                v.memset(taken[:], 0.0)

            def moments(src):
                take_wait()
                step(v.bn_stats(st6[:], src))
                take_wait()
                v.bn_aggr(mv[:], st6[:]).then_inc(sem("moments"), 1)

            def centred(dst, src, k):
                v.wait_ge(sem("std_ready"), k)
                step(v.reciprocal(rstd[:], std[:]))
                return v.tensor_scalar(dst, src, mv[:, 0:1], rstd[:, 0:1], ALU.subtract, ALU.mult)

            def norm_input(n, k, part):
                if part == 0:
                    moments(x_rows[:, n, :])
                elif part == 1:
                    step(centred(xn[:], x_rows[:, n, :], k + 1))
                    moments(xn[:])
                else:
                    step(centred(un[:], xn[:], k + 2))
                    step(v.tensor_tensor(un[:], un[:], rows[:, 0:DM], ALU.mult))
                    v.tensor_tensor(un[:], un[:], rows[:, DM:2 * DM], ALU.add).then_inc(sem("xn_un"), 1)

            for part in range(3):
                norm_input(0, 0, part)
            assert m[0] == STEPS0P, m[0]
            with v.Fori(0, NT) as n:
                m[0] = 0
                base[0] = n * STEPS0 + STEPS0P

                def hidden(gi):
                    grp = groups[gi]
                    v.wait_ge(sem("up_done"), NGRP * n + gi + 1)
                    v.wait_ge(sem("silu_done"), NGRP * n + gi + 1)
                    ub = PS[5 if gi % 2 == 0 else 7]
                    kind, c0 = grp[0][0], grp[0][1]
                    if gi == 5:
                        v.tensor_tensor(hS[:, 4, :], hs[:, 1, 0, :], ub[:, 0:P], ALU.mult)
                        last = v.tensor_tensor(hS[0:ISR, 5, :], hs[0:ISR, 1, 1, :], ub[0:ISR, P:2 * P], ALU.mult)
                    else:
                        m_rows = grp[0][3]
                        dst = hS if kind == "s" else hA if m_rows == P else hB
                        last = v.tensor_tensor(
                            dst[0:m_rows, c0:c0 + 4, :], hs[0:m_rows, gi % 2],
                            ub[0:m_rows].rearrange("p (c t) -> p c t", c=4), ALU.mult)
                    last.then_inc(sem("h_ready"), 1)

                v.tensor_tensor(acc[:], x_rows[:, n, :], xn[:], ALU.add)
                v.wait_ge(sem("proj_done"), n + 1)
                v.tensor_copy(xs[:], PS[2][:])
                step(v.tensor_tensor(dtv[:], PS[3][:, 2 * DS:NBD], hrows[:, 1], ALU.add))
                v.scalar_tensor_tensor(out=dta[:], in0=dtv[:], scalar=-1.0, in1=dtv[:],
                                       op0=ALU.mult, op1=ALU.max).then_inc(sem("dt_abs"), 1)
                v.wait_ge(sem("dt_ln"), n + 1)
                step(v.scalar_tensor_tensor(out=dtv[:], in0=dtv[:], scalar=0.0, in1=dtl[:],
                                            op0=ALU.max, op1=ALU.add))
                step(v.tensor_tensor(dA[:], dtv[:], neg_a[:], ALU.mult))
                v.tensor_tensor(dAx[:], bc(triu[:].unsqueeze(1), [P, NH0, P]),
                                bc(dA[:].unsqueeze(2), [P, NH0, P]), ALU.mult).then_inc(sem("dA_ready"), 1)
                v.wait_ge(sem("ssq_rms"), n + 1)
                step(v.reciprocal(rrms[:], rms[:]))
                for j in range(2):
                    last = v.scalar_tensor_tensor(
                        out=bcn[:, j], in0=PS[3][:, j * DS:(j + 1) * DS], scalar=rrms[:, j:j + 1],
                        in1=rows[:, 2 * DM + j * DS:2 * DM + (j + 1) * DS], op0=ALU.mult, op1=ALU.mult)
                last.then_inc(sem("bc_normed"), 1)
                hidden(0)
                v.wait_ge(sem("cum_done"), n + 1)
                v.tensor_copy(tot[:], PS[3][:, NH0:2 * NH0])
                step(v.tensor_copy(cum[:], PS[3][:, 0:NH0]))
                step(v.tensor_tensor(dend[:], tot[:], cum[:], ALU.subtract))
                for h in range(NH0):
                    last = v.tensor_scalar(Ld[:, h, :], PS[1 + h // 4][:, (h % 4) * P:(h % 4 + 1) * P],
                                           cum[:, h:h + 1], 0.0, ALU.subtract, ALU.min)
                last.then_inc(sem("logs_ready"), 1)
                hidden(1)
                v.wait_ge(sem("gram_done"), n + 1)
                step(v.tensor_tensor(Gm[:], PS[0][:, 2 * P:3 * P], triu[:], ALU.mult))
                v.wait_ge(sem("exps_ready"), n + 1)
                v.tensor_tensor(xdec[:].rearrange("p (h q) -> p h q", h=NH0),
                                xs[:].rearrange("p (h q) -> p h q", h=NH0),
                                bc(dec_end[:].unsqueeze(2), [P, NH0, HP0]), ALU.mult)
                v.tensor_tensor(Le[:], Le[:], bc(Gm[:].unsqueeze(1), [P, NH0, P]),
                                ALU.mult).then_inc(sem("mix_ready"), 1)
                v.tensor_tensor(yt[:].rearrange("p (h q) -> p h q", h=NH0),
                                xs[:].rearrange("p (h q) -> p h q", h=NH0),
                                bc(hrows[:, 0].unsqueeze(2), [P, NH0, HP0]), ALU.mult)
                step(v.tensor_copy(lg[:], PS[0][:, 3 * P:3 * P + E + 1]))
                take_wait()
                step(v.max(m8[:], lg[:, 0:E]))
                take_wait()
                step(v.max_index(i8[:], m8[:], lg[:, 0:E]))
                v.tensor_copy(i8f[:], i8[:])
                v.tensor_scalar(nmax[:], m8[:, 0:1], -1.0, None, ALU.mult).then_inc(sem("nmax0"), 1)
                v.wait_ge(sem("nmax0"), n + 1)
                v.tensor_scalar(eq0[:], iota[:], i8f[:, 0:1], None, ALU.is_equal)
                step(v.tensor_scalar(eq1[:], iota[:], i8f[:, 1:2], None, ALU.is_equal))
                step(v.tensor_tensor(eq0[:], eq0[:], eq1[:], ALU.add))
                v.wait_ge(sem("router_exp"), n + 1)
                step(v.tensor_tensor(ex[:], ex[:], eq0[:], ALU.mult))
                step(v.reduce_sum(msum[:], ex[:], AX.X))
                step(v.reciprocal(mrec[:], msum[:]))
                v.tensor_scalar(cw[:, 0:E], ex[:], mrec[:, 0:1], None, ALU.mult)
                step(v.tensor_scalar(cw[:, E:E + 1], tg[:], 1.0, 0.5, ALU.add, ALU.mult))
                hidden(2)
                hidden(3)
                v.wait_ge(sem("y_done"), n + 1)
                step(v.tensor_tensor(y[:].rearrange("p (h q) -> p h q", h=NH0),
                                     PS[2][:].rearrange("p (h q) -> p h q", h=NH0),
                                     bc(dec_in[:].unsqueeze(2), [P, NH0, HP0]), ALU.mult))
                step(v.tensor_tensor(y[:], y[:], PS[1][:], ALU.add))
                step(v.tensor_tensor(y[:], y[:], yt[:], ALU.add))
                v.tensor_tensor(y[:], y[:], zs[:], ALU.mult).then_inc(sem("y_ready"), 1)
                step(v.tensor_tensor(S0[:].rearrange("p (h q) -> p h q", h=NH0),
                                     S0[:].rearrange("p (h q) -> p h q", h=NH0),
                                     bc(rho[:].unsqueeze(2), [P, NH0, HP0]), ALU.mult))
                step(v.tensor_tensor(S0[:], S0[:], PS[3][:], ALU.add))

                hidden(4)

                v.wait_ge(sem("mixer_done"), n + 1)
                step(v.tensor_tensor(acc[:], acc[:], PS[1][:, 0:DM], ALU.add))

                hidden(5)
                for e in range(E + 1):
                    v.wait_ge(sem("down_done"), (E + 1) * n + e + 1)
                    v.scalar_tensor_tensor(out=acc[:] if e < E else x_rows[:, n, :],
                                           in0=PS[1 + e % 2][:, 0:DM], scalar=cw[:, e:e + 1], in1=acc[:],
                                           op0=ALU.mult, op1=ALU.add).then_inc(sem("down_used"), 1)
                    v.wait_ge(sem("down_used"), (E + 1) * n + e + 1)
                    if e in (0, 3, 6):
                        norm_input(n + 1, 3 * n + 2, e // 3)
                moments(x_rows[:, n, :])
                centred(x2n[:], x_rows[:, n, :], 3 * n + 5).then_inc(sem("x2n"), 1)
                v.wait_ge(sem("logits1_done"), n + 1)
                lg1 = lg[:, 0:E]
                step(v.tensor_copy(lg1, PS[6][:, 0:E]))
                take_wait()
                step(v.max(m8b[:], lg1))
                take_wait()
                step(v.max_index(i8b[:], m8b[:], lg1))
                v.tensor_copy(i8f[:], i8b[:])
                v.tensor_scalar(ek[:, 0], lg1, m8b[:, 0:1], 0.0, ALU.subtract, ALU.min)
                v.tensor_scalar(ek[:, 1], lg1, m8b[:, 1:2], 0.0, ALU.subtract, ALU.min).then_inc(sem("nmax1"), 1)
                v.wait_ge(sem("nmax1"), n + 1)
                v.tensor_scalar(eq0[:], iota[:], i8f[:, 0:1], None, ALU.is_equal)
                step(v.tensor_scalar(eq1[:], iota[:], i8f[:, 1:2], None, ALU.is_equal))
                v.wait_ge(sem("router_exp1"), n + 1)
                for j in range(2):
                    step(v.scalar_tensor_tensor(out=fac[:], in0=lg1, scalar=-1.0, in1=lg1, op0=ALU.mult, op1=ALU.max))
                    step(v.tensor_scalar(fac[:], fac[:], m8b[:, j:j + 1], None, ALU.max))
                    step(v.tensor_scalar(dif[:], lg1, -1.0, m8b[:, j:j + 1], ALU.mult, ALU.add))
                    step(v.scalar_tensor_tensor(out=keep[:], in0=fac[:], scalar=0.02, in1=dif[:],
                                                op0=ALU.mult, op1=ALU.is_ge))
                    if j == 1:
                        step(v.tensor_tensor(fac[:], ones8[:], eq0[:], ALU.subtract))
                        step(v.tensor_tensor(keep[:], keep[:], fac[:], ALU.mult))
                    step(v.tensor_tensor(ek[:, j], e12[:, j], keep[:], ALU.mult))
                    step(v.reduce_sum(den[:, j:j + 1], ek[:, j], AX.X))
                step(v.reciprocal(rden[:], den[:]))
                step(v.tensor_scalar(eq0[:], eq0[:], rden[:, 0:1], None, ALU.mult))
                step(v.scalar_tensor_tensor(out=w_tok[:, n, :], in0=eq1[:], scalar=rden[:, 1:2], in1=eq0[:],
                                            op0=ALU.mult, op1=ALU.add))
                v.wait_ge(sem("x2nT_kept"), n + 1)
                v.tensor_copy(tg[:], tg[:]).then_inc(sem("tile0_done"), 1)
                assert m[0] == STEPS0, m[0]

        @block.scalar
        def _(a):
            a.wait_ge(loaded, 16 * MIXER_LOADS)
            a.wait_ge(sem("vconst_ready"), 1)
            a.activation(neg_a[:], hrows[:, 2], ACT.Exp).then_inc(sem("nega_exp"), 1)

            def std_of(k):
                a.wait_ge(sem("moments"), k)
                a.activation(std[:], mv[:, 1:2], ACT.Sqrt, bias=eps_t[:, 0:1]).then_inc(sem("std_ready"), 1)

            def copy_transposed(n):
                a.wait_ge(sem("xn_T"), n + 1)
                a.copy(xuT[:].rearrange("p c t -> p (c t)"), PS[0][:]).then_inc(sem("xuT_ready"), 1)

            std_of(1)
            std_of(2)
            copy_transposed(0)
            with a.Fori(0, NT) as n:
                m = [0]

                def step(ins):
                    ins.then_inc(sem("act0_step"), 1)
                    m[0] += 1
                    a.wait_ge(sem("act0_step"), n * ASTEPS0 + m[0])

                def silu_of(gi):
                    grp = groups[gi]
                    a.wait_ge(sem("up_done"), NGRP * n + gi + 1)
                    if gi >= 2:
                        a.wait_ge(sem("h_ready"), NGRP * n + gi - 1)
                    gb = PS[4 if gi % 2 == 0 else 6]
                    if gi == 5:
                        a.activation(hs[:, 1, 0, :], gb[:, 0:P], ACT.Silu)
                        last = a.activation(hs[0:ISR, 1, 1, :], gb[0:ISR, P:2 * P], ACT.Silu)
                    else:
                        r = grp[0][3]
                        last = a.activation(hs[0:r, gi % 2].rearrange("p c t -> p (c t)"), gb[0:r, :], ACT.Silu)
                    last.then_inc(sem("silu_done"), 1)

                a.wait_ge(sem("dt_abs"), n + 1)
                for j in range(2):
                    last = a.activation(sq[:, j], PS[3][:, j * DS:(j + 1) * DS], ACT.Square,
                                        accum_out=ssq[:, j:j + 1])
                step(last)
                step(a.activation(dte[:], dta[:], ACT.Exp, scale=-1.0))
                a.activation(dtl[:], dte[:], ACT.Ln, bias=1.0).then_inc(sem("dt_ln"), 1)
                a.activation(rms[:], ssq[:], ACT.Sqrt, bias=eps_t[:, 0:1],
                             scale=1.0 / DS).then_inc(sem("ssq_rms"), 1)
                a.activation(zs[:], PS[1][:], ACT.Silu).then_inc(sem("z_ready"), 1)
                silu_of(0)
                a.wait_ge(sem("bcT_done"), n + 1)
                a.copy(bcT[:].rearrange("p c t -> p (c t)"), PS[0][:, 0:2 * P]).then_inc(sem("bcT_ready"), 1)
                silu_of(1)
                a.wait_ge(sem("logs_ready"), n + 1)
                a.activation(dec_in[:], cum[:], ACT.Exp)
                a.activation(rho[:], tot[:], ACT.Exp)
                a.activation(dec_end[:], dend[:], ACT.Exp)
                a.activation(Le[:], Ld[:], ACT.Exp).then_inc(sem("exps_ready"), 1)
                a.wait_ge(sem("nmax0"), n + 1)
                a.activation(ex[:], lg[:, 0:E], ACT.Exp, bias=nmax[:, 0:1])
                a.activation(tg[:], lg[:, E:E + 1], ACT.Tanh, scale=0.5).then_inc(sem("router_exp"), 1)
                silu_of(2)
                silu_of(3)
                silu_of(4)
                a.wait_ge(sem("yT_done"), n + 1)
                a.copy(yT[:].rearrange("p c t -> p (c t)"), PS[0][:]).then_inc(sem("yT_ready"), 1)
                silu_of(5)
                std_of(3 * n + 3)
                std_of(3 * n + 4)
                copy_transposed(n + 1)
                std_of(3 * n + 5)
                a.wait_ge(sem("x2nT_done"), n + 1)
                a.copy(x2T[:].rearrange("p c t -> p (c t)"), PS[0][:, 0:2 * P]).then_inc(sem("x2nT_ready"), 1)
                a.copy(xnT[:, :, bass.ts(n, P)], PS[0][:, 0:2 * P].rearrange("p (c t) -> p c t", c=KC)).then_inc(sem("x2nT_kept"), 1)
                a.wait_ge(sem("nmax1"), n + 1)
                a.activation(e12[:], ek[:], ACT.Exp).then_inc(sem("router_exp1"), 1)
                assert m[0] == ASTEPS0, m[0]

        @block.tensor
        def _(pe):
            pe.wait_ge(loaded, 16 * MIXER_LOADS)
            pe.wait_ge(sem("consts_ready"), 1)

            def transpose_input(n):
                pe.wait_ge(sem("xn_un"), n + 1)
                for j in range(2):
                    for k in range(KC):
                        last = pe.transpose(PS[0][:, (2 * j + k) * P:(2 * j + k + 1) * P],
                                            (xn, un)[j][:, k * P:(k + 1) * P], ident[:])
                last.then_inc(sem("xn_T"), 1)

            def project(n):
                pe.wait_ge(sem("xuT_ready"), n + 1)
                for b, (c0, c1) in enumerate([(0, DI), (DI, 2 * DI), (2 * DI, DPROJ)]):
                    for k in range(KC):
                        last = pe.matmul(PS[1 + b][:, 0:c1 - c0], xuT[:, KC + k, :], win[:, k, c0:c1],
                                         start=(k == 0), stop=(k == KC - 1))
                last.then_inc(sem("proj_done"), 1)

            pe.wait_ge(sem("tile0_done"), 1)
            transpose_input(0)
            project(0)
            with pe.Fori(0, NT) as n:
                def up(gi):
                    if gi >= 2:
                        pe.wait_ge(sem("h_ready"), NGRP * n + gi - 1)
                    gb, ub = (PS[4], PS[5]) if gi % 2 == 0 else (PS[6], PS[7])
                    for bank, we, ws in ((gb, wg, sg), (ub, wu, su)):
                        for c, (kind, e, i0, r) in enumerate(groups[gi]):
                            for k in range(KC):
                                w = we[:, e, k, i0:i0 + r] if kind == "e" else ws[:, k, i0:i0 + r]
                                last = pe.matmul(bank[0:r, c * P:(c + 1) * P], w, xuT[:, k, :],
                                                 start=(k == 0), stop=(k == KC - 1))
                    last.then_inc(sem("up_done"), 1)

                pe.wait_ge(experts_loaded, 16 * (len(LOADS) - MIXER_LOADS))
                up(0)
                pe.wait_ge(sem("tile0_done"), n + 1)
                up(1)
                pe.wait_ge(sem("bc_normed"), n + 1)
                for j in range(2):
                    last = pe.transpose(PS[0][:, j * P:(j + 1) * P], bcn[:, j], ident[:])
                last.then_inc(sem("bcT_done"), 1)
                pe.wait_ge(sem("dA_ready"), n + 1)
                pe.matmul(PS[3][:, 0:NH0], triu[:], dA[:], start=True, stop=True)
                pe.matmul(PS[3][:, NH0:2 * NH0], ones[:], dA[:], start=True, stop=True)
                pe.wait_ge(sem("z_ready"), n + 1)
                for b in range(2):
                    last = pe.matmul(PS[1 + b][:], ones[:], dAx[:, 4 * b:4 * b + 4, :], start=True, stop=True)
                last.then_inc(sem("cum_done"), 1)
                pe.wait_ge(sem("bcT_ready"), n + 1)
                for k in range(KC):
                    pe.matmul(PS[0][:, 3 * P:3 * P + E + 1], xuT[:, k, :], gate[:, k, :],
                              start=(k == 0), stop=(k == KC - 1))
                pe.matmul(PS[0][:, 2 * P:3 * P], bcT[:, 0], bcT[:, 1], start=True, stop=True).then_inc(sem("gram_done"), 1)
                up(2)
                up(3)
                pe.wait_ge(sem("mix_ready"), n + 1)
                pe.matmul(PS[2][:], bcT[:, 1], S0[:], start=True, stop=True)
                for h in range(NH0):
                    pe.matmul(PS[1][:, h * HP0:(h + 1) * HP0], Le[:, h, :], xs[:, h * HP0:(h + 1) * HP0],
                              start=True, stop=True)
                pe.matmul(PS[3][:], bcn[:, 0], xdec[:], start=True, stop=True).then_inc(sem("y_done"), 1)
                up(4)
                pe.wait_ge(sem("y_ready"), n + 1)
                for c in range(DI // P):
                    last = pe.transpose(PS[0][:, c * P:(c + 1) * P], y[:, c * P:(c + 1) * P], ident[:])
                last.then_inc(sem("yT_done"), 1)
                up(5)
                pe.wait_ge(sem("yT_ready"), n + 1)
                for c in range(DI // P):
                    last = pe.matmul(PS[1][:, 0:DM], yT[:, c, :], wout[:, c, :], start=(c == 0), stop=(c == DI // P - 1))
                last.then_inc(sem("mixer_done"), 1)
                pe.wait_ge(sem("h_ready"), NGRP * n + NGRP)
                for e in range(E + 1):
                    o = PS[1 + e % 2][:, 0:DM]
                    if e >= 2:
                        pe.wait_ge(sem("down_used"), (E + 1) * n + e - 1)
                    if e < E:
                        pe.matmul(o, hA[:, e, :], wda[:, e, :], start=True, stop=False)
                        last = pe.matmul(o, hB[:, e, :], wdb[:, e, :], start=False, stop=True)
                    else:
                        for c in range(ISC):
                            pe.matmul(o, hS[:, c, :], sda[:, c, :], start=(c == 0), stop=False)
                        last = pe.matmul(o, hS[0:ISR, ISC, :], sdb[:], start=False, stop=True)
                    last.then_inc(sem("down_done"), 1)
                transpose_input(n + 1)
                pe.wait_ge(sem("xuT_ready"), n + 2)
                pe.wait_ge(sem("x2n"), n + 1)
                for k in range(KC):
                    last = pe.transpose(PS[0][:, k * P:(k + 1) * P], x2n[:, k * P:(k + 1) * P], ident[:])
                last.then_inc(sem("x2nT_done"), 1)
                pe.wait_ge(sem("x2nT_ready"), n + 1)
                for k in range(KC):
                    last = pe.matmul(PS[6][:, 0:E], x2T[:, k, :], gate1[:, k, :],
                                     start=(k == 0), stop=(k == KC - 1))
                last.then_inc(sem("logits1_done"), 1)
                pe.wait_ge(sem("down_used"), (E + 1) * n + E + 1)
                project(n + 1)


STEPS0 = 52
STEPS0P = 7
ASTEPS0 = 2


def experts1(nc, A, sem, sb, PS, x_rows, xnT, w_tok, x1_dram):
    with ExitStack() as st:
        NW = 2
        w1 = [sb(st, f"w1_{i}", [P, KC, I1]) for i in range(NW)]
        w3 = [sb(st, f"w3_{i}", [P, KC, I1]) for i in range(NW)]
        w2 = [sb(st, f"w2_{i}", [P, IC1, DM]) for i in range(NW)]
        hs = sb(st, "hs1", [P, 2, 512])
        mark = sb(st, "mark1", [P, 5])
        h = sb(st, "h1", [P, 2, IC1, 512])
        HALVES = T // 512
        UPS = HALVES * IC1
        DOWNS = T // P
        loaded = [sem(f"w1_loaded{i}") for i in range(NW)]
        block = st.enter_context(nc.Block())
        d1 = A["w1T"].rearrange("e (k p) i -> e p k i", p=P)
        d3 = A["w3T"].rearrange("e (k p) i -> e p k i", p=P)
        d2 = A["w2T"].rearrange("e (k p) i -> e p k i", p=P)

        @block.sync
        def _(sp):
            for i in range(NW):
                for dst, src in ((w1, d1), (w3, d3), (w2, d2)):
                    sp.dma_start(dst[i][:], src[i]).then_inc(loaded[i], 16)
            with sp.Fori(1, E // NW) as g:
                for i in range(NW):
                    e = sp.snap(g * NW + i)
                    sp.wait_ge(sem("down1_done"), g * (NW * DOWNS) + (i + 1 - NW) * DOWNS)
                    for dst, src in ((w1, d1), (w3, d3), (w2, d2)):
                        sp.dma_start(dst[i][:], src[bass.ds(e, 1)].rearrange("o p k i -> (o p) k i")).then_inc(loaded[i], 16)
            sp.wait_ge(sem("experts1_done"), 1)
            sp.dma_start(x1_dram.rearrange("(n p) d -> p n d", p=P), x_rows[:, 0:NT]).then_inc(sem("x1_stored"), 16)
            sp.wait_ge(sem("x1_stored"), 16)

        @block.tensor
        def _(pe):
            with pe.Fori(0, E // NW) as g:
                for i in range(NW):
                    pe.wait_ge(loaded[i], g * 48 + 48)
                    for half in range(HALVES):
                        for c in range(IC1):
                            u = half * IC1 + c
                            pe.wait_ge(sem("h1_ready"), g * (NW * UPS) + i * UPS + u + 1)
                            for b, w in ((0, w1), (1, w3)):
                                for k in range(KC):
                                    last = pe.matmul(PS[2 * (u % 2) + b][:], w[i][:, k, c * P:(c + 1) * P],
                                                     xnT[:, k, half * 512:(half + 1) * 512],
                                                     start=(k == 0), stop=(k == KC - 1))
                            last.then_inc(sem("up1_done"), 1)
                        pe.wait_ge(sem("h1_ready"), g * (NW * UPS) + i * UPS + (half + 1) * IC1 + 2)
                        for t in range(4):
                            n = half * 4 + t
                            pe.wait_ge(sem("down1_used"), g * (NW * DOWNS) + i * DOWNS + n + 1)
                            for c in range(IC1):
                                last = pe.matmul(PS[4 + n % 2][:, 0:DM], h[:, half, c, t * P:(t + 1) * P],
                                                 w2[i][:, c, :], start=(c == 0), stop=(c == IC1 - 1))
                            last.then_inc(sem("down1_done"), 1)

        @block.scalar
        def _(a):
            with a.Fori(0, E // NW) as g:
                for i in range(NW):
                    for u in range(UPS):
                        a.wait_ge(sem("up1_done"), g * (NW * UPS) + i * UPS + u + 1)
                        a.wait_ge(sem("h1_ready"), g * (NW * UPS) + i * UPS + u + 1)
                        a.activation(hs[:, u % 2], PS[2 * (u % 2)][:], ACT.Silu).then_inc(sem("silu1_done"), 1)

        @block.vector
        def _(v):
            for j, name in enumerate(("h1_ready", "h1_ready", "down1_used", "down1_used")):
                v.memset(mark[:, j:j + 1], 0.0).then_inc(sem(name), 1)
            with v.Fori(0, E // NW) as g:
                for i in range(NW):
                    for half in range(HALVES):
                        for c in range(IC1):
                            u = half * IC1 + c
                            v.wait_ge(sem("silu1_done"), g * (NW * UPS) + i * UPS + u + 1)
                            v.tensor_tensor(h[:, half, c, :], hs[:, u % 2], PS[2 * (u % 2) + 1][:],
                                            ALU.mult).then_inc(sem("h1_ready"), 1)
                        for t in range(4):
                            n = half * 4 + t
                            v.wait_ge(sem("down1_done"), g * (NW * DOWNS) + i * DOWNS + n + 1)
                            v.scalar_tensor_tensor(
                                out=x_rows[:, n, :], in0=PS[4 + n % 2][:, 0:DM],
                                scalar=w_tok[:, n, bass.ds(g * NW + i, 1)], in1=x_rows[:, n, :],
                                op0=ALU.mult, op1=ALU.add).then_inc(sem("down1_used"), 1)
            v.wait_ge(sem("down1_used"), E * DOWNS + 2)
            v.memset(mark[:, 4:5], 0.0).then_inc(sem("experts1_done"), 1)


def delta1(nc, A, sem, sb, PS, xnT, ident, ones, eps_t, wp, x1_dram, out):
    with ExitStack() as st:
        def s(name, shape, dt=F32):
            return sb(st, "l1_" + name, shape, dt)

        wgate = s("wgate", [P, KC, H * D])
        wo = s("wo", [P, H, DM])
        wb = s("wb", [P, KC, H])
        cw = s("cw", [P, 3, H, CONV]); cb = s("cb", [P, 3, H])
        ba = s("ba", [P, H]); bb = s("bb", [H, 1]); hbb = s("hbb", [H, 1]); half_t = s("half", [H, 1])
        lnw = s("lnw", [P, 1]); lnb = s("lnb", [P, 1])
        maskh = s("maskh", [P, HG, 1])
        pr = s("pr", [P, H, 2, 64])
        raw = s("raw", [P, 2, HH, TB + CONV - 1])
        halo = s("halo", [P, 3, H, CONV - 1])
        ca = s("ca", [P, 2, HH, TB])
        kq = s("kq", [P, 2, H, TB, 2])
        vv = s("vv", [P, 2, H, TB])
        ia = s("ia", [P, H, TB])
        Ef = s("Ef", [P, H * TB // BK, BK])
        eref = s("eref", [P, H, TB // BK]); rho = s("rho", [P, H, TB // BK])
        kb = s("kb", [P, NCH, H, CH])
        ea = s("ea", [P, H, TB])
        gg = s("gg", [P, H, TB])
        dcy = s("dcy", [P, H, NBLK + 1]); edc = s("edc", [P, H, NBLK])
        bt = s("bt", [H, TB])
        gb = s("gb", [P, 2, H, 64])
        gs = s("gs", [P, NG, HG, 2 * (CH - BK)])
        kr = gs[:].rearrange("p g h t -> p (g h t)")[:, 0:NG * D].rearrange("p (g d) -> p g d", g=NG)
        y0 = s("y0", [P, H, TB])
        Ei = y0[:].rearrange("p h (b t) -> p (h b) t", t=BK)
        aa = on = ca[:].rearrange("p u h t -> p (u h t)").rearrange("p (h t) -> p h t", h=H)
        tmp = s("tmp", [P, H, 16]); z = s("z", [P, H, BK])
        hist = s("hist", [P, H, CH]); hT = s("hT", [P, NG, D])
        S = s("S", [P, H, D]); sT = s("sT", [P, H, D])
        osq = gb[:, 1]
        be = pr[0:H, :, 0, :]
        mark = s("mark", [P, 3])
        xr = s("xr", [TB, DM])

        LOADS = [
            (wb[:], A["WbT"].rearrange("(k p) e -> p k e", p=P)),
            *[(cw[:, i], A[f"{x}conv_wT"]) for i, x in enumerate("qkv")],
            *[(cb[:, i], A[f"{x}conv_bT"]) for i, x in enumerate("qkv")],
            (ba[:], A["baT"]), (bb[:], A["bbT"]), (lnw[:], A["ln_wT"]), (lnb[:], A["ln_bT"]),
        ]
        loaded = sem("delta_loaded")
        block = st.enter_context(nc.Block())
        offs = [sum(15 - 2 * q for q in range(t)) for t in range(BK + 1)]

        def heads(ap8):
            return ap8.rearrange("p (h t) -> p h t", h=8)

        @block.sync
        def _(sp):
            for dst, src in LOADS:
                sp.dma_start(dst, src).then_inc(loaded, 16)
            sp.dma_start(wgate[:], A["WgT"].rearrange("(k p) e -> p k e", p=P)).then_inc(sem("wo_loaded"), 16)
            sp.dma_start(wo[:], A["WoT"].rearrange("(h p) e -> p h e", p=P)).then_inc(sem("wo_loaded"), 16)
            sp.dma_start(xr[:], x1_dram[0:TB]).then_inc(sem("xr_loaded"), 16)
            with sp.Fori(0, NB - 1) as i:
                row = sp.snap(i * TB)
                next_row = sp.snap(i * TB + TB)
                sp.wait_ge(sem("xo_ready"), i + 2)
                sp.dma_start(out[bass.ds(row, TB)], xr[:]).then_inc(sem("out_stored"), 16)
                sp.wait_ge(sem("out_stored"), i * 16 + 16)
                sp.dma_start(xr[:], x1_dram[bass.ds(next_row, TB)]).then_inc(sem("xr_loaded"), 16)
            sp.wait_ge(sem("xo_ready"), NB + 1)
            sp.dma_start(out[T - TB:T], xr[:]).then_inc(sem("out_stored"), 16)
            sp.wait_ge(sem("out_stored"), 16 * NB)

        @block.gpsimd
        def _(g):
            g.memset(maskh[:], 1.0).then_inc(sem("pconst"), 1)
            g.wait_ge(sem("pconst"), 1)
            g.affine_select(out=maskh[:, :, 0], in_=maskh[:, :, 0], compare_op=ALU.is_ge, fill=0.0, base=0,
                            pattern=[[-CH, HG]], channel_multiplier=1).then_inc(sem("pconst"), 1)
            g.wait_ge(sem("pconst"), 2)
            g.affine_select(out=maskh[:, :, 0], in_=maskh[:, :, 0], compare_op=ALU.is_ge, fill=0.0, base=CH - 1,
                            pattern=[[CH, HG]], channel_multiplier=-1).then_inc(sem("mask_ready"), 1)

            def pairs(i, u, c, b):
                kqf = kq[:, u].rearrange("p h t j -> p h (t j)")
                if c or b >= 2:
                    g.wait_ge(sem("gbc_done"), i * (NCH * NBLK) + c * NBLK + b - 1)
                t0 = c * CH + b * BK
                for t in range(BK):
                    w = 15 - 2 * t
                    last = g.tensor_tensor(
                        pr[:, :, b % 2, offs[t]:offs[t] + w],
                        kqf[:, :, 2 * t0 + 2 * t + 1:2 * t0 + 2 * BK],
                        bc(kb[:, c, :, b * BK + t:b * BK + t + 1], [P, H, w]), ALU.mult)
                last.then_inc(sem("pairs_ready"), 1)

            def beta_diagonal(n):
                g.wait_ge(sem("beta_ready"), n + 1)
                g.tensor_tensor(be, bc(bt[:].unsqueeze(1), [H, H, TB]),
                                bc(ident[0:H, 0:H].unsqueeze(2), [H, H, TB]), ALU.mult).then_inc(sem("beta_rows"), 1)

            beta_diagonal(0)
            g.wait_ge(sem("kb_ready"), 1)
            pairs(0, 0, 0, 0)
            pairs(0, 0, 0, 1)
            with g.Fori(0, NB // 2) as j:
                for u in range(2):
                    i = j * 2 + u
                    for c in range(NCH):
                        for b in range(0 if c else 2, NBLK):
                            pairs(i, u, c, b)
                    g.wait_ge(sem("gbc_done"), (i + 1) * (NCH * NBLK))
                    beta_diagonal(i + 1)
                    g.wait_ge(sem("kb_ready"), i + 2)
                    pairs(i + 1, 1 - u, 0, 0)
                    pairs(i + 1, 1 - u, 0, 1)

        @block.vector
        def _(v):
            chain = sem("vec1_step")
            v.memset(S[:], 0.0)
            v.memset(half_t[:], 0.5)
            v.memset(Ef[:, :, BK // 2 - 1], 1.0)
            v.memset(xnT[:, :, T:], 0.0)
            v.memset(sT[:], 0.0)
            v.memset(halo[:], 0.0)
            v.wait_ge(loaded, 16 * len(LOADS))
            v.wait_ge(sem("mask_ready"), 1)
            v.tensor_scalar(hbb[:], bb[:], 0.5, None, ALU.mult).then_inc(sem("bb_half"), 1)
            v.tensor_scalar(lnw[:], lnw[:], 0.5, None, ALU.mult)
            v.tensor_scalar(lnb[:], lnb[:], 0.5, None, ALU.mult)
            v.memset(mark[:, 0:1], 0.0).then_inc(sem("xo_ready"), 1)
            v.wait_ge(sem("xo_ready"), 1)
            m = [0]
            base = [0]

            def step(ins, meanwhile=None):
                ins.then_inc(chain, 1)
                m[0] += 1
                if meanwhile is not None:
                    meanwhile()
                v.wait_ge(chain, base[0] + m[0])

            def tap(k, q, h):
                return v.scalar_tensor_tensor(
                    out=ca[:, k % 2, h], in0=raw[:, k % 2, h, q:q + TB],
                    scalar=cw[:, k // 2, HH * (k % 2) + h, q:q + 1], in1=ca[:, k % 2, h], op0=ALU.mult, op1=ALU.add)

            def keep_halo(k):
                hs = slice(HH * (k % 2), HH * (k % 2) + HH)
                v.tensor_copy(halo[:, k // 2, hs], raw[:, k % 2, :, TB:TB + CONV - 1]).then_inc(sem("conv_ready"), 1)

            def convolve(n, k, taps=CONV - 1):
                x, hf = k // 2, k % 2
                hs = slice(HH * hf, HH * hf + HH)
                step(v.tensor_copy(raw[:, hf, :, 0:CONV - 1], halo[:, x, hs]))
                v.wait_ge(sem("raw_ready"), 6 * n + k + 1)
                for q in range(taps):
                    for h in range(HH):
                        last = tap(k, q, h)
                    if q < CONV - 2:
                        step(last)
                if taps == CONV - 1:
                    keep_halo(k)

            def decay_logits(n):
                v.wait_ge(sem("a_copied"), 2 * n + 2)
                step(v.tensor_tensor(ea[:], ea[:], bc(ba[:].unsqueeze(2), [P, H, TB]), ALU.add))
                v.tensor_scalar(ea[:], ea[:], LOGIT_FLOOR, None, ALU.max).then_inc(sem("a_logits"), 1)

            def decays(n, u):
                v.wait_ge(sem("a_ready"), n + 1)
                a8 = aa.rearrange("p h (b t) -> p (h b) t", t=BK)
                i8 = ia[:].rearrange("p h (b t) -> p (h b) t", t=BK)
                M = BK // 2 - 1
                v.memset(Ei[:, :, M], 1.0)
                step(v.tensor_scalar(ia[:], ea[:], 1.0, None, ALU.add))
                for src, past, before in ((a8, Ef, Ei), (i8, Ei, Ef)):
                    v.tensor_copy(past[:, :, M + 1], src[:, :, M + 1])
                    last = v.tensor_copy(before[:, :, M - 1], src[:, :, M])
                step(last)
                for t in range(1, M):
                    for src, past, before in ((a8, Ef, Ei), (i8, Ei, Ef)):
                        v.tensor_tensor(before[:, :, M - 1 - t], before[:, :, M - t], src[:, :, M - t], ALU.mult)
                        last = v.tensor_tensor(past[:, :, M + 1 + t], past[:, :, M + t], src[:, :, M + 1 + t], ALU.mult)
                    step(last)
                er = eref[:].rearrange("p h b -> p (h b)")
                v.tensor_tensor(er, Ei[:, :, 0], a8[:, :, 0], ALU.mult)
                step(v.tensor_tensor(Ef[:, :, 7], Ef[:, :, 6], a8[:, :, 7], ALU.mult))
                v.tensor_tensor(rho[:].rearrange("p h b -> p (h b)"), er, Ef[:, :, 7], ALU.mult)
                v8 = vv[:, u].rearrange("p h (b t) -> p (h b) t", t=BK)
                v.tensor_tensor(v8[:, :, 0], v8[:, :, 0], er, ALU.mult)
                step(v.tensor_tensor(v8[:, :, 1:BK], v8[:, :, 1:BK], Ei[:, :, 0:BK - 1], ALU.mult))

            def scaled_keys(n, u):
                v.wait_ge(sem("beta_done"), n + 1)
                for b in range(2):
                    for c in range(NCH):
                        last = v.scalar_tensor_tensor(
                            out=kb[:, c, 8 * b:8 * b + 8], in0=kq[:, u, 8 * b:8 * b + 8, c * CH:(c + 1) * CH, 0],
                            scalar=SCALE * SCALE, in1=heads(PS[b][:])[:, :, c * CH:(c + 1) * CH],
                            op0=ALU.mult, op1=ALU.mult)
                last.then_inc(sem("kb_ready"), 1)

            def chunk_decays(c):
                v.memset(hist[:], 0.0)
                v.tensor_copy(dcy[:, :, 1:2], rho[:, :, c * NBLK:c * NBLK + 1])
                step(v.tensor_copy(edc[:, :, 0:1], eref[:, :, c * NBLK:c * NBLK + 1]))
                for b in range(1, NBLK):
                    v.tensor_tensor(edc[:, :, b:b + 1], dcy[:, :, b:b + 1],
                                    eref[:, :, c * NBLK + b:c * NBLK + b + 1], ALU.mult)
                    step(v.tensor_tensor(dcy[:, :, b + 1:b + 2], dcy[:, :, b:b + 1],
                                         rho[:, :, c * NBLK + b:c * NBLK + b + 1], ALU.mult))

            def seen_by_state(b, half):
                q0 = 2 * BK * b
                return v.tensor_tensor(
                    y0[:, :, q0:q0 + 2 * BK].rearrange("p (g q) c -> p q g c", q=HG)[:, 2 * half:2 * half + 2],
                    PS[half][:].rearrange("p (q g c) -> p q g c", q=2, g=NG)[:, :, :, q0:q0 + 2 * BK],
                    bc(edc[:, :, b:b + 1], [P, H, 2 * BK]).rearrange("p (g q) c -> p q g c", q=HG)[:, 2 * half:2 * half + 2],
                    ALU.mult)

            def less_values(u, c, b):
                kpart = y0[:, :, 2 * BK * b:2 * BK * (b + 1)].rearrange("p h (t j) -> p h t j", j=2)[:, :, :, 0]
                t0 = c * CH + b * BK
                return v.tensor_tensor(kpart, kpart, vv[:, u, :, t0:t0 + BK], ALU.subtract)

            def mask_gram(gi):
                return v.tensor_tensor(
                    gs[:, gi], PS[4 + gi // 2][:, (gi % 2) * 256:(gi % 2) * 256 + 256].rearrange(
                        "p (h t) -> p h t", h=HG)[:, :, 2 * BK:],
                    bc(maskh[:], [P, HG, 2 * (CH - BK)]), ALU.mult)

            for k in range(6):
                convolve(0, k)
            decay_logits(0)
            decays(0, 0)
            scaled_keys(0, 0)
            chunk_decays(0)
            assert m[0] == STEPS1P, m[0]
            m[0] = 0
            with v.Fori(0, NB // 2) as j:
                base[0] = j * STEPS1 + STEPS1P
                for u in range(2):
                    i = j * 2 + u
                    nxt = j * 2 + u + 1
                    o = vv[:, u]

                    for c in range(NCH):
                        g0 = i * NCH + c
                        for b in range(NBLK):
                            q0 = 2 * BK * b
                            blk = y0[:, :, q0:q0 + 2 * BK]
                            t0 = c * CH + b * BK
                            if b == 0:
                                v.wait_ge(sem("y0_done"), g0 + 1)
                                seen_by_state(0, 0)
                                step(seen_by_state(0, 1))
                                step(less_values(u, c, 0))
                            if b:
                                v.wait_ge(sem("seen_done"), g0 * (NBLK - 1) + b)
                                step(v.tensor_tensor(tmp[:], PS[3][:, 0:256].rearrange("p (h t) -> p h t", h=H),
                                                     bc(eref[:, :, c * NBLK + b:c * NBLK + b + 1], [P, H, 2 * BK]), ALU.mult))
                                step(v.tensor_tensor(blk, blk, tmp[:], ALU.subtract))
                            if b == 0:
                                v.wait_ge(sem("gram1_done"), g0 + 1)
                                for gi in range(NG):
                                    last = mask_gram(gi)
                                last.then_inc(sem("gs_ready"), 1)
                            v.wait_ge(sem("gb_ready"), g0 * NBLK + b + 1)
                            unit = b - 1 if (c, b) in ((0, 1), (0, 2)) else 5 if (c, b) == (1, 1) else None

                            def between(t):
                                if b < NBLK - 1 and t >= BK - 3:
                                    if t < BK - 1:
                                        seen_by_state(b + 1, t - (BK - 3))
                                    else:
                                        less_values(u, c, b + 1)

                            def last_tap(t):
                                if unit is not None:
                                    tap(unit, CONV - 2, t)
                                    if t == BK - 1:
                                        keep_halo(unit)

                            e7 = Ef[:].rearrange("p (h b) t -> p h b t", h=H)[:, :, c * NBLK + b, BK - 1:BK]
                            for t in range(BK):
                                w = 15 - 2 * t
                                step(v.tensor_tensor(z[:, :, t:t + 1], ia[:, :, t0 + t:t0 + t + 1],
                                                     blk[:, :, 2 * t:2 * t + 1], ALU.mult), lambda: last_tap(t))
                                if t == BK - 1:
                                    v.tensor_tensor(hist[:, :, BK * b:BK * b + BK], z[:], bc(e7, [P, H, BK]),
                                                    ALU.mult).then_inc(sem("hist_ready"), 1)
                                step(v.tensor_tensor(tmp[:, :, 0:w], gb[:, b % 2, :, offs[t]:offs[t] + w],
                                                     bc(z[:, :, t:t + 1], [P, H, w]), ALU.mult), lambda: between(t))
                                ins = v.tensor_tensor(blk[:, :, 2 * t + 1:], blk[:, :, 2 * t + 1:], tmp[:, :, 0:w], ALU.subtract)
                                if t < BK - 1:
                                    step(ins)
                                else:
                                    ins.then_inc(sem("gb_used"), 1)
                            v.wait_ge(sem("gb_used"), g0 * NBLK + b + 1)
                            if c == 0:
                                convolve(nxt, b, CONV - 2 if b < 2 else CONV - 1)
                            elif b == 0:
                                convolve(nxt, 5, CONV - 2)
                            elif b == 1:
                                decay_logits(nxt)
                            if b < NBLK - 1:
                                v.wait_ge(sem("histT_done"), g0 * NBLK + b + 1)
                                v.tensor_tensor(hist[:, :, 0:BK * (b + 1)], hist[:, :, 0:BK * (b + 1)],
                                                bc(rho[:, :, c * NBLK + b + 1:c * NBLK + b + 2], [P, H, BK * (b + 1)]), ALU.mult)
                        step(v.scalar_tensor_tensor(
                            out=o[:, :, c * CH:(c + 1) * CH], in0=y0[:].rearrange("p h (t j) -> p h t j", j=2)[:, :, :, 1],
                            scalar=1.0 / SCALE,
                            in1=Ef[:].rearrange("p (h b) t -> p h (b t)", h=H)[:, :, c * CH:(c + 1) * CH],
                            op0=ALU.mult, op1=ALU.mult))
                        if c == NCH - 1:
                            scaled_keys(nxt, 1 - u)
                        for q in range(HG):
                            v.wait_ge(sem("write_done"), g0 * HG + q + 1)
                            for gi in range(NG):
                                h = HG * gi + q
                                last = v.scalar_tensor_tensor(
                                    out=S[:, h], in0=S[:, h], scalar=dcy[:, h, NBLK:NBLK + 1],
                                    in1=PS[4 + q][:, gi * D:(gi + 1) * D], op0=ALU.mult, op1=ALU.subtract)
                            last.then_inc(sem("S_ready"), 1)
                        v.wait_ge(sem("S_ready"), g0 * HG + HG)
                        if c == 0:
                            chunk_decays(1)
                            convolve(nxt, 4)
                    for b in range(2):
                        v.wait_ge(sem("mean_done"), 2 * i + b + 1)
                        v.scalar_tensor_tensor(out=o[:, 8 * b:8 * b + 8], in0=heads(PS[2 + b][:]), scalar=-1.0 / D,
                                               in1=o[:, 8 * b:8 * b + 8], op0=ALU.mult, op1=ALU.add).then_inc(sem("centred"), 1)
                    v.wait_ge(sem("centred"), 2 * i + 2)
                    decays(nxt, 1 - u)
                    chunk_decays(0)
                    for b in range(2):
                        oh = o[:, 8 * b:8 * b + 8]
                        v.wait_ge(sem("rstd_ready"), 2 * i + b + 1)
                        step(v.tensor_tensor(oh, oh, osq[:, 8 * b:8 * b + 8], ALU.mult))
                        step(v.tensor_scalar(oh, oh, lnw[:, 0:1], lnb[:, 0:1], ALU.mult, ALU.add))
                        v.scalar_tensor_tensor(out=on[:, 8 * b:8 * b + 8], in0=gg[:, 8 * b:8 * b + 8], scalar=1.0, in1=oh,
                                               op0=ALU.add, op1=ALU.mult).then_inc(sem("gated"), 1)
                assert m[0] == STEPS1, m[0]
            v.memset(mark[:, 1:2], 0.0).then_inc(sem("gs_ready"), 1)

        @block.scalar
        def _(a):
            def copy_projected(n, k):
                a.wait_ge(sem("proj1_done"), 6 * n + k + 1)
                if not (isinstance(n, int) and k < 2):
                    a.wait_ge(sem("conv_ready"), 6 * n + k - 1)
                    a.wait_ge(sem("silu_ready"), 6 * n + k - 1)
                x, hf = k // 2, k % 2
                a.copy(raw[:, hf, :, CONV - 1:], heads(PS[4 + hf][:]))
                for h in range(HH):
                    hd = HH * hf + h
                    last = a.activation(ca[:, hf, h], PS[4 + hf][:, h * TB:(h + 1) * TB], ACT.Identity,
                                        scale=cw[:, x, hd, CONV - 1:CONV], bias=cb[:, x, hd:hd + 1])
                last.then_inc(sem("raw_ready"), 1)

            def silu(n, u, k):
                hs = slice(HH * (k % 2), HH * (k % 2) + HH)
                dst = (kq[:, u, hs, :, 1], kq[:, u, hs, :, 0], vv[:, u, hs])[k // 2]
                a.wait_ge(sem("conv_ready"), 6 * n + k + 1)
                a.activation(dst, ca[:, k % 2], ACT.Silu).then_inc(sem("silu_ready"), 1)

            def copy_logits(n):
                for hf in range(2):
                    a.wait_ge(sem("a_done"), 2 * n + hf + 1)
                    a.copy(ea[:, HH * hf:HH * hf + HH], heads(PS[4 + hf][:])).then_inc(sem("a_copied"), 1)

            def beta_gate(n):
                a.wait_ge(sem("bb_half"), 1)
                a.wait_ge(sem("b_done"), n + 1)
                a.activation(bt[:], PS[2][0:H, 0:TB], ACT.Tanh, scale=0.5, bias=hbb[:, 0:1]).then_inc(sem("beta_tanh"), 1)
                a.wait_ge(sem("beta_tanh"), n + 1)
                a.activation(bt[:], bt[:], ACT.Identity, scale=0.5, bias=half_t[:, 0:1]).then_inc(sem("beta_ready"), 1)

            def decay_exps(n):
                a.wait_ge(sem("a_logits"), n + 1)
                a.activation(ea[:], ea[:], ACT.Exp, scale=-1.0).then_inc(sem("exps1"), 1)
                a.wait_ge(sem("exps1"), n + 1)
                a.wait_ge(sem("silu_ready"), 6 * n + 6)
                a.activation(aa, ea[:], ACT.Ln, bias=1.0).then_inc(sem("softplus_ready"), 1)
                a.wait_ge(sem("softplus_ready"), n + 1)
                a.activation(aa, aa, ACT.Exp, scale=-1.0).then_inc(sem("a_ready"), 1)

            def copy_sums(block, slot):
                a.wait_ge(sem("gbc_done"), block + 1)
                for hh in range(2):
                    last = a.copy(gb[:, slot, 8 * hh:8 * hh + 8], heads(PS[6 + hh][:]))
                last.then_inc(sem("gb_ready"), 1)

            for k in range(6):
                copy_projected(0, k)
                if k:
                    silu(0, 0, k - 1)
            silu(0, 0, 5)
            copy_logits(0)
            beta_gate(0)
            decay_exps(0)
            copy_sums(0, 0)
            copy_projected(1, 0)
            with a.Fori(0, NB // 2) as j:
                for u in range(2):
                    i = j * 2 + u
                    nxt = j * 2 + u + 1
                    for c in range(NCH):
                        g0 = i * NCH + c
                        for b in range(NBLK):
                            if b < NBLK - 1 or c < NCH - 1:
                                if b >= 1 or c:
                                    a.wait_ge(sem("gb_used"), g0 * NBLK + b)
                                copy_sums(g0 * NBLK + b + 1, (b + 1) % 2)
                            if b == NBLK - 1:
                                a.wait_ge(sem("kr_done"), g0 + 1)
                                a.copy(kr.rearrange("p g d -> p (g d)"), PS[2][:]).then_inc(sem("kr_ready"), 1)
                            if c == 0:
                                if b == 3:
                                    silu(nxt, 1 - u, 2)
                                for k in ((), (1,), (2,), (3, 4))[b]:
                                    copy_projected(nxt, k)
                            elif b == 0:
                                silu(nxt, 1 - u, 3)
                                silu(nxt, 1 - u, 4)
                                copy_projected(nxt, 5)
                            elif b == 1:
                                copy_logits(nxt)
                            elif b == 2:
                                a.wait_ge(sem("g_done"), 2 * i + 1)
                                a.activation(gg[:, 0:HH], heads(PS[5][:]), ACT.Tanh, scale=0.5).then_inc(sem("g_ready"), 1)
                                beta_gate(nxt)
                                a.wait_ge(sem("g_done"), 2 * i + 2)
                                a.activation(gg[:, HH:H], heads(PS[4][:]), ACT.Tanh, scale=0.5).then_inc(sem("g_ready"), 1)
                            a.wait_ge(sem("histT_done"), g0 * NBLK + b + 1)
                            a.copy(hT[:].rearrange("p g d -> p (g d)"), PS[2][:]).then_inc(sem("hT_ready"), 1)
                            if (c, b) in ((0, 1), (0, 2), (1, 1)):
                                silu(nxt, 1 - u, b - 1 if c == 0 else 5)
                            if c == 1 and b == 2:
                                decay_exps(nxt)
                        if c == NCH - 1:
                            for b in range(2):
                                a.wait_ge(sem("centred"), 2 * i + b + 1)
                                a.activation(osq[:, 8 * b:8 * b + 8], vv[:, u, 8 * b:8 * b + 8],
                                             ACT.Square).then_inc(sem("squared"), 1)
                        for q in range(HG):
                            a.wait_ge(sem("sT_done"), g0 * HG + q + 1)
                            a.copy(sT[:].rearrange("p (g q) d -> p g q d", q=HG)[:, :, q, :],
                                   PS[4 + q][:].rearrange("p (g d) -> p g d", g=NG)).then_inc(sem("sT_ready"), 1)
                    for b in range(2):
                        a.wait_ge(sem("var_done"), 2 * i + b + 1)
                        a.activation(osq[:, 8 * b:8 * b + 8], heads(PS[2 + b][:]), ACT.Ln, scale=1.0 / D,
                                     bias=eps_t[:, 0:1]).then_inc(sem("log_ready"), 1)
                    for b in range(2):
                        a.wait_ge(sem("log_ready"), 2 * i + b + 1)
                        a.activation(osq[:, 8 * b:8 * b + 8], osq[:, 8 * b:8 * b + 8], ACT.Exp,
                                     scale=-0.5).then_inc(sem("rstd_ready"), 1)
                    copy_sums((i + 1) * (NCH * NBLK), 0)
                    copy_projected(nxt + 1, 0)
                    a.wait_ge(sem("attn_done"), i + 1)
                    a.copy(xr[:], PS[2][0:TB, 0:DM]).then_inc(sem("xo_ready"), 1)

        @block.tensor
        def _(pe):
            pe.wait_ge(sem("wp_loaded"), 16 * len(wp))
            pe.wait_ge(loaded, 16 * len(LOADS))
            pe.wait_ge(sem("xo_ready"), 1)

            def project(w, hf, bank, n):
                for h in range(HH):
                    for k in range(KC):
                        hd = HH * hf + h
                        last = pe.matmul(PS[bank][:, h * TB:(h + 1) * TB], w[:, k, hd * D:(hd + 1) * D],
                                         xnT[:, k, bass.ds(n * TB, TB)], start=(k == 0), stop=(k == KC - 1))
                return last

            def project_qkv(n, k):
                if not (isinstance(n, int) and k < 2):
                    pe.wait_ge(sem("raw_ready"), 6 * n + k - 1)
                project(wp[k // 2], k % 2, 4 + k % 2, n).then_inc(sem("proj1_done"), 1)

            def project_a(n):
                for hf in range(2):
                    pe.wait_ge(sem("raw_ready"), 6 * n + 5 + hf)
                    project(wp[3], hf, 4 + hf, n).then_inc(sem("a_done"), 1)

            def project_b(n):
                for k in range(KC):
                    last = pe.matmul(PS[2][0:H, 0:TB], wb[:, k, :], xnT[:, k, bass.ds(n * TB, TB)],
                                     start=(k == 0), stop=(k == KC - 1))
                last.then_inc(sem("b_done"), 1)

            def spread_beta(n):
                pe.wait_ge(sem("beta_rows"), n + 1)
                for b in range(2):
                    last = pe.matmul(PS[b][:], ones[0:H, :], be[:, 8 * b:8 * b + 8, :], start=True, stop=True)
                last.then_inc(sem("beta_done"), 1)

            def pair_sums(block, slot):
                pe.wait_ge(sem("pairs_ready"), block + 1)
                for hh in range(2):
                    last = pe.matmul(PS[6 + hh][:], ones[:], pr[:, 8 * hh:8 * hh + 8, slot, :], start=True, stop=True)
                last.then_inc(sem("gbc_done"), 1)

            def start_chunk(i, u, c):
                g0 = i * NCH + c
                kqf = kq[:, u].rearrange("p h t j -> p h (t j)")
                first = isinstance(i, int)
                if c == 0:
                    pe.wait_ge(sem("kb_ready"), i + 1)
                for q in range(HG):
                    if not (first and c == 0):
                        pe.wait_ge(sem("sT_ready"), g0 * HG - HG + q + 1)
                    for g in range(NG):
                        p0 = ((q % 2) * NG + g) * 64
                        last = pe.matmul(PS[q // 2][:, p0:p0 + 64], sT[:, HG * g + q, :],
                                         kqf[:, HG * g + q, 2 * c * CH:2 * (c + 1) * CH], start=True, stop=True)
                last.then_inc(sem("y0_done"), 1)
                if c == 0:
                    pair_sums(g0 * NBLK, 0)
                for g in range(NG):
                    last = pe.matmul(PS[4 + g // 2][:, (g % 2) * 256:(g % 2) * 256 + 256],
                                     kb[:, c, HG * g:HG * g + HG, :],
                                     kqf[:, HG * g:HG * g + HG, 2 * c * CH:2 * (c + 1) * CH], start=True, stop=True)
                last.then_inc(sem("gram1_done"), 1)
                if c == 0:
                    pe.wait_ge(sem("gb_ready"), g0 * NBLK + 1)
                    pair_sums(g0 * NBLK + 1, 1)

            for k in range(6):
                project_qkv(0, k)
            project_a(0)
            pe.wait_ge(sem("a_copied"), 2)
            project_b(0)
            spread_beta(0)
            start_chunk(0, 0, 0)
            pe.wait_ge(sem("gs_ready"), 1)
            project_qkv(1, 0)
            pe.wait_ge(sem("wo_loaded"), 32)
            with pe.Fori(0, NB // 2) as j:
                for u in range(2):
                    i = j * 2 + u
                    nxt = j * 2 + u + 1
                    for c in range(NCH):
                        g0 = i * NCH + c
                        for b in range(NBLK):
                            if (b < NBLK - 1 or c < NCH - 1) and not (b == 0 and c == 0):
                                pe.wait_ge(sem("gb_ready"), g0 * NBLK + b + 1)
                                pair_sums(g0 * NBLK + b + 1, (b + 1) % 2)
                            if b == 0:
                                pe.wait_ge(sem("gs_ready"), g0 + 1)
                            if b == NBLK - 1:
                                for g in range(NG):
                                    last = pe.transpose(PS[2][:, g * P:(g + 1) * P], kb[:, c, HG * g:HG * g + HG, :],
                                                        ident[:])
                                last.then_inc(sem("kr_done"), 1)
                            if c == 0:
                                for k in ((), (1,), (2,), (3, 4))[b]:
                                    project_qkv(nxt, k)
                            elif b == 0:
                                project_qkv(nxt, 5)
                            elif b == 1:
                                project_a(nxt)
                            elif b == 2:
                                pe.wait_ge(sem("a_copied"), 2 * nxt + 2)
                                project(wgate, 0, 5, i).then_inc(sem("g_done"), 1)
                                project_b(nxt)
                                project(wgate, 1, 4, i).then_inc(sem("g_done"), 1)
                            else:
                                spread_beta(nxt)
                            if b == NBLK - 1:
                                pe.wait_ge(sem("kr_ready"), g0 + 1)
                            if b == 2 and c == NCH - 1:
                                pe.wait_ge(sem("beta_tanh"), nxt + 1)
                            if b == 0 and c == 0:
                                pe.wait_ge(sem("xo_ready"), i + 1)
                            pe.wait_ge(sem("hist_ready"), g0 * NBLK + b + 1)
                            for g in range(NG):
                                last = pe.transpose(PS[2][:, g * P:(g + 1) * P], hist[:, HG * g:HG * g + HG, :], ident[:])
                            last.then_inc(sem("histT_done"), 1)
                            pe.wait_ge(sem("hT_ready"), g0 * NBLK + b + 1)
                            if b < NBLK - 1:
                                for g in range(NG):
                                    last = pe.matmul(PS[3][:, g * 64:(g + 1) * 64], hT[:, g, :],
                                                     gs[:, g, :, 2 * BK * b:2 * BK * (b + 1)], start=True, stop=True)
                                last.then_inc(sem("seen_done"), 1)
                        pe.wait_ge(sem("gb_ready"), g0 * NBLK + NBLK + (c < NCH - 1))
                        if c == 0:
                            pe.wait_ge(sem("raw_ready"), 6 * nxt + 5)
                        else:
                            pe.wait_ge(sem("g_ready"), 2 * i + 2)
                        for q in range(HG):
                            for g in range(NG):
                                last = pe.matmul(PS[4 + q][:, g * D:(g + 1) * D], hT[CH * q:CH * q + CH, g, :],
                                                 kr[CH * q:CH * q + CH, g, :], start=True, stop=True)
                            last.then_inc(sem("write_done"), 1)
                        if c == NCH - 1:
                            for b in range(2):
                                if b == 0:
                                    pe.wait_ge(sem("S_ready"), g0 * HG + 1)
                                pe.matmul(PS[2 + b][:], ones[:], vv[:, u, 8 * b:8 * b + 8, :], start=True,
                                          stop=True).then_inc(sem("mean_done"), 1)
                            for b in range(2):
                                pe.wait_ge(sem("squared"), 2 * i + b + 1)
                                pe.matmul(PS[2 + b][:], ones[:], osq[:, 8 * b:8 * b + 8, :], start=True,
                                          stop=True).then_inc(sem("var_done"), 1)
                        for q in range(HG):
                            pe.wait_ge(sem("S_ready"), g0 * HG + q + 1)
                            for g in range(NG):
                                last = pe.transpose(PS[4 + q][:, g * P:(g + 1) * P], S[:, HG * g + q, :], ident[:])
                            last.then_inc(sem("sT_done"), 1)
                        if c < NCH - 1:
                            start_chunk(i, u, c + 1)
                    start_chunk(nxt, 1 - u, 0)
                    pe.wait_ge(sem("xr_loaded"), i * 16 + 16)
                    for h in range(H):
                        if h % HH == 0:
                            pe.wait_ge(sem("gated"), 2 * i + h // HH + 1)
                        if h == H - HH // 2:
                            pe.wait_ge(sem("gs_ready"), nxt * NCH + 1)
                            project_qkv(nxt + 1, 0)
                        pe.matmul(PS[2][0:TB, 0:DM], on[:, h, :], wo[:, h, :], start=(h == 0), stop=False)
                    pe.matmul(PS[2][0:TB, 0:DM], ident[0:TB, 0:TB], xr[:], start=False,
                              stop=True).then_inc(sem("attn_done"), 1)


STEPS1 = 478
STEPS1P = 29


def kernel(**inputs):
    import numpy as np
    import concourse.bacc as bacc
    from concourse.bass_utils import run_bass_kernel_spmd as run

    nc = bacc.Bacc("TRN2", target_bir_lowering=False, num_devices=1)
    i = {k: np.asarray(v) for k, v in inputs.items()}
    c = np.ascontiguousarray
    arrays = {
        "L0_attn_u": c(i["L0_attn_u"].reshape(T, DM)),
        "in_projT": c(i["L0_attn_in_proj_w"].T),
        "out_projT": c(i["L0_attn_out_proj_w"].T),
        "gate0T": c(np.concatenate([i["L0_ffn_gate_w"].T, i["L0_ffn_shared_gate_w"]], axis=1)),
        "gate1T": c(i["L1_ffn_gate_w"].T),
        "w1T": c(i["L1_ffn_w1"].transpose(0, 2, 1)),
        "w3T": c(i["L1_ffn_w3"].transpose(0, 2, 1)),
        "w2T": c(i["L1_ffn_w2"].transpose(0, 2, 1)),
        "WbT": c(i["L1_attn_Wb"].T),
        "WoT": c(i["L1_attn_Wo"].T),
        "baT": c(i["L1_attn_ba"].reshape(H, D).T),
        "bbT": c(i["L1_attn_bb"].reshape(H, 1)),
        "ln_wT": c(i["L1_attn_ln_w"].reshape(D, 1)),
        "ln_bT": c(i["L1_attn_ln_b"].reshape(D, 1)),
    }
    for x in "qkvag":
        arrays[f"W{x}T"] = c(i[f"L1_attn_W{x}"].T)
    for x in "qkv":
        arrays[f"{x}conv_wT"] = c(i[f"L1_attn_{x}conv_w"].reshape(H, D, CONV).transpose(1, 0, 2))
        arrays[f"{x}conv_bT"] = c(i[f"L1_attn_{x}conv_b"].reshape(H, D).T)
    for name in ("L0_attn_D", "L0_attn_dt_bias", "L0_attn_A_log", "L0_attn_bnorm_w", "L0_attn_cnorm_w",
                 "L0_attn_ln_w", "L0_attn_ln_b", "L0_ffn_w_gate", "L0_ffn_w_up", "L0_ffn_w_down",
                 "L0_ffn_sw_gate", "L0_ffn_sw_up", "L0_ffn_sw_down"):
        arrays[name] = c(i[name])
    A = {n: nc.dram_tensor(f"in_{n}", a.shape, mybir.dt.from_np(a.dtype), kind="ExternalInput").ap()
         for n, a in arrays.items()}
    out = nc.dram_tensor("out", (T, DM), F32, kind="ExternalOutput").ap()
    program(nc, A, out)
    r = run(nc, [{f"in_{n}": a for n, a in arrays.items()}], core_ids=[0])
    return r.results[0]["out"].reshape(1, T, DM)
```
